# Optimizing a Trainium2 kernel written in Bass

```python
import numpy as np
import jax
import jax.numpy as jnp

def _softmax(x, axis=-1):
    return jax.nn.softmax(x, axis=axis)

def _gelu(x):
    return jax.nn.gelu(x, approximate=True)

def _silu(x):
    return jax.nn.silu(x)

def _sigmoid(x):
    return jax.nn.sigmoid(x)

def _layernorm(x, axis=-1, eps=1e-05):
    m = jnp.mean(x, axis=axis, keepdims=True)
    v = jnp.var(x, axis=axis, keepdims=True)
    return (x - m) / jnp.sqrt(v + eps)

def _scatter_add(tgt, idx, src, axis=0):
    return tgt.at[idx].add(src)

def _segment_sum(src, seg, n):
    return jax.ops.segment_sum(src, seg, n)
kernel_name = 'mk_decoder_postln_d1_seqx_r8_0147c6'

def setup_inputs(seed: int=0):
    np.random.seed(seed)
    _w = jnp.asarray

    def _rec_inputs():
        import jax
        import jax.numpy as jnp
        _rk = jax.random.key(seed)
        x = -0.0003929 + 0.9999 * jax.random.normal(jax.random.fold_in(_rk, 1), (32, 64, 512), jnp.float32)
        _lenS = 64 - jax.random.randint(jax.random.fold_in(_rk, 7), (32,), 0, max(1, 64 // 4) + 1, jnp.int32)
        _lenS2 = 64 - jax.random.randint(jax.random.fold_in(_rk, 8), (32,), 0, max(1, 64 // 4) + 1, jnp.int32)
        _ctx_4096P = jax.random.normal(jax.random.fold_in(_rk, 11), (32, 16, 512), jnp.float32)
        _ctx_4096c = jax.random.dirichlet(jax.random.fold_in(_rk, 511), 0.3 * jnp.ones((16,), jnp.float32), (32, 64))
        _ctx_4096t = jnp.einsum('bsk,bkd->bsd', _ctx_4096c, _ctx_4096P)
        _ctx_4096t = _ctx_4096t * jax.lax.rsqrt(jnp.mean(jnp.square(_ctx_4096t)) + 1e-12) * 0.953939
        ctx_4096 = 2.81802e-05 + 1.00001 * (_ctx_4096t + 0.3 * jax.random.normal(jax.random.fold_in(_rk, 611), (32, 64, 512), jnp.float32))
        return (x, ctx_4096)
    x, ctx_4096 = _rec_inputs()

    def _L0_attn_setup():
        import jax, jax.numpy as jnp
        import numpy as np
        import math
        B, L, D, H = (32, 64, 512, 32)
        HD = D // H
        key = jax.random.key(seed)
        ks = jax.random.split(key, 9)
        s = 1.0 / math.sqrt(D)
        return {'x': jax.random.normal(ks[0], (B, L, D), jnp.float32), 'Wq': jax.random.normal(ks[1], (D, D), jnp.float32) * s, 'bq': jax.random.normal(ks[2], (D,), jnp.float32) * s, 'Wk': jax.random.normal(ks[3], (D, D), jnp.float32) * s, 'bk': jax.random.normal(ks[4], (D,), jnp.float32) * s, 'Wv': jax.random.normal(ks[5], (D, D), jnp.float32) * s, 'bv': jax.random.normal(ks[6], (D,), jnp.float32) * s, 'Wo': jax.random.normal(ks[7], (D, D), jnp.float32) * s, 'bo': jax.random.normal(ks[8], (D,), jnp.float32) * s}
    _L0_attn_all = _L0_attn_setup()
    _L0_attn_in = {k: v for k, v in _L0_attn_all.items() if k in ('Wq', 'bq', 'Wk', 'bk', 'Wv', 'bv', 'Wo', 'bo')}
    del _L0_attn_all

    def _L0_xattn_setup():
        import jax, jax.numpy as jnp
        import numpy as np
        DIM = 64
        HEADS = 8
        DIM_HEAD = 64
        HIDDEN = HEADS * DIM_HEAD
        SCALE = DIM_HEAD ** (-0.5)
        key = jax.random.key(seed)
        ks = jax.random.split(key, 9)
        b, n = (8, 512)
        std = 1.0 / np.sqrt(DIM)
        return {'q': jax.random.normal(ks[0], (b, DIM, n), jnp.float32), 'k': jax.random.normal(ks[1], (b, DIM, n), jnp.float32), 'v': jax.random.normal(ks[2], (b, DIM, n), jnp.float32), 'Wq': jax.random.normal(ks[3], (HIDDEN, DIM), jnp.float32) * std, 'Wk': jax.random.normal(ks[4], (HIDDEN, DIM), jnp.float32) * std, 'Wv': jax.random.normal(ks[5], (HIDDEN, DIM), jnp.float32) * std, 'Wo': jax.random.normal(ks[6], (DIM, HIDDEN), jnp.float32) * (1.0 / np.sqrt(HIDDEN)), 'bo': jax.random.normal(ks[7], (DIM,), jnp.float32) * 0.01, 'g': jnp.ones((1, DIM, 1), jnp.float32)}
    _L0_xattn_all = _L0_xattn_setup()
    _L0_xattn_in = {k: v for k, v in _L0_xattn_all.items() if k in ('Wq', 'Wk', 'Wv', 'Wo', 'bo', 'g')}
    del _L0_xattn_all

    def _L0_ffn_setup():
        import jax, jax.numpy as jnp
        import numpy as np
        HD, M = (512, 1792)
        key = jax.random.key(seed)
        k_x, k_g, k_u, k_d = jax.random.split(key, 4)
        scale = 1.0 / np.sqrt(HD)
        x = jax.random.normal(k_x, (4, 256, HD), dtype=jnp.float16)
        W_gate = jax.random.normal(k_g, (M, HD), dtype=jnp.float16) * jnp.float16(scale)
        W_up = jax.random.normal(k_u, (M, HD), dtype=jnp.float16) * jnp.float16(scale)
        W_down = jax.random.normal(k_d, (HD, M), dtype=jnp.float16) * jnp.float16(1.0 / np.sqrt(M))
        return {'x': x, 'W_gate': W_gate, 'W_up': W_up, 'W_down': W_down}
    _L0_ffn_all = _L0_ffn_setup()
    _L0_ffn_in = {k: v for k, v in _L0_ffn_all.items() if k in ('W_gate', 'W_up', 'W_down')}
    del _L0_ffn_all
    return {'x': x, 'ctx_4096': ctx_4096, 'L0_attn_Wq': _L0_attn_in['Wq'], 'L0_attn_bq': _L0_attn_in['bq'], 'L0_attn_Wk': _L0_attn_in['Wk'], 'L0_attn_bk': _L0_attn_in['bk'], 'L0_attn_Wv': _L0_attn_in['Wv'], 'L0_attn_bv': _L0_attn_in['bv'], 'L0_attn_Wo': _L0_attn_in['Wo'], 'L0_attn_bo': _L0_attn_in['bo'], 'L0_xattn_Wq': _L0_xattn_in['Wq'], 'L0_xattn_Wk': _L0_xattn_in['Wk'], 'L0_xattn_Wv': _L0_xattn_in['Wv'], 'L0_xattn_Wo': _L0_xattn_in['Wo'], 'L0_xattn_bo': _L0_xattn_in['bo'], 'L0_xattn_g': _L0_xattn_in['g'], 'L0_ffn_W_gate': _L0_ffn_in['W_gate'], 'L0_ffn_W_up': _L0_ffn_in['W_up'], 'L0_ffn_W_down': _L0_ffn_in['W_down']}

def reference(x, ctx_4096, L0_attn_Wq, L0_attn_bq, L0_attn_Wk, L0_attn_bk, L0_attn_Wv, L0_attn_bv, L0_attn_Wo, L0_attn_bo, L0_xattn_Wq, L0_xattn_Wk, L0_xattn_Wv, L0_xattn_Wo, L0_xattn_bo, L0_xattn_g, L0_ffn_W_gate, L0_ffn_W_up, L0_ffn_W_down):
    import jax
    import jax.numpy as jnp

    def _L0_attn_ref(x, Wq, bq, Wk, bk, Wv, bv, Wo, bo):
        import jax, jax.numpy as jnp
        import numpy as np
        import math
        B, L, D, H = (32, 64, 512, 32)
        HD = D // H
        b, l, d = x.shape
        h, hd = (H, HD)
        q = (x @ Wq.T + bq).reshape(b, l, h, hd).transpose(0, 2, 1, 3)
        k = (x @ Wk.T + bk).reshape(b, l, h, hd).transpose(0, 2, 1, 3)
        v = (x @ Wv.T + bv).reshape(b, l, h, hd).transpose(0, 2, 1, 3)
        scores = jnp.einsum('bhqd,bhkd->bhqk', q, k) / math.sqrt(hd)
        causal = jnp.tril(jnp.ones((l, l), bool))
        scores = jnp.where(causal, scores, -jnp.inf)
        att = jax.nn.softmax(scores, axis=-1)
        out = jnp.einsum('bhqk,bhkd->bhqd', att, v)
        out = out.transpose(0, 2, 1, 3).reshape(b, l, d)
        return out @ Wo.T + bo

    def _L0_xattn_ref(q, k, v, Wq, Wk, Wv, Wo, bo, g):
        import jax, jax.numpy as jnp
        import numpy as np
        DIM = 64
        HEADS = 8
        DIM_HEAD = 64
        HIDDEN = HEADS * DIM_HEAD
        SCALE = DIM_HEAD ** (-0.5)
        b = q.shape[0]
        qh = jnp.einsum('bcn,oc->bon', q, Wq).reshape(b, HEADS, DIM_HEAD, -1)
        kh = jnp.einsum('bcn,oc->bon', k, Wk).reshape(b, HEADS, DIM_HEAD, -1)
        vh = jnp.einsum('bcn,oc->bon', v, Wv).reshape(b, HEADS, DIM_HEAD, -1)
        qh = jax.nn.softmax(qh, axis=-2) * SCALE
        kh = jax.nn.softmax(kh, axis=-1)
        context = jnp.einsum('bhdn,bhen->bhde', kh, vh)
        out = jnp.einsum('bhde,bhdn->bhen', context, qh)
        out = out.reshape(b, HIDDEN, -1)
        out = jnp.einsum('bcn,oc->bon', out, Wo) + bo[None, :, None]
        norm = jnp.maximum(jnp.sqrt(jnp.sum(out * out, axis=1, keepdims=True)), 1e-12)
        return out / norm * g * np.sqrt(DIM)

    def _L0_ffn_ref(x, W_gate, W_up, W_down):
        import jax, jax.numpy as jnp
        import numpy as np
        HD, M = (512, 1792)
        gate = jnp.einsum('bsh,mh->bsm', x, W_gate)
        up = jnp.einsum('bsh,mh->bsm', x, W_up)
        h = jax.nn.silu(gate) * up
        out = jnp.einsum('bsm,hm->bsh', h, W_down)
        return out
    x = _layernorm(x + _L0_attn_ref(x, L0_attn_Wq, L0_attn_bq, L0_attn_Wk, L0_attn_bk, L0_attn_Wv, L0_attn_bv, L0_attn_Wo, L0_attn_bo), axis=-1)
    x = _layernorm(x + _L0_xattn_ref(x, ctx_4096, ctx_4096, L0_xattn_Wq, L0_xattn_Wk, L0_xattn_Wv, L0_xattn_Wo, L0_xattn_bo, L0_xattn_g), axis=-1)
    x = _layernorm(x + _L0_ffn_ref(x, L0_ffn_W_gate, L0_ffn_W_up, L0_ffn_W_down), axis=-1)
    return x

_drawn_inputs = setup_inputs


def setup_inputs(seed=0):
    import zlib

    import numpy as np

    out = dict(_drawn_inputs(seed))
    spreads = {'L0_xattn_g': (1.0, 0.2)}
    factors = {'L0_attn_bq': 4.396, 'L0_attn_bk': 8.0}
    for name, (base, spread) in spreads.items():
        noise = np.random.default_rng([zlib.crc32(name.encode()), seed]).standard_normal(out[name].shape)
        drawn = base * np.exp(spread * noise) if base else spread * noise
        out[name] = jnp.asarray(drawn.astype(out[name].dtype))
    for name, factor in factors.items():
        out[name] = (out[name] * factor).astype(out[name].dtype)
    return out
```

```python
from contextlib import ExitStack

import concourse.bass as bass
from concourse import mybir

F32 = mybir.dt.float32
F32R = mybir.dt.float32r
F16 = mybir.dt.float16
BF16 = mybir.dt.bfloat16
ACT = mybir.ActivationFunctionType
ALU = mybir.AluOpType
AX = mybir.AxisListType

P = 128
B, L, D, H = 32, 64, 512, 32
HD = D // H
DC = D // P
TOK = 256
NT = B * L // TOK
PAIRS = B // 2
HC = P // HD
VW = HD + 1
MASKED = -1.0e30
EPS = 1e-5


def attention_phase(nc, persist, x_d, xT_d, wT_d, b_d, bo_d, bv_d, y1, stats):
    ident, identb = persist
    with ExitStack() as c:
        def sb(name, shape, dt=F32):
            return c.enter_context(nc.sbuf_tensor(name, shape, dt))

        def sem(name):
            return c.enter_context(nc.semaphore(name))

        w_hi = [sb(f"w_hi{i}", [P, DC, D], F32R) for i in range(4)]
        w_lo = [sb(f"w_lo{i}", [P, DC, D], F32R) for i in range(4)]
        xT = sb("xT", [P, DC, TOK])
        xT_hi = sb("xT_hi", [P, DC, TOK], F32R)
        xT_lo = sb("xT_lo", [P, DC, TOK], F32R)
        x_res = sb("x_res", [P, 2, D])
        xb = sb("xb", [P, 2, D])
        bo_all = sb("bo_all", [P, D])
        bv_all = sb("bv_all", [P, D])
        bq_col = sb("bq_col", [P, DC])
        bq_scaled = sb("bq_scaled", [P, DC])
        bk_col = sb("bk_col", [P, DC])
        qT = sb("qT", [P, DC, TOK])
        kT = sb("kT", [P, DC, TOK])
        k_diag = sb("k_diag", [P, DC, HC, TOK])
        v_diag = sb("v_diag", [P, 4, H // 2, 2 * VW])
        stage = k_diag[:, :, :, :].rearrange("p a h t -> p (a h t)")
        mask = sb("mask", [P, L], BF16)
        neg_max = sb("neg_max", [P, 2, HC], BF16)
        prob = sb("prob", [P, 2, 512])
        probT = sb("probT", [P, 2, 512])
        inv_sum = sb("inv_sum", [P, 2, 16])
        o = sb("o", [P, D])
        landed = sb("landed", [P, 2])
        oT_hi = sb("oT_hi", [P, DC, P], F32R)
        oT_lo = sb("oT_lo", [P, DC, P], F32R)
        ps = c.enter_context(nc.psum_tensor("ps_a", [P, 8, 512], F32))
        M0, M1 = ps[:, 0, :], ps[:, 1, :]

        def S(g):
            return ps[:, 2 + g % 2, :]

        def T(g):
            return ps[:, 4 + g % 2, :]

        O = ps[:, 6:8, :]

        consts_in = sem("consts_in")
        w_in = [sem(f"w_in{i}") for i in range(4)]
        w_hi_ready, w_ready = sem("w_hi_ready"), sem("w_ready")
        setup_done = sem("setup_done")
        pool_step, dve_step = sem("pool_step"), sem("dve_step")
        bq_ready = sem("bq_ready")
        xThi_ready = sem("xThi_ready")
        xT_in, xres_in, xT_ready, xb_ready = sem("xT_in"), sem("xres_in"), sem("xT_ready"), sem("xb_ready")
        qk_done, v_done = sem("qk_done"), sem("v_done")
        kT_ready, kdiag_ready, v_ready = sem("kT_ready"), sem("kdiag_ready"), sem("v_ready")
        m0_free, m1_free = sem("m0_free"), sem("m1_free")
        s_done, max_done, shift_done, exp_done = sem("s_done"), sem("max_done"), sem("shift_done"), sem("exp_done")
        t_done, probT_done, av_done = sem("t_done"), sem("probT_done"), sem("av_done")
        o_ready, oT_done, oThi_ready, oT_ready = sem("o_ready"), sem("oT_done"), sem("oThi_ready"), sem("oT_ready")
        proj_done, y_done = sem("proj_done"), sem("y_done")

        with nc.Block() as block:
            @block.sync
            def _(sp):
                def load_xT(t):
                    sp.dma_start(xT[:, :, :], xT_d[:, :, bass.ds(t * TOK, TOK)]).then_inc(xT_in, 16)

                def load_xres(t):
                    sp.dma_start(x_res[:, :, :], x_d[:, bass.ds(t * 2, 2), :]).then_inc(xres_in, 16)

                def diagonal(t):
                    sp.wait_ge(kT_ready, 4 * t + 4)
                    for h in range(HC):
                        sp.dma_start(k_diag[HD * h:HD * h + HD, :, h, :],
                                     kT[HD * h:HD * h + HD, :, :]).then_inc(kdiag_ready, 16)

                for i in range(4):
                    if i >= 2:
                        sp.wait_ge(w_ready, i - 1)
                    sp.dma_start(stage[:, (i % 2) * DC * D:(i % 2 + 1) * DC * D], wT_d[i]).then_inc(w_in[i], 16)
                    if i == 0:
                        load_xT(0)
                        sp.dma_start(bq_col[:, :], b_d[0]).then_inc(consts_in, 16)
                        sp.dma_start(bk_col[:, :], b_d[1]).then_inc(consts_in, 16)
                        sp.dma_start(bv_all[:, :], bv_d).then_inc(consts_in, 16)
                        sp.dma_start(bo_all[:, :], bo_d).then_inc(consts_in, 16)
                        load_xres(0)
                sp.wait_ge(setup_done, 1)
                diagonal(0)
                sp.wait_ge(xT_ready, 1)
                load_xT(1)
                with sp.Fori(0, NT - 2) as t:
                    sp.wait_ge(xb_ready, t + 1)
                    load_xres(t + 1)
                    diagonal(t + 1)
                    sp.wait_ge(xT_ready, t + 2)
                    load_xT(t + 2)
                sp.wait_ge(xb_ready, NT - 1)
                load_xres(NT - 1)
                diagonal(NT - 1)

            @block.gpsimd
            def _(pool):
                pool.memset(mask[:, :], 0.0).then_inc(pool_step, 1)
                pool.memset(v_diag[:, :, :, :], 0.0).then_inc(pool_step, 1)
                for b in range(2):
                    pool.wait_ge(pool_step, 2 + b)
                    m = mask[L * b:L * b + L, :]
                    pool.affine_select(out=m, in_=m, compare_op=ALU.is_ge, fill=MASKED, base=0,
                                       pattern=[[-1, L]], channel_multiplier=1).then_inc(pool_step, 1)
                for half in range(2):
                    pool.wait_ge(pool_step, 4 + half)
                    pool.memset(v_diag[L * half:L * half + L, :, :, half * VW + HD], 1.0).then_inc(pool_step, 1)
                pool.wait_ge(pool_step, 6)

                def split_x(t):
                    pool.wait_ge(xThi_ready, t + 1)
                    pool.tensor_tensor(xT_lo[:, :, :], xT[:, :, :], xT_hi[:, :, :].bitcast(F32),
                                       ALU.subtract).then_inc(xT_ready, 1)

                split_x(0)
                pool.wait_ge(w_ready, 4)
                pool.memset(stage, 0.0).then_inc(setup_done, 1)
                pool.wait_ge(consts_in, 64)

                def residual(t):
                    pool.wait_ge(xres_in, 16 * t + 16)
                    pool.wait_ge(y_done, 2 * t + 2)
                    for p in range(2):
                        ins = pool.tensor_tensor(xb[:, p, :], x_res[:, p, :], bo_all[:, :], ALU.add)
                    ins.then_inc(xb_ready, 1)

                residual(0)
                with pool.Fori(0, NT - 1) as t:
                    split_x(t + 1)
                    residual(t + 1)

            @block.scalar
            def _(act):
                def split_x(t):
                    act.wait_ge(xT_in, 16 * t + 16)
                    act.activation(xT_hi[:, :, :], xT[:, :, :], ACT.Copy).then_inc(xThi_ready, 1)

                for i in range(4):
                    act.wait_ge(w_in[i], 16)
                    act.activation(w_hi[i][:, :, :], stage[:, (i % 2) * DC * D:(i % 2 + 1) * DC * D]
                                   .rearrange("p (c f) -> p c f", c=DC), ACT.Copy).then_inc(w_hi_ready, 1)
                split_x(0)
                act.wait_ge(consts_in, 64)
                act.activation(bq_scaled[:, :], bq_col[:, :], ACT.Copy, scale=HD ** -0.5).then_inc(bq_ready, 1)
                act.wait_ge(bq_ready, 1)

                def qk(t, f):
                    bank, free = (M0, m0_free) if f == 2 else (M1, m1_free)
                    act.wait_ge(qk_done, 4 * t + f + 1)
                    act.activation(qT[:, f, :], bank[:, 0:TOK], ACT.Identity, bias=bq_scaled[:, f:f + 1],
                                   scale=HD ** -0.5)
                    act.activation(kT[:, f, :], bank[:, TOK:2 * TOK], ACT.Identity,
                                   bias=bk_col[:, f:f + 1]).then_inc(kT_ready, 1)

                def exp(t, s):
                    act.wait_ge(shift_done, 8 * t + s + 1)
                    act.wait_ge(t_done, 8 * t + s + 1)
                    act.activation(prob[:, s % 2, :], S(s), ACT.Exp).then_inc(exp_done, 1)

                def oT(t, p):
                    act.wait_ge(oT_done, 2 * t + p + 1)
                    act.wait_ge(proj_done, 2 * t + p + 1)
                    act.activation(oT_hi[:, :, :], M0.rearrange("p (c t) -> p c t", c=DC), ACT.Copy)\
                       .then_inc(oThi_ready, 1)

                for f in range(4):
                    qk(0, f)

                def attention(t, last):
                    if not last:
                        act.wait_ge(v_done, 2 * t + 2)
                        split_x(t + 1)
                    for s in range(8):
                        exp(t, s)
                    oT(t, 0)
                    if not last:
                        act.wait_ge(kdiag_ready, 16 * HC * (t + 1))
                        for f in range(4):
                            qk(t + 1, f)
                    oT(t, 1)

                with act.Fori(0, NT - 1) as t:
                    attention(t, False)
                attention(NT - 1, True)

            @block.vector
            def _(dve):
                for i in range(4):
                    dve.wait_ge(w_hi_ready, i + 1)
                    dve.tensor_tensor(w_lo[i][:, :, :], stage[:, (i % 2) * DC * D:(i % 2 + 1) * DC * D]
                                      .rearrange("p (c f) -> p c f", c=DC), w_hi[i][:, :, :].bitcast(F32),
                                      ALU.subtract).then_inc(w_ready, 1)
                for s, n in ((t_done, 2), (exp_done, 2), (probT_done, 2), (av_done, 2), (o_ready, 1), (proj_done, 1),
                             (y_done, 2)):
                    dve.sem_inc(s, n)
                dve.memset(landed[:, :], 0.0)
                dve.wait_ge(consts_in, 64)
                dve.wait_ge(pool_step, 6)

                def v(t, tt):
                    dve.wait_ge(v_done, 2 * t + tt + 1)
                    for b in range(2):
                        src = M1[L * b:L * b + L, :].rearrange("p (h two d) -> p h two d", two=2, d=HD)
                        bv = bv_all[L * b:L * b + L, :].rearrange("p (h two d) -> p h two d", two=2, d=HD)
                        for half in range(2):
                            ins = dve.tensor_tensor(
                                v_diag[L * half:L * half + L, 2 * tt + b, :, half * VW:half * VW + HD],
                                src[:, :, half, :], bv[:, :, half, :], ALU.add)
                            ins.then_inc(v_ready, 1)

                def row_max(t, s):
                    dve.wait_ge(s_done, 8 * t + s + 1)
                    dve.tensor_reduce(neg_max[:, s % 2, :], S(s).rearrange("p (h k) -> p h k", k=L), AX.X, ALU.max,
                                      negate=True).then_inc(max_done, 1)

                def evacuate(t, s):
                    dve.wait_ge(t_done, 8 * t + s + 3)
                    dve.wait_ge(av_done, 8 * t + s + 1)
                    dve.tensor_copy(probT[:, s % 2, :], T(s)).then_inc(probT_done, 1)

                def normalise(t, p):
                    dve.wait_ge(av_done, 8 * t + 4 * p + 6)
                    Oh = O[:, :, 0:16 * VW].rearrange("p n (h w) -> p n h w", w=VW)
                    dve.reciprocal(inv_sum[:, :, :], Oh[:, :, :, HD]).then_inc(dve_step, 1)
                    dve.wait_ge(dve_step, 2 * t + p + 1)
                    for n in range(2):
                        ins = dve.tensor_tensor(
                            o[:, 256 * n:256 * n + 256].rearrange("p (h d) -> p h d", d=HD), Oh[:, n, :, 0:HD],
                            inv_sum[:, n, :].unsqueeze(2).broadcast_to([P, 16, HD]), ALU.mult)
                    ins.then_inc(o_ready, 1)

                def oT(t, p):
                    dve.wait_ge(oThi_ready, 2 * t + p + 1)
                    dve.tensor_tensor(oT_lo[:, :, :], M0.rearrange("p (c t) -> p c t", c=DC),
                                      oT_hi[:, :, :].bitcast(F32), ALU.subtract).then_inc(oT_ready, 1)

                def y(t, p):
                    dve.wait_ge(proj_done, 2 * t + p + 2)
                    dve.wait_ge(xb_ready, t + 1)
                    dve.tensor_tensor(y1[:, bass.ds(2 * t + p, 1), :], M0.unsqueeze(1), xb[:, p:p + 1, :],
                                      ALU.add).then_inc(y_done, 1)
                    dve.wait_ge(y_done, 2 * t + p + 3)
                    dve.tensor_copy(landed[:, 0:1], landed[:, 1:2])
                    dve.bn_stats(stats[:, bass.ds((2 * t + p) * 6, 6)], y1[:, bass.ds(2 * t + p, 1), :])

                for tt in range(2):
                    v(0, tt)

                def attention(t, last):
                    for s in range(8):
                        row_max(t, s)
                        if s >= 2:
                            evacuate(t, s - 2)
                        if s == 6:
                            normalise(t, 0)
                    evacuate(t, 6)
                    oT(t, 0)
                    evacuate(t, 7)
                    y(t, 0)
                    normalise(t, 1)
                    oT(t, 1)
                    if not last:
                        v(t + 1, 0)
                    y(t, 1)
                    if not last:
                        v(t + 1, 1)

                with dve.Fori(0, NT - 1) as t:
                    attention(t, False)
                attention(NT - 1, True)

            @block.tensor
            def _(pe):
                def three(out, stat_hi, stat_lo, mov_hi, mov_lo, c, n=DC):
                    parts = [(stat_hi, mov_hi), (stat_hi, mov_lo), (stat_lo, mov_hi)]
                    for k, (a, b) in enumerate(parts):
                        ins = pe.matmul(out, a, b, start=(c == 0 and k == 0), stop=(c == n - 1 and k == 2))
                    return ins

                def qk(t, f):
                    for w in range(2):
                        bank = M0 if f == 2 else M1
                        for cc in range(DC):
                            fs = slice(P * f, P * f + P)
                            ins = three(bank[:, TOK * w:TOK * w + TOK], w_hi[w][:, cc, fs], w_lo[w][:, cc, fs],
                                        xT_hi[:, cc, :], xT_lo[:, cc, :], cc)
                    ins.then_inc(qk_done, 1)

                def v(t, tt):
                    for cc in range(DC):
                        ts = slice(P * tt, P * tt + P)
                        ins = three(M1, xT_hi[:, cc, ts], xT_lo[:, cc, ts], w_hi[2][:, cc, :], w_lo[2][:, cc, :], cc)
                    ins.then_inc(v_done, 1)

                def scores(t, s):
                    p, cc = s // 4, s % 4
                    if s == 0:
                        pe.wait_ge(kdiag_ready, 16 * HC * (t + 1))
                    pe.wait_ge(exp_done, 8 * t + s + 1)
                    pe.matmul(S(s).rearrange("p (h k) -> p h k", k=L), identb[:, :],
                              mask[:, :].unsqueeze(1).broadcast_to([P, HC, L]), start=True, stop=True)
                    for b in range(2):
                        ts = slice(L * (2 * p + b), L * (2 * p + b) + L)
                        ins = pe.matmul(S(s)[L * b:L * b + L, :].rearrange("p (h k) -> p h k", k=L),
                                        qT[:, cc, ts], k_diag[:, cc, :, ts], start=False, stop=True, skip_group_check=True)
                    ins.then_inc(s_done, 1)

                def shift(t, s):
                    pe.wait_ge(max_done, 8 * t + s + 1)
                    pe.matmul(S(s).rearrange("p (h k) -> p h k", k=L), identb[:, :],
                              neg_max[:, s % 2, :].unsqueeze(2).broadcast_to([P, HC, L]), start=False, stop=True,
                              skip_group_check=True).then_inc(shift_done, 1)

                def transposes(t, s):
                    pe.wait_ge(exp_done, 8 * t + s + 3)
                    pe.wait_ge(probT_done, 8 * t + s + 1)
                    for k in range(4):
                        ins = pe.transpose(T(s)[:, P * k:P * k + P], prob[:, s % 2, P * k:P * k + P], ident[:, :])
                    ins.then_inc(t_done, 1)

                def values(t, s):
                    p, cc = s // 4, s % 4
                    pe.wait_ge(probT_done, 8 * t + s + 3)
                    if cc == 0:
                        pe.wait_ge(o_ready, 2 * t + p + 1)
                    if s == 0:
                        pe.wait_ge(v_ready, 8 * t + 8)
                    for k in range(4):
                        hp = 4 * cc + k
                        for b in range(2):
                            ins = pe.matmul(O[L * b:L * b + L, hp // 8, 2 * VW * (hp % 8):2 * VW * (hp % 8 + 1)],
                                            probT[:, s % 2, P * k + L * b:P * k + L * b + L],
                                            v_diag[:, 2 * p + b, hp, :], start=True, stop=True)
                    ins.then_inc(av_done, 1)

                def oT(t, p):
                    pe.wait_ge(o_ready, 2 * t + p + 2)
                    for k in range(DC):
                        ins = pe.transpose(M0[:, P * k:P * k + P], o[:, P * k:P * k + P], ident[:, :])
                    ins.then_inc(oT_done, 1)

                def project(t, p):
                    pe.wait_ge(oT_ready, 2 * t + p + 1)
                    for cc in range(DC):
                        ins = three(M0, oT_hi[:, cc, :], oT_lo[:, cc, :], w_hi[3][:, cc, :], w_lo[3][:, cc, :], cc)
                    ins.then_inc(proj_done, 1)

                pe.wait_ge(w_ready, 2)
                pe.wait_ge(xT_ready, 1)
                for f in range(4):
                    if f == 1 or f == 3:
                        pe.wait_ge(kT_ready, f)
                    qk(0, f)
                pe.wait_ge(w_ready, 4)
                pe.wait_ge(kT_ready, 4)
                v(0, 0)
                pe.wait_ge(v_ready, 4)
                v(0, 1)

                def attention(t, last):
                    for s in range(8):
                        scores(t, s)
                        if s >= 1:
                            shift(t, s - 1)
                        if s >= 2:
                            transposes(t, s - 2)
                        if s >= 3:
                            values(t, s - 3)
                    shift(t, 7)
                    transposes(t, 6)
                    values(t, 5)
                    pe.wait_ge(y_done, 2 * t + 2)
                    oT(t, 0)
                    if not last:
                        pe.wait_ge(xT_ready, t + 2)
                        pe.wait_ge(v_ready, 8 * t + 8)
                        qk(t + 1, 0)
                    transposes(t, 7)
                    values(t, 6)
                    project(t, 0)
                    if not last:
                        pe.wait_ge(kT_ready, 4 * t + 5)
                        qk(t + 1, 1)
                    values(t, 7)
                    pe.wait_ge(y_done, 2 * t + 3)
                    if not last:
                        qk(t + 1, 2)
                        pe.wait_ge(kT_ready, 4 * t + 6)
                        qk(t + 1, 3)
                        pe.wait_ge(kT_ready, 4 * t + 7)
                    oT(t, 1)
                    if not last:
                        pe.wait_ge(kT_ready, 4 * t + 8)
                        v(t + 1, 0)
                    project(t, 1)
                    if not last:
                        pe.wait_ge(v_ready, 8 * t + 12)
                        v(t + 1, 1)

                with pe.Fori(0, NT - 1) as t:
                    attention(t, False)
                attention(NT - 1, True)


def layer_norm_terms(nc, stats, scale, shift):
    with ExitStack() as c:
        def sb(name):
            return c.enter_context(nc.sbuf_tensor(name, [P, PAIRS], F32))

        half_sum, half_diff, var, sq, mean, root = (sb(n) for n in ("ln_sum", "ln_diff", "ln_var", "ln_sq", "ln_mean", "ln_root"))
        eps = sb("ln_eps")
        step, var_ready, root_ready = (c.enter_context(nc.semaphore(n)) for n in ("ln_step", "var_ready", "root_ready"))
        st = stats[:, :].rearrange("p (i k) -> p i k", k=6)
        with nc.Block() as block:
            @block.vector
            def _(dve):
                n = [0]

                def done(ins):
                    n[0] += 1
                    ins.then_inc(step, 1)
                    dve.wait_ge(step, n[0])

                dve.memset(eps[:, :], EPS)
                dve.tensor_tensor(half_sum[:, :], st[:, :, 1], st[:, :, 4], ALU.add)
                dve.tensor_tensor(half_diff[:, :], st[:, :, 1], st[:, :, 4], ALU.subtract)
                done(dve.tensor_tensor(var[:, :], st[:, :, 2], st[:, :, 5], ALU.add))
                dve.tensor_scalar(mean[:, :], half_sum[:, :], 0.5, None, ALU.mult)
                done(dve.tensor_tensor(sq[:, :], half_diff[:, :], half_diff[:, :], ALU.mult))
                done(dve.tensor_scalar(sq[:, :], sq[:, :], 0.25, EPS, ALU.mult, ALU.add))
                dve.scalar_tensor_tensor(var[:, :], var[:, :], 1.0 / D, sq[:, :], ALU.mult, ALU.add)\
                   .then_inc(var_ready, 1)
                dve.wait_ge(root_ready, 1)
                done(dve.reciprocal(scale[:, :], root[:, :]))
                dve.scalar_tensor_tensor(shift[:, :], mean[:, :], -1.0, scale[:, :], ALU.mult, ALU.mult)

            @block.scalar
            def _(act):
                act.wait_ge(var_ready, 1)
                act.activation(root[:, :], var[:, :], ACT.Sqrt).then_inc(root_ready, 1)


def cross_phase(nc, persist, x1, ln_scale, ln_shift, ctx_d, ctxT_d, wT_d, wv_d, woT_d, bo_d, out_y, sumsq):
    ident = persist[0]
    XH = 8
    HW = D // XH
    with ExitStack() as c:
        def sb(name, shape, dt=F32):
            return c.enter_context(nc.sbuf_tensor(name, shape, dt))

        def sem(name):
            return c.enter_context(nc.semaphore(name))

        w_raw = [sb(f"xw_raw{i}", [P, D]) for i in range(2)]
        w_same = [sb(f"xw_same{i}", [P, D], F32R) for i in range(2)]
        w_cross = [sb(f"xw_cross{i}", [P, D], F32R) for i in range(2)]
        wv = sb("wv", [P, DC, HW])
        woT = sb("woT", [P, DC, HW])
        bo = sb("xbo", [P, 1])
        wvo = sb("wvo", [P, XH, HW])
        x_raw = sb("x_raw", [P, 2, D])
        x_split = sb("x_split", [P, 2, D], F32R)
        c_raw = sb("c_raw", [P, 2, D])
        c_split = sb("c_split", [P, 2, D], F32R)
        ctxT = sb("ctxT", [P, DC, 2, HW])
        e = sb("e", [P, 4, 2, D])
        kT = sb("ekT", [P, 2, 2, DC, P])
        q = sb("qs", [P, 2, DC, D])
        gT = sb("gT", [P, D])
        m = sb("m", [P, 2, DC, HW])
        k_max = sb("k_max", [P, 4, 2, 1])
        k_sum = sb("k_sum", [P, 2, DC])
        k_inv = sb("k_inv", [P, 2, DC])
        q_max = sb("q_max", [P, 2, 2, XH], BF16)
        q_sum = sb("q_sum", [P, 4, 2, XH])
        q_inv = sb("q_inv", [P, 4, 2, XH])
        square = sb("square", [P, D])
        half_ones = sb("half_ones", [P, 2])
        landed = sb("x_landed", [P, 2])
        ps = c.enter_context(nc.psum_tensor("ps_b", [P, 8, 512], F32))

        def proj_bank(s, b):
            return ps[:, 2 * (s % 2) + b, :]

        def t_bank(b):
            return ps[:, 4 + b, :]

        G, Y = ps[:, 6, :], ps[:, 7, :]
        m_bank = (G, Y)

        w_in = [sem("xwk_in"), sem("xwq_in")]
        small_in, w_rounded, w_split = sem("xsmall_in"), sem("xw_rounded"), sem("xw_split")
        wvo_done, wvo_ready, ones_step = sem("wvo_done"), sem("wvo_ready"), sem("ones_step")
        c_in, c_rounded, c_ready = sem("c_in"), sem("c_rounded"), sem("c_ready")
        x1_ready, x_in, x_rounded, x_ready = sem("x1_ready"), sem("x_in"), sem("x_rounded"), sem("x_ready")
        ctxT_in = sem("ctxT_in")
        p_done, kmax_done, qmax_done, shift_done, exp_done = (sem(n) for n in (
            "p_done", "kmax_done", "qmax_done", "xshift_done", "xexp_done"))
        sum_done, inv_done, q_ready = sem("sum_done"), sem("inv_done"), sem("q_ready")
        t_done, g_done, gT_ready = sem("xt_done"), sem("g_done"), sem("gT_ready")
        tcopy_done = [sem("tcopy_done0"), sem("tcopy_done1")]
        m_done, kinv_done, m_ready = sem("m_done"), sem("kinv_done"), sem("m_ready")
        waited, sp_waited = sem("waited"), sem("sp_waited")
        y_done, y_ready, sq_ready, sumsq_done, sumsq_ready = (sem(n) for n in (
            "xy_done", "xy_ready", "sq_ready", "sumsq_done", "sumsq_ready"))

        with nc.Block() as block:
            @block.sync
            def _(sp):
                def load_ctx(i):
                    for half in range(2):
                        sp.dma_start(c_raw[L * half:L * half + L, :, :],
                                     ctx_d[:, bass.ds(2 * i, 2), :]).then_inc(c_in, 16)

                def load_ctxT(i):
                    for b in range(2):
                        sp.dma_start(ctxT[:, :, b, :], ctxT_d[:, bass.ds((2 * i + b) * DC, DC), :]).then_inc(ctxT_in, 16)

                for w in range(2):
                    for half in range(2):
                        sp.dma_start(w_raw[w][L * half:L * half + L, :], wT_d[w]).then_inc(w_in[w], 16)
                    if w == 0:
                        load_ctx(0)
                sp.dma_start(wv[:, :, :], wv_d).then_inc(small_in, 16)
                sp.dma_start(woT[:, :, :], woT_d).then_inc(small_in, 16)
                for half in range(2):
                    sp.dma_start(bo[L * half:L * half + L, :], bo_d).then_inc(small_in, 16)
                load_ctxT(0)

                def load_x(i):
                    sp.wait_ge(x1_ready, i + 1)
                    sp.sem_inc(sp_waited, 1)
                    for b in range(2):
                        for half in range(2):
                            sp.dma_start(x_raw[L * half:L * half + L, b, :].unsqueeze(1),
                                         x1[L * b:L * b + L, bass.ds(i, 1), :]).then_inc(x_in, 16)

                load_x(0)
                with sp.Fori(0, PAIRS - 1) as i:
                    sp.wait_ge(c_ready, i + 1)
                    sp.sem_inc(sp_waited, 1)
                    load_ctx(i + 1)
                    sp.wait_ge(x_ready, i + 1)
                    sp.sem_inc(sp_waited, 1)
                    load_x(i + 1)
                    sp.wait_ge(g_done, 4 * i + 4)
                    sp.sem_inc(sp_waited, 1)
                    load_ctxT(i + 1)

            @block.gpsimd
            def _(pool):
                pool.memset(half_ones[:, :], 0.0).then_inc(ones_step, 1)
                for b in range(2):
                    pool.wait_ge(ones_step, b + 1)
                    pool.memset(half_ones[L * b:L * b + L, b:b + 1], 1.0).then_inc(ones_step, 1)
                pool.wait_ge(ones_step, 3)

                def low_part(split, raw, half):
                    rows = slice(L * half, L * half + L)
                    return pool.tensor_tensor(split[rows], raw[rows], split[rows].bitcast(F32), ALU.subtract)

                def split_ctx(i):
                    pool.wait_ge(c_rounded, i + 1)
                    low_part(c_split, c_raw, 1).then_inc(c_ready, 1)

                for w in range(2):
                    pool.wait_ge(w_rounded, 2 * w + 2)
                    low_part(w_same[w], w_raw[w], 1).then_inc(w_split, 1)
                    pool.wait_ge(w_split, 2 * w + 1)
                    low_part(w_cross[w], w_raw[w], 0).then_inc(w_split, 1)
                    pool.wait_ge(w_split, 2 * w + 2)
                    if w == 0:
                        split_ctx(0)
                        pool.wait_ge(c_ready, 1)

                def divide(i, n, b):
                    pool.wait_ge(inv_done, 8 * i + 2 * n + b + 1)
                    es = e[:, n, b, :].rearrange("p (h d) -> p h d", d=HW)
                    pool.tensor_tensor(es, es, q_inv[:, n, b, :].unsqueeze(2).broadcast_to([P, XH, HW]), ALU.mult)\
                        .then_inc(q_ready, 1)

                def iteration(i, first, last):
                    if not first:
                        for b in range(2):
                            divide(i - 1, 3, b)
                        pool.wait_ge(q_ready, 8 * i)
                    pool.wait_ge(x_rounded, i + 1)
                    low_part(x_split, x_raw, 1).then_inc(x_ready, 1)
                    pool.wait_ge(x_ready, i + 1)
                    if not first:
                        squares(i - 1)
                    if not last:
                        if not first:
                            pool.wait_ge(sq_ready, i)
                        split_ctx(i + 1)
                        pool.wait_ge(c_ready, i + 2)
                    for n in range(3):
                        for b in range(2):
                            divide(i, n, b)

                def squares(i):
                    pool.wait_ge(y_ready, i + 1)
                    ys = out_y[:, bass.ds(i, 1), :]
                    pool.tensor_tensor(square[:, :].unsqueeze(1), ys, ys, ALU.mult).then_inc(sq_ready, 1)

                iteration(0, True, False)
                with pool.Fori(1, PAIRS - 1) as i:
                    iteration(i, False, False)
                iteration(PAIRS - 1, False, True)
                for b in range(2):
                    divide(PAIRS - 1, 3, b)
                squares(PAIRS - 1)

            @block.scalar
            def _(act):
                def split_ctx(i):
                    act.wait_ge(c_in, 32 * i + 32)
                    act.activation(c_split[:, :, :], c_raw[:, :, :], ACT.Copy).then_inc(c_rounded, 1)

                for w in range(2):
                    act.wait_ge(w_in[w], 32)
                    for t in (w_same, w_cross):
                        act.activation(t[w][:, :], w_raw[w][:, :], ACT.Copy).then_inc(w_rounded, 1)
                    if w == 0:
                        split_ctx(0)

                act.wait_ge(wvo_done, 1)
                for odd in range(2):
                    act.activation(wvo[:, :, :].rearrange("p (j two) c -> p j two c", two=2)[:, :, odd, :],
                                   m_bank[odd][:, 0:DC * HW].rearrange("p (j c) -> p j c", c=HW),
                                   ACT.Copy, scale=HW ** -0.5).then_inc(wvo_ready, 1)

                def exp_k(i, j):
                    for b in range(2):
                        act.wait_ge(kmax_done, 8 * i + 2 * j + b + 1)
                        act.activation(e[:, j, b, :], proj_bank(j, b), ACT.Exp, bias=k_max[:, j, b, :],
                                       accum_out=k_sum[:, b, j:j + 1]).then_inc(exp_done, 1)

                def exp_q(i, n):
                    for b in range(2):
                        act.wait_ge(shift_done, 8 * i + 2 * n + b + 1)
                        act.activation(e[:, n, b, :], proj_bank(n, b), ACT.Exp).then_inc(exp_done, 1)

                def copy_k(i, j):
                    for b in range(2):
                        act.wait_ge(t_done, 16 * i + 2 * j + b + 1)
                        act.activation(kT[:, j % 2, b, :, :], t_bank(b).rearrange("p (n k) -> p n k", k=P), ACT.Copy)\
                           .then_inc(tcopy_done[b], 1)

                def copy_q(i, n):
                    for b in range(2):
                        act.wait_ge(t_done, 16 * i + 8 + 2 * n + b + 1)
                        act.activation(q[:, b, :, P * n:P * n + P], t_bank(b).rearrange("p (j n) -> p j n", n=P),
                                       ACT.Copy).then_inc(tcopy_done[b], 1)

                def copy_g(i):
                    act.wait_ge(g_done, 4 * i + 4)
                    act.activation(gT[:, :], G, ACT.Copy).then_inc(gT_ready, 1)

                def copy_y(i):
                    act.wait_ge(y_done, i + 1)
                    act.activation(out_y[:, bass.ds(i, 1), :], Y.unsqueeze(1), ACT.Identity, bias=bo[:, :])\
                       .then_inc(y_ready, 1)

                def iteration(i, first, last):
                    if not first:
                        exp_q(i - 1, 3)
                        copy_g(i - 1)
                    exp_k(i, 0)
                    if not first:
                        copy_q(i - 1, 1)
                    exp_k(i, 1)
                    exp_k(i, 2)
                    act.wait_ge(x_in, 64 * i + 64)
                    act.activation(x_split[:, :, :], x_raw[:, :, :], ACT.Copy).then_inc(x_rounded, 1)
                    exp_k(i, 3)
                    if not first:
                        copy_y(i - 1)
                    copy_k(i, 1)
                    if not last:
                        split_ctx(i + 1)
                    exp_q(i, 0)
                    copy_k(i, 2)
                    exp_q(i, 1)
                    copy_k(i, 3)
                    exp_q(i, 2)
                    copy_q(i, 0)

                act.wait_ge(small_in, 64)
                iteration(0, True, False)
                with act.Fori(1, PAIRS - 1) as i:
                    iteration(i, False, False)
                iteration(PAIRS - 1, False, True)
                exp_q(PAIRS - 1, 3)
                copy_g(PAIRS - 1)
                copy_q(PAIRS - 1, 1)
                copy_y(PAIRS - 1)

            @block.vector
            def _(dve):
                for s, n in ((exp_done, 4), (tcopy_done[0], 1), (tcopy_done[1], 1), (sumsq_ready, 1)):
                    dve.sem_inc(s, n)

                def max_k(i, j):
                    for b in range(2):
                        dve.wait_ge(p_done, 16 * i + 2 * j + b + 1)
                        dve.tensor_reduce(k_max[:, j, b, :], proj_bank(j, b), AX.X, ALU.max, negate=True)\
                           .then_inc(kmax_done, 1)

                def max_q(i, n):
                    for b in range(2):
                        dve.wait_ge(p_done, 16 * i + 8 + 2 * n + b + 1)
                        dve.tensor_reduce(q_max[:, n % 2, b, :], proj_bank(n, b).rearrange("p (h d) -> p h d", d=HW),
                                          AX.X, ALU.max, negate=True).then_inc(qmax_done, 1)

                def sum_q(i, n):
                    for b in range(2):
                        dve.wait_ge(exp_done, 16 * i + 8 + 2 * n + b + 5)
                        dve.tensor_reduce(q_sum[:, n, b, :], e[:, n, b, :].rearrange("p (h d) -> p h d", d=HW), AX.X,
                                          ALU.add).then_inc(sum_done, 1)
                        dve.wait_ge(sum_done, 8 * i + 2 * n + b + 1)
                        dve.reciprocal(q_inv[:, n, b, :], q_sum[:, n, b, :]).then_inc(inv_done, 1)

                def normalise(i):
                    rows = x1[:, bass.ds(i, 1), :]
                    dve.tensor_scalar(rows, rows, ln_scale[:, bass.ds(i, 1)], ln_shift[:, bass.ds(i, 1)],
                                      ALU.mult, ALU.add).then_inc(x1_ready, 1)

                def invert_k_sums(i):
                    dve.wait_ge(exp_done, 16 * i + 12)
                    dve.reciprocal(k_inv[:, :, :], k_sum[:, :, :]).then_inc(kinv_done, 1)

                def fold_sums(i):
                    dve.wait_ge(m_done, 2 * i + 2)
                    dve.wait_ge(kinv_done, i + 1)
                    for b in range(2):
                        dve.tensor_tensor(m[:, b, :, :], m_bank[b][:, 0:DC * HW].rearrange("p (j c) -> p j c", c=HW),
                                          k_inv[:, b, :].unsqueeze(2).broadcast_to([P, DC, HW]), ALU.mult)\
                           .then_inc(m_ready, 1)

                def copy_k(i, j):
                    for b in range(2):
                        dve.wait_ge(t_done, 16 * i + 2 * j + b + 1)
                        dve.tensor_copy(kT[:, j % 2, b, :, :], t_bank(b).rearrange("p (n k) -> p n k", k=P))\
                           .then_inc(tcopy_done[b], 1)

                def copy_q(i, n):
                    for b in range(2):
                        dve.wait_ge(t_done, 16 * i + 8 + 2 * n + b + 1)
                        dve.tensor_copy(q[:, b, :, P * n:P * n + P], t_bank(b).rearrange("p (j n) -> p j n", n=P))\
                           .then_inc(tcopy_done[b], 1)

                def copy_sumsq(i):
                    dve.wait_ge(sumsq_done, i + 1)
                    dve.tensor_scalar(sumsq[:, bass.ds(i * 8, 8)], Y[:, 0:8], 1e-24, None, ALU.max)\
                       .then_inc(sumsq_ready, 1)

                def iteration(i, first, last):
                    max_k(i, 0)
                    if not first:
                        sum_q(i - 1, 3)
                    max_k(i, 1)
                    if not first:
                        copy_q(i - 1, 2)
                        fold_sums(i - 1)
                    max_k(i, 2)
                    if not first:
                        copy_q(i - 1, 3)
                    max_k(i, 3)
                    copy_k(i, 0)
                    max_q(i, 0)
                    invert_k_sums(i)
                    if not last:
                        normalise(i + 1)
                    max_q(i, 1)
                    sum_q(i, 0)
                    max_q(i, 2)
                    sum_q(i, 1)
                    max_q(i, 3)
                    sum_q(i, 2)
                    if not first:
                        copy_sumsq(i - 1)

                normalise(0)
                iteration(0, True, False)
                with dve.Fori(1, PAIRS - 1) as i:
                    iteration(i, False, False)
                iteration(PAIRS - 1, False, True)
                sum_q(PAIRS - 1, 3)
                copy_q(PAIRS - 1, 2)
                fold_sums(PAIRS - 1)
                copy_q(PAIRS - 1, 3)
                copy_sumsq(PAIRS - 1)

            @block.tensor
            def _(pe):
                pe.wait_ge(small_in, 64)
                for j in range(DC):
                    for odd in range(2):
                        rows = slice(HW * odd, HW * odd + HW)
                        for half in range(2):
                            ins = pe.matmul(m_bank[odd][HW * half:HW * half + HW, HW * j:HW * j + HW], wv[rows, j, :],
                                            woT[rows, j, :], start=True, stop=True)
                ins.then_inc(wvo_done, 1)
                pe.wait_ge(wvo_ready, 2)

                def project_k(i, j):
                    if j == 0:
                        pe.wait_ge(c_ready, i + 1)
                    for b in range(2):
                        pe.wait_ge(exp_done, 16 * i + 2 * j + b + 1)
                        for r, w in enumerate((w_same[0], w_cross[0])):
                            ins = pe.matmul(proj_bank(j, b), w[:, P * j:P * j + P], c_split[:, b, :],
                                            start=(r == 0), stop=(r == 1))
                        ins.then_inc(p_done, 1)

                def project_q(i, n):
                    if n == 0:
                        pe.wait_ge(x_ready, i + 1)
                    for b in range(2):
                        pe.wait_ge(exp_done, 16 * i + 8 + 2 * n + b + 1)
                        for r, w in enumerate((w_same[1], w_cross[1])):
                            ins = pe.matmul(proj_bank(n, b), x_split[:, b, P * n:P * n + P], w[:, :],
                                            start=(r == 0), stop=(r == 1))
                        ins.then_inc(p_done, 1)

                def shift_q(i, n):
                    for b in range(2):
                        pe.wait_ge(qmax_done, 8 * i + 2 * n + b + 1)
                        pe.matmul(proj_bank(n, b).rearrange("p (h d) -> p h d", d=HW), persist[1][:, :],
                                  q_max[:, n % 2, b, :].unsqueeze(2).broadcast_to([P, XH, HW]), start=False, stop=True,
                                  skip_group_check=True).then_inc(shift_done, 1)

                def transpose_e(index, slot):
                    for b in range(2):
                        pe.wait_ge(tcopy_done[b], index + 1)
                        for r in range(4):
                            ins = pe.transpose(t_bank(b)[:, P * r:P * r + P], e[:, slot, b, P * r:P * r + P], ident[:, :])
                        ins.then_inc(t_done, 1)

                def transpose_k(i, j):
                    pe.wait_ge(exp_done, 16 * i + 2 * j + 6)
                    transpose_e(8 * i + j, j)

                def transpose_q(i, n):
                    pe.wait_ge(q_ready, 8 * i + 2 * n + 2)
                    transpose_e(8 * i + 4 + n, n)

                def keys_ctx(i, j):
                    for b in range(2):
                        pe.wait_ge(tcopy_done[b], 8 * i + j + 2)
                    if j == 0:
                        pe.wait_ge(ctxT_in, 32 * i + 32)
                    for n in range(DC):
                        for b in range(2):
                            ins = pe.matmul(G[HW * b:HW * b + HW, P * j:P * j + P], ctxT[:, n, b, :], kT[:, j % 2, b, n, :],
                                            start=(n == 0), stop=(n == DC - 1))
                    ins.then_inc(g_done, 1)

                def mix(i):
                    pe.wait_ge(gT_ready, i + 1)
                    pe.wait_ge(sumsq_ready, i + 1)
                    pe.sem_inc(waited, 1)
                    for b in range(2):
                        rows = slice(HW * b, HW * b + HW)
                        for h in range(XH):
                            half = h % 2
                            ins = pe.matmul(m_bank[b][HW * half:HW * half + HW, HW * (h // 2):HW * (h // 2) + HW],
                                            gT[rows, HW * h:HW * h + HW], wvo[rows, h, :], start=True, stop=True)
                        ins.then_inc(m_done, 1)

                def output(i):
                    pe.wait_ge(m_ready, 2 * i + 2)
                    for b in range(2):
                        pe.wait_ge(tcopy_done[b], 8 * i + 9)
                    for j in range(DC):
                        for b in range(2):
                            ins = pe.matmul(Y[HW * b:HW * b + HW, :], m[:, b, j, :], q[:, b, j, :],
                                            start=(j == 0), stop=(j == DC - 1))
                    ins.then_inc(y_done, 1)

                def sum_squares(i):
                    pe.wait_ge(sq_ready, i + 1)
                    for n in range(DC):
                        ins = pe.matmul(Y[:, 2 * n:2 * n + 2], square[:, P * n:P * n + P], half_ones[:, :],
                                        start=True, stop=True)
                    ins.then_inc(sumsq_done, 1)

                pe.wait_ge(ones_step, 3)
                pe.wait_ge(w_split, 4)

                def iteration(i, first):
                    project_k(i, 0)
                    if not first:
                        shift_q(i - 1, 3)
                        transpose_q(i - 1, 1)
                    project_k(i, 1)
                    if not first:
                        transpose_q(i - 1, 2)
                        mix(i - 1)
                    project_k(i, 2)
                    if not first:
                        transpose_q(i - 1, 3)
                    project_k(i, 3)
                    transpose_k(i, 0)
                    if not first:
                        output(i - 1)
                    project_q(i, 0)
                    transpose_k(i, 1)
                    keys_ctx(i, 0)
                    project_q(i, 1)
                    shift_q(i, 0)
                    transpose_k(i, 2)
                    keys_ctx(i, 1)
                    project_q(i, 2)
                    shift_q(i, 1)
                    transpose_k(i, 3)
                    keys_ctx(i, 2)
                    if not first:
                        sum_squares(i - 1)
                    project_q(i, 3)
                    shift_q(i, 2)
                    transpose_q(i, 0)
                    keys_ctx(i, 3)

                iteration(0, True)
                with pe.Fori(1, PAIRS) as i:
                    iteration(i, False)
                shift_q(PAIRS - 1, 3)
                transpose_q(PAIRS - 1, 1)
                transpose_q(PAIRS - 1, 2)
                mix(PAIRS - 1)
                transpose_q(PAIRS - 1, 3)
                output(PAIRS - 1)
                sum_squares(PAIRS - 1)


def inverse_norms(nc, sumsq):
    with ExitStack() as c:
        root = c.enter_context(nc.sbuf_tensor("norm", [P, PAIRS * 8], F32))
        root_ready = c.enter_context(nc.semaphore("norm_ready"))
        with nc.Block() as block:
            @block.scalar
            def _(act):
                act.activation(root[:, :], sumsq[:, :], ACT.Sqrt).then_inc(root_ready, 1)

            @block.vector
            def _(dve):
                dve.wait_ge(root_ready, 1)
                dve.reciprocal(sumsq[:, :], root[:, :])


def feed_forward_phase(nc, persist, x, cross_y, inv_norm, weights, w_in, g_d, out_d):
    ident = persist[0]
    wg, wu, wd = weights
    FC = wd.shape[1]
    with ExitStack() as c:
        def sb(name, shape, dt=F32):
            return c.enter_context(nc.sbuf_tensor(name, shape, dt))

        def sem(name):
            return c.enter_context(nc.semaphore(name))

        g_raw = sb("g_raw", [P, 1])
        g_scaled = sb("g_scaled", [P, 1])
        eps = sb("f_eps", [P, 1])
        inv_wide = sb("inv_wide", [P, 2, DC, 2, L])
        scaled = sb("scaled", [P, 2, D])
        z = sb("z", [P, 2, D])
        x2 = sb("x2", [P, 2, D])
        xT_hi = sb("x2T_hi", [P, DC, TOK], F16)
        xT_lo = sb("x2T_lo", [P, DC, TOK], F16)
        gate = sb("gate", [P, 2, TOK])
        h = sb("h", [P, 2, TOK])
        h_hi = sb("h_hi", [P, FC, TOK], BF16)
        h_lo = sb("h_lo", [P, FC, TOK], F16)
        y3 = sb("y3", [P, 2, D])
        result = sb("result", [P, 2, D])
        row_stats = sb("row_stats", [P, 4, 6])
        moments = sb("moments", [P, 4, 2])
        root = sb("f_root", [P, 4])
        scale = sb("f_scale", [P, 4])
        shift = sb("f_shift", [P, 4])
        ps = c.enter_context(nc.psum_tensor("ps_c", [P, 8, 512], F32))

        def GU(f):
            return ps[:, f % 2, :]

        def down(tt):
            return ps[:, 2 + tt, :]

        norm_bank = ps[:, 4, :]

        def T(p):
            return ps[:, 5 + p, :]

        g_in, consts_ready = sem("g_in"), sem("f_consts_ready")
        waited = sem("f_waited")
        wide_ready, norm_done, scaled_done, z_done, stats_done = (sem(n) for n in (
            "wide_ready", "norm_done", "scaled_done", "z_done", "stats_done"))
        moments_ready, root_ready, scale_ready, shift_ready = (sem(n) for n in (
            "moments_ready", "f_root_ready", "f_scale_ready", "f_shift_ready"))
        x2_ready, kept, t_done, hi_ready, xT_ready = (sem(n) for n in (
            "x2_ready", "x2_kept", "x2T_done", "x2T_hi_ready", "x2T_ready"))
        gu_done, silu_done, h_done, hhi_done, h_ready = (sem(n) for n in (
            "gu_done", "silu_done", "h_done", "h_hi_done", "h_ready"))
        down_done, y3_done, y3_stats, result_ready, stored = (sem(n) for n in (
            "down_done", "y3_done", "y3_stats", "result_ready", "stored"))

        with nc.Block() as block:
            @block.sync
            def _(sp):
                for half in range(2):
                    sp.dma_start(g_raw[L * half:L * half + L, :], g_d).then_inc(g_in, 16)

                def store(t):
                    sp.wait_ge(result_ready, 2 * t + 2)
                    sp.dma_start(out_d[:, bass.ds(2 * t, 2), :], result[:, :, :]).then_inc(stored, 16)

                sp.sem_inc(stored, 16)
                with sp.Fori(0, NT) as t:
                    store(t)
                sp.wait_ge(stored, 16 * NT + 16)

            @block.gpsimd
            def _(pool):
                def widen(t):
                    pool.wait_ge(norm_done, 2 * t + 1)
                    pool.sem_inc(waited, 1)
                    for p in range(2):
                        pool.tensor_copy(inv_wide[:, p, :, :, :].rearrange("p n b c -> p (n b) c"),
                                         inv_norm[:, bass.ds(16 * t + 8 * p, 8)].unsqueeze(2).broadcast_to([P, 8, L]))\
                            .then_inc(wide_ready, 1)

                def low(t, f):
                    pool.wait_ge(hhi_done, FC * t + f + 1)
                    pool.tensor_tensor(h_lo[:, f, :], h[:, f % 2, :], h_hi[:, f, :], ALU.subtract).then_inc(h_ready, 1)

                widen(0)

                def iteration(t, last):
                    if not last:
                        widen(t + 1)
                    for f in range(FC):
                        low(t, f)

                with pool.Fori(0, NT - 1) as t:
                    iteration(t, False)
                iteration(NT - 1, True)

            @block.scalar
            def _(act):
                act.wait_ge(g_in, 32)
                act.activation(g_scaled[:, :], g_raw[:, :], ACT.Copy, scale=float(L) ** 0.5).then_inc(consts_ready, 1)

                def roots(n):
                    act.wait_ge(moments_ready, n)
                    act.activation(root[:, :], moments[:, :, 1], ACT.Sqrt, bias=eps[:, :]).then_inc(root_ready, 1)

                def high(t, p):
                    act.wait_ge(t_done, 2 * t + p + 1)
                    act.activation(xT_hi[:, :, P * p:P * p + P], T(p).rearrange("p (c t) -> p c t", c=DC), ACT.Copy)\
                       .then_inc(hi_ready, 1)

                def silu(t, f):
                    act.wait_ge(gu_done, FC * t + f + 1)
                    act.activation(gate[:, f % 2, :], GU(f)[:, 0:TOK], ACT.Silu).then_inc(silu_done, 1)

                def h_high(t, f):
                    act.wait_ge(h_done, FC * t + f + 1)
                    act.activation(h_hi[:, f, :], h[:, f % 2, :], ACT.Copy).then_inc(hhi_done, 1)

                act.wait_ge(consts_ready, 3)
                roots(1)
                for p in range(2):
                    high(0, p)

                def iteration(t, last):
                    for f in range(FC):
                        if f == 6:
                            roots(t + 2)
                        silu(t, f)
                        if f >= 1:
                            h_high(t, f - 1)
                    if not last:
                        high(t + 1, 0)
                    h_high(t, FC - 1)
                    if not last:
                        high(t + 1, 1)

                with act.Fori(0, NT - 1) as t:
                    iteration(t, False)
                iteration(NT - 1, True)
                roots(NT + 2)

            @block.vector
            def _(dve):
                dve.memset(eps[:, :], EPS).then_inc(consts_ready, 1)
                dve.memset(moments[:, :, :], 1.0).then_inc(consts_ready, 1)
                for s, n in ((norm_done, 1), (h_ready, 2), (y3_done, 2)):
                    dve.sem_inc(s, n)
                dve.wait_ge(consts_ready, 3)

                def add(t, p):
                    pair = bass.ds(2 * t + p, 1)
                    dve.wait_ge(norm_done, 2 * t + p + 2)
                    dve.tensor_tensor(scaled[:, p:p + 1, :], norm_bank.unsqueeze(1), cross_y[:, pair, :], ALU.mult)\
                       .then_inc(scaled_done, 1)
                    dve.wait_ge(scaled_done, 2 * t + p + 1)
                    dve.scalar_tensor_tensor(z[:, p, :], scaled[:, p, :], g_scaled[:, :], x[:, pair, :].squeeze(1),
                                             ALU.mult, ALU.add).then_inc(z_done, 1)
                    dve.wait_ge(z_done, 2 * t + p + 1)
                    dve.bn_stats(row_stats[:, 2 + p, :], z[:, p, :]).then_inc(stats_done, 1)

                def aggregate(t, first_row, n):
                    dve.sem_inc(waited, 1)
                    for p in range(2):
                        ins = dve.bn_aggr(moments[:, first_row + p, :], row_stats[:, first_row + p, :])
                        if p == 1 and n is not None:
                            ins.then_inc(moments_ready, 1)

                def norm_terms(n):
                    dve.wait_ge(root_ready, n)
                    dve.reciprocal(scale[:, :], root[:, :]).then_inc(scale_ready, 1)
                    dve.wait_ge(scale_ready, n)
                    dve.scalar_tensor_tensor(shift[:, :], moments[:, :, 0], -1.0, scale[:, :], ALU.mult, ALU.mult)\
                       .then_inc(shift_ready, 1)
                    dve.wait_ge(shift_ready, n)

                def normalise(t):
                    for p in range(2):
                        dve.tensor_scalar(x2[:, p, :], z[:, p, :], scale[:, 2 + p:3 + p], shift[:, 2 + p:3 + p],
                                          ALU.mult, ALU.add).then_inc(x2_ready, 1)

                def keep(t):
                    for p in range(2):
                        dve.tensor_scalar(x[:, bass.ds(2 * t + p, 1), :], z[:, p:p + 1, :], scale[:, 2 + p:3 + p],
                                          shift[:, 2 + p:3 + p], ALU.mult, ALU.add).then_inc(kept, 1)

                def finish(t):
                    dve.wait_ge(stored, 16 * t + 16)
                    for p in range(2):
                        dve.tensor_scalar(result[:, p, :], y3[:, p, :], scale[:, p:p + 1], shift[:, p:p + 1],
                                          ALU.mult, ALU.add).then_inc(result_ready, 1)

                def low(t, p):
                    dve.wait_ge(hi_ready, 2 * t + p + 1)
                    dve.tensor_tensor(xT_lo[:, :, P * p:P * p + P], T(p).rearrange("p (c t) -> p c t", c=DC),
                                      xT_hi[:, :, P * p:P * p + P], ALU.subtract).then_inc(xT_ready, 1)

                def gated(t, f):
                    dve.wait_ge(silu_done, FC * t + f + 1)
                    dve.wait_ge(h_ready, FC * t + f + 1)
                    dve.tensor_tensor(h[:, f % 2, :], GU(f)[:, TOK:2 * TOK], gate[:, f % 2, :], ALU.mult)\
                       .then_inc(h_done, 1)

                def residual(t):
                    dve.wait_ge(down_done, t + 1)
                    dve.wait_ge(kept, 2 * t + 2)
                    for p in range(2):
                        dve.tensor_tensor(y3[:, p:p + 1, :], down(p).unsqueeze(1), x[:, bass.ds(2 * t + p, 1), :],
                                          ALU.add).then_inc(y3_done, 1)
                    for p in range(2):
                        dve.wait_ge(y3_done, 2 * t + p + 3)
                        dve.bn_stats(row_stats[:, p, :], y3[:, p, :]).then_inc(y3_stats, 1)

                for p in range(2):
                    add(0, p)
                dve.wait_ge(stats_done, 2)
                aggregate(0, 2, 1)
                norm_terms(1)
                normalise(0)
                keep(0)
                for p in range(2):
                    low(0, p)

                def iteration(t, first, last):
                    for f in range(FC):
                        gated(t, f)
                        if not last and f in (1, 3):
                            add(t + 1, f // 2)
                        if f == 3:
                            if not first:
                                dve.wait_ge(y3_stats, 2 * t)
                                aggregate(t, 0, None)
                            if not last:
                                dve.wait_ge(stats_done, 2 * t + 4)
                                aggregate(t, 2, 1)
                            else:
                                dve.wait_ge(y3_stats, 2 * t)
                                dve.tensor_copy(moments[:, 2:4, :], moments[:, 2:4, :]).then_inc(moments_ready, 1)
                        if f == 6:
                            norm_terms(t + 2)
                            if not last:
                                normalise(t + 1)
                                keep(t + 1)
                        if f == 7 and not first:
                            finish(t - 1)
                    if not last:
                        for p in range(2):
                            low(t + 1, p)
                    residual(t)

                iteration(0, True, False)
                with dve.Fori(1, NT - 1) as t:
                    iteration(t, False, False)
                iteration(NT - 1, False, True)
                dve.wait_ge(y3_stats, 2 * NT)
                aggregate(NT, 0, 1)
                norm_terms(NT + 2)
                finish(NT - 1)

            @block.tensor
            def _(pe):
                def spread_norms(t, p):
                    pe.wait_ge(wide_ready, 2 * t + p + 1)
                    if p == 1 or not isinstance(t, int) or t > 0:
                        pe.wait_ge(scaled_done, 2 * t + p)
                    for n in range(DC):
                        ins = pe.matmul(norm_bank[:, P * n:P * n + P],
                                        inv_wide[:, p, n, :, :].rearrange("p b c -> p (b c)"), ident[:, :],
                                        start=True, stop=True)
                    ins.then_inc(norm_done, 1)

                def transposes(t, p):
                    pe.wait_ge(x2_ready, 2 * t + p + 1)
                    for n in range(DC):
                        ins = pe.transpose(T(p)[:, P * n:P * n + P], x2[:, p, P * n:P * n + P], ident[:, :])
                    ins.then_inc(t_done, 1)

                def gate_up(t, f):
                    if f >= 2 or not isinstance(t, int) or t > 0:
                        pe.wait_ge(h_done, FC * t + f - 1)
                    fs = slice(P * f, P * f + P)
                    for k, w in enumerate((wg, wu)):
                        for cc in range(DC):
                            for r, part in enumerate((xT_hi, xT_lo)):
                                ins = pe.matmul(GU(f)[:, TOK * k:TOK * k + TOK], w[:, cc, fs], part[:, cc, :],
                                                start=(cc == 0 and r == 0), stop=(cc == DC - 1 and r == 1))
                    ins.then_inc(gu_done, 1)

                def down_product(t, f):
                    pe.wait_ge(h_ready, FC * t + f + 3)
                    if f == 0:
                        pe.wait_ge(y3_done, 2 * t + 2)
                    for tt in range(2):
                        for r, part in enumerate((h_hi, h_lo)):
                            ins = pe.matmul(down(tt), part[:, f, P * tt:P * tt + P], wd[:, f, :],
                                            start=(f == 0 and r == 0), stop=(f == FC - 1 and r == 1))
                    if f == FC - 1:
                        ins.then_inc(down_done, 1)

                for p in range(2):
                    spread_norms(0, p)
                for p in range(2):
                    transposes(0, p)
                pe.wait_ge(w_in, 48)

                def iteration(t, last):
                    pe.wait_ge(xT_ready, 2 * t + 2)
                    for f in range(FC):
                        gate_up(t, f)
                        if not last and f in (1, 3):
                            spread_norms(t + 1, f // 2)
                        if f >= 2 and f < FC - 1:
                            down_product(t, f - 2)
                    if not last:
                        for p in range(2):
                            transposes(t + 1, p)
                    for f in range(FC - 3, FC):
                        down_product(t, f)

                iteration(0, False)
                with pe.Fori(1, NT - 1) as t:
                    iteration(t, False)
                iteration(NT - 1, True)


def program(nc, x, xT, ctx, ctxT, wqT, wkT, wvT, woT, bq, bk, bv, bo, xwqT, xwkT, xwv, xwoT, xbo, g, wgT, wuT, wdT, out):
    with ExitStack() as c:
        y1 = c.enter_context(nc.sbuf_tensor("y1", [P, PAIRS, D], F32))
        ident = c.enter_context(nc.sbuf_tensor("ident", [P, P], F32))
        identb = c.enter_context(nc.sbuf_tensor("identb", [P, P], BF16))
        stats = c.enter_context(nc.sbuf_tensor("stats", [P, PAIRS * 6], F32))
        ln_scale = c.enter_context(nc.sbuf_tensor("ln_scale", [P, PAIRS], F32))
        ln_shift = c.enter_context(nc.sbuf_tensor("ln_shift", [P, PAIRS], F32))
        zeroed = c.enter_context(nc.semaphore("zeroed"))
        with nc.Block() as block:
            @block.gpsimd
            def _(pool):
                pool.memset(ident[:, :], 0.0).then_inc(zeroed, 1)
                pool.memset(identb[:, :], 0.0).then_inc(zeroed, 1)
                pool.wait_ge(zeroed, 2)
                for m in (ident, identb):
                    pool.affine_select(out=m[:, :], in_=m[:, :], compare_op=ALU.not_equal, fill=1.0, base=0,
                                       pattern=[[-1, P]], channel_multiplier=1).then_inc(zeroed, 1)
                pool.wait_ge(zeroed, 4)
        pairs = "(i b) l d -> (b l) i d"
        x_d = x.rearrange(pairs, b=2)
        attention_phase(nc, (ident, identb), x_d, xT.rearrange("(c p) t -> p c t", p=P),
                        [w.rearrange("(c p) f -> p c f", p=P) for w in (wqT, wkT, wvT, woT)],
                        (bq, bk),
                        bo.rearrange("(a d) -> a d", a=1).broadcast_to([P, D]),
                        bv.rearrange("(a d) -> a d", a=1).broadcast_to([P, D]), y1, stats)
        layer_norm_terms(nc, stats, ln_scale, ln_shift)
        cross_y = c.enter_context(nc.sbuf_tensor("cross_y", [P, PAIRS, D], F32))
        sumsq = c.enter_context(nc.sbuf_tensor("sumsq", [P, PAIRS * 8], F32))
        FC = wdT.shape[0] // P
        wg = c.enter_context(nc.sbuf_tensor("wg", [P, DC, FC * P], F16))
        wu = c.enter_context(nc.sbuf_tensor("wu", [P, DC, FC * P], F16))
        wd = c.enter_context(nc.sbuf_tensor("wd", [P, FC, D], F16))
        w_in = c.enter_context(nc.semaphore("ffn_w_in"))
        with nc.Block() as block:
            @block.sync
            def _(sp):
                for w, w_d in ((wg, wgT), (wu, wuT), (wd, wdT)):
                    sp.dma_start(w[:, :, :], w_d.rearrange("(c p) f -> p c f", p=P)).then_inc(w_in, 16)
        cross_phase(nc, (ident, identb), y1, ln_scale, ln_shift, ctx.rearrange("b l d -> l b d"),
                    ctxT.rearrange("b (n p) c -> p (b n) c", p=P), (xwkT, xwqT),
                    xwv.rearrange("(j p) c -> p j c", p=P), xwoT.rearrange("(j p) c -> p j c", p=P),
                    xbo.rearrange("(c a) -> c a", a=1), cross_y, sumsq)
        inverse_norms(nc, sumsq)
        feed_forward_phase(nc, (ident, identb), y1, cross_y, sumsq, (wg, wu, wd), w_in,
                           g.rearrange("(c a) -> c a", a=1), out.rearrange(pairs, b=2))


def kernel(**inputs):
    import numpy as _np
    import concourse.bacc as _bacc
    from concourse import mybir as _mybir
    from concourse.bass_utils import run_bass_kernel_spmd as _run

    nc = _bacc.Bacc("TRN2", target_bir_lowering=False, num_devices=1)
    i = {k: _np.asarray(v) for k, v in inputs.items()}
    given = {
        "x": i["x"], "xT": i["x"].reshape(B * L, D).T,
        "ctx": i["ctx_4096"], "ctxT": i["ctx_4096"].transpose(0, 2, 1),
        "wqT": i["L0_attn_Wq"].T, "wkT": i["L0_attn_Wk"].T, "wvT": i["L0_attn_Wv"].T, "woT": i["L0_attn_Wo"].T,
        "bq": i["L0_attn_bq"].reshape(DC, P).T, "bk": i["L0_attn_bk"].reshape(DC, P).T, "bv": i["L0_attn_bv"], "bo": i["L0_attn_bo"],
        "xwqT": i["L0_xattn_Wq"].T, "xwkT": i["L0_xattn_Wk"].T, "xwv": i["L0_xattn_Wv"], "xwoT": i["L0_xattn_Wo"].T,
        "xbo": i["L0_xattn_bo"], "g": i["L0_xattn_g"].reshape(L),
        "wgT": i["L0_ffn_W_gate"].T, "wuT": i["L0_ffn_W_up"].T, "wdT": i["L0_ffn_W_down"].T,
    }
    arrays, args = {}, []
    for name, a in given.items():
        a = _np.ascontiguousarray(a)
        arrays[f"in_{name}"] = a
        args.append(nc.dram_tensor(f"in_{name}", a.shape, _mybir.dt.from_np(a.dtype), kind="ExternalInput").ap())
    args.append(nc.dram_tensor("out", (B, L, D), _mybir.dt.float32, kind="ExternalOutput").ap())
    program(nc, *args)
    return _run(nc, [arrays], core_ids=[0]).results[0]["out"]
```

```python
from contextlib import ExitStack

import concourse.bass as bass
from concourse import mybir

F32 = mybir.dt.float32
F32R = mybir.dt.float32r
F16 = mybir.dt.float16
BF16 = mybir.dt.bfloat16
ACT = mybir.ActivationFunctionType
ALU = mybir.AluOpType
AX = mybir.AxisListType

P = 128
B, L, D, H = 32, 64, 512, 32
HD = D // H
DC = D // P
TOK = 256
NT = B * L // TOK
PAIRS = B // 2
HC = P // HD
VW = HD + 1
MASKED = -1.0e30
EPS = 1e-5
XH = 8
HW = D // XH


class CrossOperands:

    def __init__(self, nc, c):
        def sb(name, shape, dt=F32):
            return c.enter_context(nc.sbuf_tensor(name, shape, dt))

        def sem(name):
            return c.enter_context(nc.semaphore(name))

        self.w_raw = [sb(f"xw_raw{i}", [P, D]) for i in range(2)]
        self.w_same = [sb(f"xw_same{i}", [P, D], F32R) for i in range(2)]
        self.w_cross = [sb(f"xw_cross{i}", [P, D], F32R) for i in range(2)]
        self.wv, self.woT, self.bo = sb("wv", [P, DC, HW]), sb("woT", [P, DC, HW]), sb("xbo", [P, 1])
        self.c_raw, self.c_split = sb("c_raw", [P, 2, D]), sb("c_split", [P, 2, D], F32R)
        self.ctxT = sb("ctxT", [P, DC, 2, HW])
        self.w_in, self.small_in, self.w_rounded, self.w_split = (sem(n) for n in (
            "xw_in", "xsmall_in", "xw_rounded", "xw_split"))
        self.c_in, self.c_rounded, self.c_ready, self.ctxT_in = (sem(n) for n in (
            "c_in", "c_rounded", "c_ready", "ctxT_in"))


def low_part(pool, split, raw, half):
    rows = slice(L * half, L * half + L)
    return pool.tensor_tensor(split[rows], raw[rows], split[rows].bitcast(F32), ALU.subtract)


def attention_phase(nc, persist, x_d, xT_d, wT_d, b_d, bo_d, bv_d, y1, stats, cross, xwT_d, xwv_d, xwoT_d, xbo_d,
                    ctx_d, ctxT_d):
    ident, identb = persist
    with ExitStack() as c:
        def sb(name, shape, dt=F32):
            return c.enter_context(nc.sbuf_tensor(name, shape, dt))

        def sem(name):
            return c.enter_context(nc.semaphore(name))

        w_hi = [sb(f"w_hi{i}", [P, DC, D], F32R) for i in range(4)]
        w_lo = [sb(f"w_lo{i}", [P, DC, D], F32R) for i in range(4)]
        xT = sb("xT", [P, DC, TOK])
        xT_hi = sb("xT_hi", [P, DC, TOK], F32R)
        xT_lo = sb("xT_lo", [P, DC, TOK], F32R)
        xb = sb("xb", [P, 2, D])
        bo_all = sb("bo_all", [P, D])
        bv_all = sb("bv_all", [P, D])
        bq_col = sb("bq_col", [P, DC])
        bq_scaled = sb("bq_scaled", [P, DC])
        bk_col = sb("bk_col", [P, DC])
        qT = sb("qT", [P, DC, TOK])
        kT = sb("kT", [P, DC, TOK])
        k_diag = sb("k_diag", [P, DC, HC, TOK])
        v_diag = sb("v_diag", [P, 4, H // 2, 2 * VW])
        mask = sb("mask", [P, L], BF16)
        neg_max = sb("neg_max", [P, 2, HC], BF16)
        prob = sb("prob", [P, 2, 512])
        probT = sb("probT", [P, 2, 512])
        inv_sum = sb("inv_sum", [P, 2, 16])
        o = sb("o", [P, D])
        landed = sb("landed", [P, 2])
        oT_hi = sb("oT_hi", [P, DC, P], F32R)
        oT_lo = sb("oT_lo", [P, DC, P], F32R)
        ps = c.enter_context(nc.psum_tensor("ps_a", [P, 8, 512], F32))
        M0, M1 = ps[:, 0, :], ps[:, 1, :]

        def S(g):
            return ps[:, 2 + g % 2, :]

        def T(g):
            return ps[:, 4 + g % 2, :]

        O = ps[:, 6:8, :]

        consts_in, bo_in = sem("consts_in"), sem("bo_in")
        w_in = [sem(f"w_in{i}") for i in range(4)]
        w_hi_ready, w_ready = sem("w_hi_ready"), sem("w_ready")
        zeros_ready = sem("zeros_ready")
        pool_step, dve_step = sem("pool_step"), sem("dve_step")
        bq_ready = sem("bq_ready")
        xThi_ready = sem("xThi_ready")
        xT_in, xres_in, xT_ready, xb_ready = sem("xT_in"), sem("xres_in"), sem("xT_ready"), sem("xb_ready")
        qk_done, v_done = sem("qk_done"), sem("v_done")
        kT_ready, kdiag_ready, v_ready = sem("kT_ready"), sem("kdiag_ready"), sem("v_ready")
        m0_free, m1_free = sem("m0_free"), sem("m1_free")
        s_done, max_done, shift_done, exp_done = sem("s_done"), sem("max_done"), sem("shift_done"), sem("exp_done")
        t_done, probT_done, av_done = sem("t_done"), sem("probT_done"), sem("av_done")
        o_ready, oT_done, oThi_ready, oT_ready = sem("o_ready"), sem("oT_done"), sem("oThi_ready"), sem("oT_ready")
        proj_done, y_done = sem("proj_done"), sem("y_done")

        def staged(i):
            return y1[:, DC * i:DC * i + DC, :]

        with nc.Block() as block:
            @block.sync
            def _(sp):
                def load_xT(t):
                    sp.dma_start(xT[:, :, :], xT_d[:, :, bass.ds(t * TOK, TOK)]).then_inc(xT_in, 16)

                def load_xres(t):
                    sp.dma_start(xb[:, :, :], x_d[:, bass.ds(t * 2, 2), :]).then_inc(xres_in, 16)

                def diagonal(t):
                    sp.wait_ge(kT_ready, 4 * t + 4)
                    for h in range(HC):
                        sp.dma_start(k_diag[HD * h:HD * h + HD, :, h, :],
                                     kT[HD * h:HD * h + HD, :, :]).then_inc(kdiag_ready, 16)

                load_xT(0)
                for i in range(4):
                    sp.dma_start(staged(i), wT_d[i]).then_inc(w_in[i], 16)
                    if i == 1:
                        sp.dma_start(bq_col[:, :], b_d[0]).then_inc(consts_in, 16)
                        sp.dma_start(bk_col[:, :], b_d[1]).then_inc(consts_in, 16)
                        sp.dma_start(bv_all[:, :], bv_d).then_inc(consts_in, 16)
                load_xres(0)
                sp.dma_start(bo_all[:, :], bo_d).then_inc(bo_in, 16)
                sp.wait_ge(zeros_ready, 1)
                diagonal(0)
                sp.wait_ge(xT_ready, 1)
                load_xT(1)
                for half in range(2):
                    rows = slice(L * half, L * half + L)
                    for w in range(2):
                        sp.dma_start(cross.w_raw[w][rows, :], xwT_d[w]).then_inc(cross.w_in, 16)
                    sp.dma_start(cross.c_raw[rows, :, :], ctx_d[:, 0:2, :]).then_inc(cross.c_in, 16)
                    sp.dma_start(cross.bo[rows, :], xbo_d).then_inc(cross.small_in, 16)
                sp.dma_start(cross.wv[:, :, :], xwv_d).then_inc(cross.small_in, 16)
                sp.dma_start(cross.woT[:, :, :], xwoT_d).then_inc(cross.small_in, 16)
                for b in range(2):
                    sp.dma_start(cross.ctxT[:, :, b, :], ctxT_d[:, b * DC:b * DC + DC, :]).then_inc(cross.ctxT_in, 16)
                with sp.Fori(0, NT - 2) as t:
                    diagonal(t + 1)
                    sp.wait_ge(xT_ready, t + 2)
                    load_xT(t + 2)
                    sp.wait_ge(y_done, 2 * t + 4)
                    load_xres(t + 1)
                diagonal(NT - 1)
                sp.wait_ge(y_done, 2 * NT)
                load_xres(NT - 1)

            @block.gpsimd
            def _(pool):
                pool.memset(k_diag[:, :, :, :], 0.0).then_inc(zeros_ready, 1)
                pool.memset(mask[:, :], 0.0).then_inc(pool_step, 1)
                pool.memset(v_diag[:, :, :, :], 0.0).then_inc(pool_step, 1)
                for b in range(2):
                    pool.wait_ge(pool_step, 2 + b)
                    m = mask[L * b:L * b + L, :]
                    pool.affine_select(out=m, in_=m, compare_op=ALU.is_ge, fill=MASKED, base=0,
                                       pattern=[[-1, L]], channel_multiplier=1).then_inc(pool_step, 1)
                for half in range(2):
                    pool.wait_ge(pool_step, 4 + half)
                    pool.memset(v_diag[L * half:L * half + L, :, :, half * VW + HD], 1.0).then_inc(pool_step, 1)
                pool.wait_ge(pool_step, 6)

                def split_x(t):
                    pool.wait_ge(xThi_ready, t + 1)
                    pool.tensor_tensor(xT_lo[:, :, :], xT[:, :, :], xT_hi[:, :, :].bitcast(F32),
                                       ALU.subtract).then_inc(xT_ready, 1)

                split_x(0)
                pool.wait_ge(bo_in, 16)

                def residual(t):
                    pool.wait_ge(xres_in, 16 * t + 16)
                    for p in range(2):
                        ins = pool.tensor_tensor(xb[:, p, :], xb[:, p, :], bo_all[:, :], ALU.add)
                    ins.then_inc(xb_ready, 1)

                residual(0)
                with pool.Fori(0, NT - 1) as t:
                    split_x(t + 1)
                    residual(t + 1)

                pool.wait_ge(xb_ready, NT)
                for w in range(2):
                    pool.wait_ge(cross.w_rounded, 2 * w + 2)
                    low_part(pool, cross.w_same[w], cross.w_raw[w], 1).then_inc(cross.w_split, 1)
                    pool.wait_ge(cross.w_split, 2 * w + 1)
                    low_part(pool, cross.w_cross[w], cross.w_raw[w], 0).then_inc(cross.w_split, 1)
                    pool.wait_ge(cross.w_split, 2 * w + 2)
                pool.wait_ge(cross.c_rounded, 1)
                low_part(pool, cross.c_split, cross.c_raw, 1).then_inc(cross.c_ready, 1)

            @block.scalar
            def _(act):
                def split_x(t):
                    act.wait_ge(xT_in, 16 * t + 16)
                    act.activation(xT_hi[:, :, :], xT[:, :, :], ACT.Copy).then_inc(xThi_ready, 1)

                split_x(0)
                for i in range(4):
                    act.wait_ge(w_in[i], 16)
                    act.activation(w_hi[i][:, :, :], staged(i), ACT.Copy).then_inc(w_hi_ready, 1)
                act.wait_ge(consts_in, 48)
                act.activation(bq_scaled[:, :], bq_col[:, :], ACT.Copy, scale=HD ** -0.5).then_inc(bq_ready, 1)
                act.wait_ge(bq_ready, 1)

                def qk(t, f):
                    bank, free = (M0, m0_free) if f == 2 else (M1, m1_free)
                    act.wait_ge(qk_done, 4 * t + f + 1)
                    act.activation(qT[:, f, :], bank[:, 0:TOK], ACT.Identity, bias=bq_scaled[:, f:f + 1],
                                   scale=HD ** -0.5)
                    act.activation(kT[:, f, :], bank[:, TOK:2 * TOK], ACT.Identity,
                                   bias=bk_col[:, f:f + 1]).then_inc(kT_ready, 1)

                def exp(t, s):
                    act.wait_ge(shift_done, 8 * t + s + 1)
                    act.wait_ge(t_done, 8 * t + s + 1)
                    act.activation(prob[:, s % 2, :], S(s), ACT.Exp).then_inc(exp_done, 1)

                def oT(t, p):
                    act.wait_ge(oT_done, 2 * t + p + 1)
                    act.wait_ge(proj_done, 2 * t + p + 1)
                    act.activation(oT_hi[:, :, :], M0.rearrange("p (c t) -> p c t", c=DC), ACT.Copy)\
                       .then_inc(oThi_ready, 1)

                for f in range(4):
                    qk(0, f)

                def round_cross_operand(n):
                    if n < 2:
                        act.wait_ge(cross.w_in, 64)
                        for w in (cross.w_same, cross.w_cross):
                            act.activation(w[n][:, :], cross.w_raw[n][:, :], ACT.Copy).then_inc(cross.w_rounded, 1)
                    else:
                        act.wait_ge(cross.c_in, 32)
                        act.activation(cross.c_split[:, :, :], cross.c_raw[:, :, :], ACT.Copy)\
                           .then_inc(cross.c_rounded, 1)

                def attention(t, last):
                    if not last:
                        act.wait_ge(v_done, 2 * t + 2)
                        split_x(t + 1)
                    for s in range(8):
                        exp(t, s)
                        if last and s < 3:
                            round_cross_operand(s)
                    oT(t, 0)
                    if not last:
                        act.wait_ge(kdiag_ready, 16 * HC * (t + 1))
                        for f in range(4):
                            qk(t + 1, f)
                    oT(t, 1)

                with act.Fori(0, NT - 1) as t:
                    attention(t, False)
                attention(NT - 1, True)

            @block.vector
            def _(dve):
                for i in range(4):
                    dve.wait_ge(w_hi_ready, i + 1)
                    dve.tensor_tensor(w_lo[i][:, :, :], staged(i), w_hi[i][:, :, :].bitcast(F32),
                                      ALU.subtract).then_inc(w_ready, 1)
                for s, n in ((t_done, 2), (exp_done, 2), (probT_done, 2), (av_done, 2), (o_ready, 1), (proj_done, 1),
                             (y_done, 2)):
                    dve.sem_inc(s, n)
                dve.memset(landed[:, :], 0.0)
                dve.wait_ge(consts_in, 48)
                dve.wait_ge(pool_step, 6)

                def v(t, tt):
                    dve.wait_ge(v_done, 2 * t + tt + 1)
                    for b in range(2):
                        src = M1[L * b:L * b + L, :].rearrange("p (h two d) -> p h two d", two=2, d=HD)
                        bv = bv_all[L * b:L * b + L, :].rearrange("p (h two d) -> p h two d", two=2, d=HD)
                        for half in range(2):
                            ins = dve.tensor_tensor(
                                v_diag[L * half:L * half + L, 2 * tt + b, :, half * VW:half * VW + HD],
                                src[:, :, half, :], bv[:, :, half, :], ALU.add)
                            ins.then_inc(v_ready, 1)

                def row_max(t, s):
                    dve.wait_ge(s_done, 8 * t + s + 1)
                    dve.tensor_reduce(neg_max[:, s % 2, :], S(s).rearrange("p (h k) -> p h k", k=L), AX.X, ALU.max,
                                      negate=True).then_inc(max_done, 1)

                def evacuate(t, s):
                    dve.wait_ge(t_done, 8 * t + s + 3)
                    dve.wait_ge(av_done, 8 * t + s + 1)
                    dve.tensor_copy(probT[:, s % 2, :], T(s)).then_inc(probT_done, 1)

                def normalise(t, p):
                    dve.wait_ge(av_done, 8 * t + 4 * p + 6)
                    Oh = O[:, :, 0:16 * VW].rearrange("p n (h w) -> p n h w", w=VW)
                    dve.reciprocal(inv_sum[:, :, :], Oh[:, :, :, HD]).then_inc(dve_step, 1)
                    dve.wait_ge(dve_step, 2 * t + p + 1)
                    for n in range(2):
                        ins = dve.tensor_tensor(
                            o[:, 256 * n:256 * n + 256].rearrange("p (h d) -> p h d", d=HD), Oh[:, n, :, 0:HD],
                            inv_sum[:, n, :].unsqueeze(2).broadcast_to([P, 16, HD]), ALU.mult)
                    ins.then_inc(o_ready, 1)

                def oT(t, p):
                    dve.wait_ge(oThi_ready, 2 * t + p + 1)
                    dve.tensor_tensor(oT_lo[:, :, :], M0.rearrange("p (c t) -> p c t", c=DC),
                                      oT_hi[:, :, :].bitcast(F32), ALU.subtract).then_inc(oT_ready, 1)

                def y(t, p):
                    dve.wait_ge(proj_done, 2 * t + p + 2)
                    dve.wait_ge(xb_ready, t + 1)
                    dve.tensor_tensor(y1[:, bass.ds(2 * t + p, 1), :], M0.unsqueeze(1), xb[:, p:p + 1, :],
                                      ALU.add).then_inc(y_done, 1)
                    dve.wait_ge(y_done, 2 * t + p + 3)
                    dve.tensor_copy(landed[:, 0:1], landed[:, 1:2])
                    dve.bn_stats(stats[:, bass.ds((2 * t + p) * 6, 6)], y1[:, bass.ds(2 * t + p, 1), :])

                for tt in range(2):
                    v(0, tt)

                def attention(t, last):
                    for s in range(8):
                        row_max(t, s)
                        if s >= 2:
                            evacuate(t, s - 2)
                        if s == 6:
                            normalise(t, 0)
                    evacuate(t, 6)
                    oT(t, 0)
                    evacuate(t, 7)
                    y(t, 0)
                    normalise(t, 1)
                    oT(t, 1)
                    if not last:
                        v(t + 1, 0)
                    y(t, 1)
                    if not last:
                        v(t + 1, 1)

                with dve.Fori(0, NT - 1) as t:
                    attention(t, False)
                attention(NT - 1, True)

            @block.tensor
            def _(pe):
                def three(out, stat_hi, stat_lo, mov_hi, mov_lo, c, n=DC):
                    parts = [(stat_hi, mov_hi), (stat_hi, mov_lo), (stat_lo, mov_hi)]
                    for k, (a, b) in enumerate(parts):
                        ins = pe.matmul(out, a, b, start=(c == 0 and k == 0), stop=(c == n - 1 and k == 2))
                    return ins

                def qk(t, f, first=False):
                    for w in range(2):
                        bank = M0 if f == 2 else M1
                        if first:
                            pe.wait_ge(w_ready, w + 1)
                        for cc in range(DC):
                            fs = slice(P * f, P * f + P)
                            ins = three(bank[:, TOK * w:TOK * w + TOK], w_hi[w][:, cc, fs], w_lo[w][:, cc, fs],
                                        xT_hi[:, cc, :], xT_lo[:, cc, :], cc)
                    ins.then_inc(qk_done, 1)

                def v(t, tt):
                    for cc in range(DC):
                        ts = slice(P * tt, P * tt + P)
                        ins = three(M1, xT_hi[:, cc, ts], xT_lo[:, cc, ts], w_hi[2][:, cc, :], w_lo[2][:, cc, :], cc)
                    ins.then_inc(v_done, 1)

                def scores(t, s):
                    p, cc = s // 4, s % 4
                    if s == 0:
                        pe.wait_ge(kdiag_ready, 16 * HC * (t + 1))
                    pe.wait_ge(exp_done, 8 * t + s + 1)
                    pe.matmul(S(s).rearrange("p (h k) -> p h k", k=L), identb[:, :],
                              mask[:, :].unsqueeze(1).broadcast_to([P, HC, L]), start=True, stop=True)
                    for b in range(2):
                        ts = slice(L * (2 * p + b), L * (2 * p + b) + L)
                        ins = pe.matmul(S(s)[L * b:L * b + L, :].rearrange("p (h k) -> p h k", k=L),
                                        qT[:, cc, ts], k_diag[:, cc, :, ts], start=False, stop=True, skip_group_check=True)
                    ins.then_inc(s_done, 1)

                def shift(t, s):
                    pe.wait_ge(max_done, 8 * t + s + 1)
                    pe.matmul(S(s).rearrange("p (h k) -> p h k", k=L), identb[:, :],
                              neg_max[:, s % 2, :].unsqueeze(2).broadcast_to([P, HC, L]), start=False, stop=True,
                              skip_group_check=True).then_inc(shift_done, 1)

                def transposes(t, s):
                    pe.wait_ge(exp_done, 8 * t + s + 3)
                    pe.wait_ge(probT_done, 8 * t + s + 1)
                    for k in range(4):
                        ins = pe.transpose(T(s)[:, P * k:P * k + P], prob[:, s % 2, P * k:P * k + P], ident[:, :])
                    ins.then_inc(t_done, 1)

                def values(t, s):
                    p, cc = s // 4, s % 4
                    pe.wait_ge(probT_done, 8 * t + s + 3)
                    if cc == 0:
                        pe.wait_ge(o_ready, 2 * t + p + 1)
                    if s == 0:
                        pe.wait_ge(v_ready, 8 * t + 8)
                    for k in range(4):
                        hp = 4 * cc + k
                        for b in range(2):
                            ins = pe.matmul(O[L * b:L * b + L, hp // 8, 2 * VW * (hp % 8):2 * VW * (hp % 8 + 1)],
                                            probT[:, s % 2, P * k + L * b:P * k + L * b + L],
                                            v_diag[:, 2 * p + b, hp, :], start=True, stop=True)
                    ins.then_inc(av_done, 1)

                def oT(t, p):
                    pe.wait_ge(o_ready, 2 * t + p + 2)
                    for k in range(DC):
                        ins = pe.transpose(M0[:, P * k:P * k + P], o[:, P * k:P * k + P], ident[:, :])
                    ins.then_inc(oT_done, 1)

                def project(t, p):
                    pe.wait_ge(oT_ready, 2 * t + p + 1)
                    for cc in range(DC):
                        ins = three(M0, oT_hi[:, cc, :], oT_lo[:, cc, :], w_hi[3][:, cc, :], w_lo[3][:, cc, :], cc)
                    ins.then_inc(proj_done, 1)

                pe.wait_ge(xT_ready, 1)
                for f in range(4):
                    if f == 1 or f == 3:
                        pe.wait_ge(kT_ready, f)
                    qk(0, f, f == 0)
                pe.wait_ge(w_ready, 3)
                pe.wait_ge(kT_ready, 4)
                v(0, 0)
                pe.wait_ge(v_ready, 4)
                v(0, 1)
                pe.wait_ge(w_ready, 4)

                def attention(t, last):
                    for s in range(8):
                        scores(t, s)
                        if s >= 1:
                            shift(t, s - 1)
                        if s >= 2:
                            transposes(t, s - 2)
                        if s >= 3:
                            values(t, s - 3)
                    shift(t, 7)
                    transposes(t, 6)
                    values(t, 5)
                    pe.wait_ge(y_done, 2 * t + 2)
                    oT(t, 0)
                    if not last:
                        pe.wait_ge(xT_ready, t + 2)
                        pe.wait_ge(v_ready, 8 * t + 8)
                        qk(t + 1, 0)
                    transposes(t, 7)
                    values(t, 6)
                    project(t, 0)
                    if not last:
                        pe.wait_ge(kT_ready, 4 * t + 5)
                        qk(t + 1, 1)
                    values(t, 7)
                    pe.wait_ge(y_done, 2 * t + 3)
                    if not last:
                        qk(t + 1, 2)
                        pe.wait_ge(kT_ready, 4 * t + 6)
                        qk(t + 1, 3)
                        pe.wait_ge(kT_ready, 4 * t + 7)
                    oT(t, 1)
                    if not last:
                        pe.wait_ge(kT_ready, 4 * t + 8)
                        v(t + 1, 0)
                    project(t, 1)
                    if not last:
                        pe.wait_ge(v_ready, 8 * t + 12)
                        v(t + 1, 1)

                with pe.Fori(0, NT - 1) as t:
                    attention(t, False)
                attention(NT - 1, True)


def cross_phase(nc, persist, x1, stats, cross, ctx_d, ctxT_d, out_y, sumsq, ffn_weights, ffn_w_in, g_d, g_scaled, xT_hi, xT_lo):
    ident = persist[0]
    w_same, w_cross, wv, woT, bo = cross.w_same, cross.w_cross, cross.wv, cross.woT, cross.bo
    c_raw, c_split, ctxT = cross.c_raw, cross.c_split, cross.ctxT
    c_in, c_rounded, c_ready, ctxT_in = cross.c_in, cross.c_rounded, cross.c_ready, cross.ctxT_in
    with ExitStack() as c:
        def sb(name, shape, dt=F32):
            return c.enter_context(nc.sbuf_tensor(name, shape, dt))

        def sem(name):
            return c.enter_context(nc.semaphore(name))

        wvo = sb("wvo", [P, XH, HW])
        x_raw = sb("x_raw", [P, 2, D])
        x_split = sb("x_split", [P, 2, D], F32R)
        e = sb("e", [P, 4, 2, D])
        kT = sb("ekT", [P, 2, 2, DC, P])
        q = sb("qs", [P, 2, DC, D])
        gT = sb("gT", [P, D])
        m = sb("m", [P, 2, DC, HW])
        k_max = sb("k_max", [P, 4, 2, 1])
        k_sum = sb("k_sum", [P, 2, DC])
        k_inv = sb("k_inv", [P, 2, DC])
        q_max = sb("q_max", [P, 2, 2, XH], BF16)
        q_sum = sb("q_sum", [P, 4, 2, XH])
        q_inv = sb("q_inv", [P, 4, 2, XH])
        square = sb("square", [P, D])
        half_ones = sb("half_ones", [P, 2])
        half_sum, half_diff, var, sq, mean, ln_root, ln_scale, ln_shift = (sb(n, [P, PAIRS]) for n in (
            "ln_sum", "ln_diff", "ln_var", "ln_sq", "ln_mean", "ln_root", "ln_scale", "ln_shift"))
        ps = c.enter_context(nc.psum_tensor("ps_b", [P, 8, 512], F32))

        def proj_bank(s, b):
            return ps[:, 2 * (s % 2) + b, :]

        def t_bank(b):
            return ps[:, 4 + b, :]

        G, Y = ps[:, 6, :], ps[:, 7, :]
        m_bank = (G, Y)

        g_raw = sb("g_raw", [P, 1])
        inv_wide, scaled, z = x_raw, c_raw, e[:, 0, :, :]
        x2 = scaled
        r_norm, r_inv = sb("r_norm", [P, 2 * 2 * DC]), sb("r_inv", [P, 2 * 2 * DC])
        r_eps = sb("r_eps", [P, 1])
        r_stats, r_moments = sb("r_stats", [P, 2, 6]), sb("r_moments", [P, 2, 2])
        r_root, r_scale, r_shift = sb("r_root", [P, 2]), sb("r_scale", [P, 2]), sb("r_shift", [P, 2])
        g_in, g_ready = sem("g_in"), sem("g_ready")
        r_norm_ready, r_wide_ready, r_spread, r_step, r_moments_ready, r_root_ready, r_x2_ready, r_t_done, r_hi_ready = (
            sem(n) for n in ("r_norm_ready", "r_wide_ready", "r_spread", "r_step", "r_moments_ready", "r_root_ready",
                             "r_x2_ready", "r_t_done", "r_hi_ready"))
        ln_step, ln_var_ready, ln_root_ready = sem("ln_step"), sem("ln_var_ready"), sem("ln_root_ready")
        wvo_done, wvo_ready, ones_step = sem("wvo_done"), sem("wvo_ready"), sem("ones_step")
        x1_ready, x_in, x_rounded, x_ready = sem("x1_ready"), sem("x_in"), sem("x_rounded"), sem("x_ready")
        p_done, kmax_done, qmax_done, shift_done, exp_done = (sem(n) for n in (
            "p_done", "kmax_done", "qmax_done", "xshift_done", "xexp_done"))
        sum_done, inv_done, q_ready = sem("sum_done"), sem("inv_done"), sem("q_ready")
        t_done, g_done, gT_ready = sem("xt_done"), sem("g_done"), sem("gT_ready")
        tcopy_done = [sem("tcopy_done0"), sem("tcopy_done1")]
        m_done, kinv_done, m_ready = sem("m_done"), sem("kinv_done"), sem("m_ready")
        waited, sp_waited = sem("waited"), sem("sp_waited")
        y_done, y_ready, sq_ready, sumsq_done, sumsq_ready = (sem(n) for n in (
            "xy_done", "xy_ready", "sq_ready", "sumsq_done", "sumsq_ready"))

        with nc.Block() as block:
            @block.sync
            def _(sp):
                def load_ctx(i):
                    for half in range(2):
                        sp.dma_start(c_raw[L * half:L * half + L, :, :],
                                     ctx_d[:, bass.ds(2 * i, 2), :]).then_inc(c_in, 16)

                def load_ctxT(i):
                    for b in range(2):
                        sp.dma_start(ctxT[:, :, b, :], ctxT_d[:, bass.ds((2 * i + b) * DC, DC), :]).then_inc(ctxT_in, 16)

                def load_x(i):
                    sp.wait_ge(x1_ready, i + 1)
                    sp.sem_inc(sp_waited, 1)
                    for b in range(2):
                        for half in range(2):
                            sp.dma_start(x_raw[L * half:L * half + L, b, :].unsqueeze(1),
                                         x1[L * b:L * b + L, bass.ds(i, 1), :]).then_inc(x_in, 16)

                def load_next(i):
                    sp.wait_ge(c_ready, i + 1)
                    sp.sem_inc(sp_waited, 1)
                    load_ctx(i + 1)
                    sp.wait_ge(x_ready, i + 1)
                    sp.sem_inc(sp_waited, 1)
                    load_x(i + 1)
                    sp.wait_ge(g_done, 4 * i + 4)
                    sp.sem_inc(sp_waited, 1)
                    load_ctxT(i + 1)

                load_x(0)
                for half in range(2):
                    sp.dma_start(g_raw[L * half:L * half + L, :], g_d).then_inc(g_in, 16)
                load_next(0)
                for w, w_d in ffn_weights:
                    sp.dma_start(w[:, :, :], w_d).then_inc(ffn_w_in, 16)
                with sp.Fori(1, PAIRS - 1) as i:
                    load_next(i)

            @block.gpsimd
            def _(pool):
                pool.memset(half_ones[:, :], 0.0).then_inc(ones_step, 1)
                for b in range(2):
                    pool.wait_ge(ones_step, b + 1)
                    pool.memset(half_ones[L * b:L * b + L, b:b + 1], 1.0).then_inc(ones_step, 1)
                pool.wait_ge(ones_step, 3)

                def split_ctx(i):
                    pool.wait_ge(c_rounded, i + 1)
                    low_part(pool, c_split, c_raw, 1).then_inc(c_ready, 1)

                def divide(i, n, b):
                    pool.wait_ge(inv_done, 8 * i + 2 * n + b + 1)
                    es = e[:, n, b, :].rearrange("p (h d) -> p h d", d=HW)
                    pool.tensor_tensor(es, es, q_inv[:, n, b, :].unsqueeze(2).broadcast_to([P, XH, HW]), ALU.mult)\
                        .then_inc(q_ready, 1)

                def iteration(i, first, last):
                    if not first:
                        for b in range(2):
                            divide(i - 1, 3, b)
                        pool.wait_ge(q_ready, 8 * i)
                    pool.wait_ge(x_rounded, i + 1)
                    low_part(pool, x_split, x_raw, 1).then_inc(x_ready, 1)
                    pool.wait_ge(x_ready, i + 1)
                    if not first:
                        squares(i - 1)
                    if not last:
                        if not first:
                            pool.wait_ge(sq_ready, i)
                        split_ctx(i + 1)
                        pool.wait_ge(c_ready, i + 2)
                    for n in range(3):
                        for b in range(2):
                            divide(i, n, b)

                def squares(i):
                    pool.wait_ge(y_ready, i + 1)
                    ys = out_y[:, bass.ds(i, 1), :]
                    pool.tensor_tensor(square[:, :].unsqueeze(1), ys, ys, ALU.mult).then_inc(sq_ready, 1)

                iteration(0, True, False)
                with pool.Fori(1, PAIRS - 1) as i:
                    iteration(i, False, False)
                iteration(PAIRS - 1, False, True)
                for b in range(2):
                    divide(PAIRS - 1, 3, b)
                squares(PAIRS - 1)

            @block.scalar
            def _(act):
                def split_ctx(i):
                    act.wait_ge(c_in, 32 * i + 32)
                    act.activation(c_split[:, :, :], c_raw[:, :, :], ACT.Copy).then_inc(c_rounded, 1)

                act.wait_ge(ln_var_ready, 1)
                act.activation(ln_root[:, :], var[:, :], ACT.Sqrt).then_inc(ln_root_ready, 1)
                act.wait_ge(wvo_done, 1)
                for odd in range(2):
                    act.activation(wvo[:, :, :].rearrange("p (j two) c -> p j two c", two=2)[:, :, odd, :],
                                   m_bank[odd][:, 0:DC * HW].rearrange("p (j c) -> p j c", c=HW),
                                   ACT.Copy, scale=HW ** -0.5).then_inc(wvo_ready, 1)

                def exp_k(i, j):
                    for b in range(2):
                        act.wait_ge(kmax_done, 8 * i + 2 * j + b + 1)
                        act.activation(e[:, j, b, :], proj_bank(j, b), ACT.Exp, bias=k_max[:, j, b, :],
                                       accum_out=k_sum[:, b, j:j + 1]).then_inc(exp_done, 1)

                def exp_q(i, n):
                    for b in range(2):
                        act.wait_ge(shift_done, 8 * i + 2 * n + b + 1)
                        act.activation(e[:, n, b, :], proj_bank(n, b), ACT.Exp).then_inc(exp_done, 1)

                def copy_k(i, j):
                    for b in range(2):
                        act.wait_ge(t_done, 16 * i + 2 * j + b + 1)
                        act.activation(kT[:, j % 2, b, :, :], t_bank(b).rearrange("p (n k) -> p n k", k=P), ACT.Copy)\
                           .then_inc(tcopy_done[b], 1)

                def copy_q(i, n):
                    for b in range(2):
                        act.wait_ge(t_done, 16 * i + 8 + 2 * n + b + 1)
                        act.activation(q[:, b, :, P * n:P * n + P], t_bank(b).rearrange("p (j n) -> p j n", n=P),
                                       ACT.Copy).then_inc(tcopy_done[b], 1)

                def copy_g(i):
                    act.wait_ge(g_done, 4 * i + 4)
                    act.activation(gT[:, :], G, ACT.Copy).then_inc(gT_ready, 1)

                def copy_y(i):
                    act.wait_ge(y_done, i + 1)
                    act.activation(out_y[:, bass.ds(i, 1), :], Y.unsqueeze(1), ACT.Identity, bias=bo[:, :])\
                       .then_inc(y_ready, 1)

                def first_rows_high(p):
                    act.wait_ge(r_t_done, p + 1)
                    act.activation(xT_hi[:, :, P * p:P * p + P], ps[:, 2 + p, :].rearrange("p (c t) -> p c t", c=DC),
                                   ACT.Copy).then_inc(r_hi_ready, 1)

                def iteration(i, first, last):
                    if not first:
                        exp_q(i - 1, 3)
                        copy_q(i - 1, 1)
                        copy_g(i - 1)
                    exp_k(i, 0)
                    exp_k(i, 1)
                    exp_k(i, 2)
                    act.wait_ge(x_in, 64 * i + 64)
                    act.activation(x_split[:, :, :], x_raw[:, :, :], ACT.Copy).then_inc(x_rounded, 1)
                    exp_k(i, 3)
                    if not first:
                        copy_y(i - 1)
                    copy_k(i, 1)
                    if not last:
                        split_ctx(i + 1)
                    exp_q(i, 0)
                    copy_k(i, 2)
                    exp_q(i, 1)
                    copy_k(i, 3)
                    exp_q(i, 2)
                    copy_q(i, 0)

                act.wait_ge(cross.small_in, 64)
                iteration(0, True, False)
                act.wait_ge(g_in, 32)
                act.activation(g_scaled[:, :], g_raw[:, :], ACT.Copy, scale=float(L) ** 0.5).then_inc(g_ready, 1)
                with act.Fori(1, PAIRS - 1) as i:
                    iteration(i, False, False)
                iteration(PAIRS - 1, False, True)
                exp_q(PAIRS - 1, 3)
                copy_q(PAIRS - 1, 1)
                copy_g(PAIRS - 1)
                act.activation(r_norm[:, :], sumsq[:, 0:2 * 2 * DC], ACT.Sqrt).then_inc(r_norm_ready, 1)
                copy_y(PAIRS - 1)
                act.wait_ge(r_moments_ready, 1)
                act.activation(r_root[:, :], r_moments[:, :, 1], ACT.Sqrt, bias=r_eps[:, :]).then_inc(r_root_ready, 1)
                for p in range(2):
                    first_rows_high(p)

            @block.vector
            def _(dve):
                for s, n in ((exp_done, 4), (tcopy_done[0], 1), (tcopy_done[1], 1), (sumsq_ready, 1)):
                    dve.sem_inc(s, n)

                def max_k(i, j):
                    for b in range(2):
                        dve.wait_ge(p_done, 16 * i + 2 * j + b + 1)
                        dve.tensor_reduce(k_max[:, j, b, :], proj_bank(j, b), AX.X, ALU.max, negate=True)\
                           .then_inc(kmax_done, 1)

                def max_q(i, n):
                    for b in range(2):
                        dve.wait_ge(p_done, 16 * i + 8 + 2 * n + b + 1)
                        dve.tensor_reduce(q_max[:, n % 2, b, :], proj_bank(n, b).rearrange("p (h d) -> p h d", d=HW),
                                          AX.X, ALU.max, negate=True).then_inc(qmax_done, 1)

                def sum_q(i, n):
                    for b in range(2):
                        dve.wait_ge(exp_done, 16 * i + 8 + 2 * n + b + 5)
                        dve.tensor_reduce(q_sum[:, n, b, :], e[:, n, b, :].rearrange("p (h d) -> p h d", d=HW), AX.X,
                                          ALU.add).then_inc(sum_done, 1)
                        dve.wait_ge(sum_done, 8 * i + 2 * n + b + 1)
                        dve.reciprocal(q_inv[:, n, b, :], q_sum[:, n, b, :]).then_inc(inv_done, 1)

                def normalise(i):
                    rows = x1[:, bass.ds(i, 1), :]
                    dve.tensor_scalar(rows, rows, ln_scale[:, bass.ds(i, 1)], ln_shift[:, bass.ds(i, 1)],
                                      ALU.mult, ALU.add).then_inc(x1_ready, 1)

                def invert_k_sums(i):
                    dve.wait_ge(exp_done, 16 * i + 12)
                    dve.reciprocal(k_inv[:, :, :], k_sum[:, :, :]).then_inc(kinv_done, 1)

                def fold_sums(i):
                    dve.wait_ge(m_done, 2 * i + 2)
                    dve.wait_ge(kinv_done, i + 1)
                    for b in range(2):
                        dve.tensor_tensor(m[:, b, :, :], m_bank[b][:, 0:DC * HW].rearrange("p (j c) -> p j c", c=HW),
                                          k_inv[:, b, :].unsqueeze(2).broadcast_to([P, DC, HW]), ALU.mult)\
                           .then_inc(m_ready, 1)

                def copy_k(i, j):
                    for b in range(2):
                        dve.wait_ge(t_done, 16 * i + 2 * j + b + 1)
                        dve.tensor_copy(kT[:, j % 2, b, :, :], t_bank(b).rearrange("p (n k) -> p n k", k=P))\
                           .then_inc(tcopy_done[b], 1)

                def copy_q(i, n):
                    for b in range(2):
                        dve.wait_ge(t_done, 16 * i + 8 + 2 * n + b + 1)
                        dve.tensor_copy(q[:, b, :, P * n:P * n + P], t_bank(b).rearrange("p (j n) -> p j n", n=P))\
                           .then_inc(tcopy_done[b], 1)

                def copy_sumsq(i):
                    dve.wait_ge(sumsq_done, i + 1)
                    dve.tensor_scalar(sumsq[:, bass.ds(i * 8, 8)], Y[:, 0:8], 1e-24, None, ALU.max)\
                       .then_inc(sumsq_ready, 1)

                def layer_norm_variances():
                    st = stats[:, :].rearrange("p (i k) -> p i k", k=6)
                    dve.tensor_tensor(half_sum[:, :], st[:, :, 1], st[:, :, 4], ALU.add)
                    dve.tensor_tensor(half_diff[:, :], st[:, :, 1], st[:, :, 4], ALU.subtract)
                    dve.tensor_tensor(var[:, :], st[:, :, 2], st[:, :, 5], ALU.add).then_inc(ln_step, 1)
                    dve.wait_ge(ln_step, 1)
                    dve.tensor_scalar(mean[:, :], half_sum[:, :], 0.5, None, ALU.mult)
                    dve.tensor_tensor(sq[:, :], half_diff[:, :], half_diff[:, :], ALU.mult).then_inc(ln_step, 1)
                    dve.wait_ge(ln_step, 2)
                    dve.tensor_scalar(sq[:, :], sq[:, :], 0.25, EPS, ALU.mult, ALU.add).then_inc(ln_step, 1)
                    dve.wait_ge(ln_step, 3)
                    dve.scalar_tensor_tensor(var[:, :], var[:, :], 1.0 / D, sq[:, :], ALU.mult, ALU.add)\
                       .then_inc(ln_var_ready, 1)

                def layer_norm_terms():
                    dve.wait_ge(ln_root_ready, 1)
                    dve.reciprocal(ln_scale[:, :], ln_root[:, :]).then_inc(ln_step, 1)
                    dve.wait_ge(ln_step, 4)
                    dve.scalar_tensor_tensor(ln_shift[:, :], mean[:, :], -1.0, ln_scale[:, :], ALU.mult, ALU.mult)\
                       .then_inc(ln_step, 1)
                    dve.wait_ge(ln_step, 5)

                def iteration(i, first, last):
                    max_k(i, 0)
                    if first:
                        layer_norm_terms()
                        normalise(0)
                    if not first:
                        sum_q(i - 1, 3)
                    max_k(i, 1)
                    if not first:
                        copy_q(i - 1, 2)
                        fold_sums(i - 1)
                    max_k(i, 2)
                    if not first:
                        copy_q(i - 1, 3)
                    max_k(i, 3)
                    copy_k(i, 0)
                    max_q(i, 0)
                    invert_k_sums(i)
                    if not last:
                        normalise(i + 1)
                    max_q(i, 1)
                    sum_q(i, 0)
                    max_q(i, 2)
                    sum_q(i, 1)
                    max_q(i, 3)
                    sum_q(i, 2)
                    if not first:
                        copy_sumsq(i - 1)

                def first_rows_norms():
                    dve.wait_ge(r_norm_ready, 1)
                    dve.reciprocal(r_inv[:, :], r_norm[:, :]).then_inc(r_step, 1)
                    dve.wait_ge(r_step, 1)
                    dve.wait_ge(x_ready, PAIRS)
                    dve.wait_ge(c_ready, PAIRS)
                    for p in range(2):
                        dve.tensor_copy(inv_wide[:, p, :].rearrange("p (n c) -> p n c", c=L),
                                        r_inv[:, 2 * DC * p:2 * DC * p + 2 * DC].unsqueeze(2).broadcast_to([P, 2 * DC, L]))\
                           .then_inc(r_wide_ready, 1)

                def first_rows_add(p):
                    dve.wait_ge(r_spread, p + 1)
                    dve.tensor_tensor(scaled[:, p, :], ps[:, p, :], out_y[:, p, :], ALU.mult).then_inc(r_step, 1)
                    dve.wait_ge(r_step, 3 * p + 2)
                    dve.scalar_tensor_tensor(z[:, p, :], scaled[:, p, :], g_scaled[:, :], x1[:, p, :],
                                             ALU.mult, ALU.add).then_inc(r_step, 1)
                    dve.wait_ge(r_step, 3 * p + 3)
                    dve.bn_stats(r_stats[:, p, :], z[:, p, :]).then_inc(r_step, 1)

                def first_rows_normalise():
                    dve.wait_ge(r_step, 7)
                    for p in range(2):
                        ins = dve.bn_aggr(r_moments[:, p, :], r_stats[:, p, :])
                    ins.then_inc(r_moments_ready, 1)
                    dve.wait_ge(r_root_ready, 1)
                    dve.reciprocal(r_scale[:, :], r_root[:, :]).then_inc(r_step, 1)
                    dve.wait_ge(r_step, 8)
                    dve.scalar_tensor_tensor(r_shift[:, :], r_moments[:, :, 0], -1.0, r_scale[:, :], ALU.mult, ALU.mult)\
                       .then_inc(r_step, 1)
                    dve.wait_ge(r_step, 9)
                    for p in range(2):
                        dve.tensor_scalar(x2[:, p, :], z[:, p, :], r_scale[:, p:p + 1], r_shift[:, p:p + 1],
                                          ALU.mult, ALU.add).then_inc(r_x2_ready, 1)
                    for p in range(2):
                        dve.tensor_scalar(x1[:, p, :], z[:, p, :], r_scale[:, p:p + 1], r_shift[:, p:p + 1],
                                          ALU.mult, ALU.add)

                def first_rows_low(p):
                    dve.wait_ge(r_hi_ready, p + 1)
                    dve.tensor_tensor(xT_lo[:, :, P * p:P * p + P], ps[:, 2 + p, :].rearrange("p (c t) -> p c t", c=DC),
                                      xT_hi[:, :, P * p:P * p + P], ALU.subtract)

                layer_norm_variances()
                dve.memset(r_eps[:, :], EPS)
                iteration(0, True, False)
                with dve.Fori(1, PAIRS - 1) as i:
                    iteration(i, False, False)
                iteration(PAIRS - 1, False, True)
                sum_q(PAIRS - 1, 3)
                copy_q(PAIRS - 1, 2)
                fold_sums(PAIRS - 1)
                copy_q(PAIRS - 1, 3)
                first_rows_norms()
                dve.wait_ge(g_ready, 1)
                for p in range(2):
                    first_rows_add(p)
                copy_sumsq(PAIRS - 1)
                first_rows_normalise()
                for p in range(2):
                    first_rows_low(p)

            @block.tensor
            def _(pe):
                pe.wait_ge(cross.small_in, 64)
                for j in range(DC):
                    for odd in range(2):
                        rows = slice(HW * odd, HW * odd + HW)
                        for half in range(2):
                            ins = pe.matmul(m_bank[odd][HW * half:HW * half + HW, HW * j:HW * j + HW], wv[rows, j, :],
                                            woT[rows, j, :], start=True, stop=True)
                ins.then_inc(wvo_done, 1)

                def project_k(i, j):
                    if j == 0:
                        pe.wait_ge(c_ready, i + 1)
                    for b in range(2):
                        pe.wait_ge(exp_done, 16 * i + 2 * j + b + 1)
                        for r, w in enumerate((w_same[0], w_cross[0])):
                            ins = pe.matmul(proj_bank(j, b), w[:, P * j:P * j + P], c_split[:, b, :],
                                            start=(r == 0), stop=(r == 1))
                        ins.then_inc(p_done, 1)

                def project_q(i, n):
                    if n == 0:
                        pe.wait_ge(x_ready, i + 1)
                    for b in range(2):
                        pe.wait_ge(exp_done, 16 * i + 8 + 2 * n + b + 1)
                        for r, w in enumerate((w_same[1], w_cross[1])):
                            ins = pe.matmul(proj_bank(n, b), x_split[:, b, P * n:P * n + P], w[:, :],
                                            start=(r == 0), stop=(r == 1))
                        ins.then_inc(p_done, 1)

                def shift_q(i, n):
                    for b in range(2):
                        pe.wait_ge(qmax_done, 8 * i + 2 * n + b + 1)
                        pe.matmul(proj_bank(n, b).rearrange("p (h d) -> p h d", d=HW), persist[1][:, :],
                                  q_max[:, n % 2, b, :].unsqueeze(2).broadcast_to([P, XH, HW]), start=False, stop=True,
                                  skip_group_check=True).then_inc(shift_done, 1)

                def transpose_e(index, slot):
                    for b in range(2):
                        pe.wait_ge(tcopy_done[b], index + 1)
                        for r in range(4):
                            ins = pe.transpose(t_bank(b)[:, P * r:P * r + P], e[:, slot, b, P * r:P * r + P], ident[:, :])
                        ins.then_inc(t_done, 1)

                def transpose_k(i, j):
                    pe.wait_ge(exp_done, 16 * i + 2 * j + 6)
                    transpose_e(8 * i + j, j)

                def transpose_q(i, n):
                    pe.wait_ge(q_ready, 8 * i + 2 * n + 2)
                    transpose_e(8 * i + 4 + n, n)

                def keys_ctx(i, j):
                    for b in range(2):
                        pe.wait_ge(tcopy_done[b], 8 * i + j + 2)
                    if j == 0:
                        pe.wait_ge(ctxT_in, 32 * i + 32)
                    for n in range(DC):
                        for b in range(2):
                            ins = pe.matmul(G[HW * b:HW * b + HW, P * j:P * j + P], ctxT[:, n, b, :], kT[:, j % 2, b, n, :],
                                            start=(n == 0), stop=(n == DC - 1))
                    ins.then_inc(g_done, 1)

                def mix(i):
                    pe.wait_ge(gT_ready, i + 1)
                    pe.wait_ge(sumsq_ready, i + 1)
                    pe.sem_inc(waited, 1)
                    for b in range(2):
                        rows = slice(HW * b, HW * b + HW)
                        for h in range(XH):
                            half = h % 2
                            ins = pe.matmul(m_bank[b][HW * half:HW * half + HW, HW * (h // 2):HW * (h // 2) + HW],
                                            gT[rows, HW * h:HW * h + HW], wvo[rows, h, :], start=True, stop=True)
                        ins.then_inc(m_done, 1)

                def output(i):
                    pe.wait_ge(m_ready, 2 * i + 2)
                    for b in range(2):
                        pe.wait_ge(tcopy_done[b], 8 * i + 9)
                    for j in range(DC):
                        for b in range(2):
                            ins = pe.matmul(Y[HW * b:HW * b + HW, :], m[:, b, j, :], q[:, b, j, :],
                                            start=(j == 0), stop=(j == DC - 1))
                    ins.then_inc(y_done, 1)

                def sum_squares(i):
                    pe.wait_ge(sq_ready, i + 1)
                    for n in range(DC):
                        ins = pe.matmul(Y[:, 2 * n:2 * n + 2], square[:, P * n:P * n + P], half_ones[:, :],
                                        start=True, stop=True)
                    ins.then_inc(sumsq_done, 1)

                pe.wait_ge(ones_step, 3)
                pe.wait_ge(cross.w_split, 4)

                def iteration(i, first):
                    project_k(i, 0)
                    if not first:
                        shift_q(i - 1, 3)
                        transpose_q(i - 1, 1)
                    project_k(i, 1)
                    if not first:
                        transpose_q(i - 1, 2)
                        mix(i - 1)
                    project_k(i, 2)
                    if not first:
                        transpose_q(i - 1, 3)
                    project_k(i, 3)
                    transpose_k(i, 0)
                    if not first:
                        output(i - 1)
                    project_q(i, 0)
                    transpose_k(i, 1)
                    if first:
                        pe.wait_ge(wvo_ready, 2)
                    keys_ctx(i, 0)
                    project_q(i, 1)
                    shift_q(i, 0)
                    transpose_k(i, 2)
                    keys_ctx(i, 1)
                    project_q(i, 2)
                    shift_q(i, 1)
                    transpose_k(i, 3)
                    keys_ctx(i, 2)
                    if not first:
                        sum_squares(i - 1)
                    project_q(i, 3)
                    shift_q(i, 2)
                    transpose_q(i, 0)
                    keys_ctx(i, 3)

                iteration(0, True)
                with pe.Fori(1, PAIRS) as i:
                    iteration(i, False)
                shift_q(PAIRS - 1, 3)
                transpose_q(PAIRS - 1, 1)
                transpose_q(PAIRS - 1, 2)
                mix(PAIRS - 1)
                transpose_q(PAIRS - 1, 3)
                for p in range(2):
                    pe.wait_ge(r_wide_ready, p + 1)
                    for n in range(DC):
                        ins = pe.matmul(ps[:, p, P * n:P * n + P], inv_wide[:, p, P * n:P * n + P], ident[:, :],
                                        start=True, stop=True)
                    ins.then_inc(r_spread, 1)
                output(PAIRS - 1)
                sum_squares(PAIRS - 1)
                for p in range(2):
                    pe.wait_ge(r_x2_ready, p + 1)
                    for n in range(DC):
                        ins = pe.transpose(ps[:, 2 + p, P * n:P * n + P], x2[:, p, P * n:P * n + P], ident[:, :])
                    ins.then_inc(r_t_done, 1)


def feed_forward_phase(nc, persist, x, cross_y, sumsq, weights, w_in, g_scaled, xT_hi, xT_lo, out_d):
    ident = persist[0]
    wg, wu, wd = weights
    FC = wd.shape[1]
    with ExitStack() as c:
        def sb(name, shape, dt=F32):
            return c.enter_context(nc.sbuf_tensor(name, shape, dt))

        def sem(name):
            return c.enter_context(nc.semaphore(name))

        norm, inv_norm = sb("norm", [P, PAIRS * 8]), sb("inv_norm", [P, PAIRS * 8])
        eps = sb("f_eps", [P, 1])
        inv_wide = sb("inv_wide", [P, 2, DC, 2, L])
        scaled = sb("scaled", [P, 2, D])
        z = sb("z", [P, 2, D])
        x2 = sb("x2", [P, 2, D])
        gate = sb("gate", [P, 2, TOK])
        h = sb("h", [P, 2, TOK])
        h_hi = sb("h_hi", [P, FC, TOK], BF16)
        h_lo = sb("h_lo", [P, FC, TOK], F16)
        y3 = sb("y3", [P, 2, D])
        result = sb("result", [P, 2, D])
        row_stats = sb("row_stats", [P, 4, 6])
        moments = sb("moments", [P, 4, 2])
        root = sb("f_root", [P, 4])
        scale = sb("f_scale", [P, 4])
        shift = sb("f_shift", [P, 4])
        ps = c.enter_context(nc.psum_tensor("ps_c", [P, 8, 512], F32))

        def GU(f):
            return ps[:, f % 2, :]

        def down(tt):
            return ps[:, 2 + tt, :]

        norm_bank = ps[:, 4, :]

        def T(p):
            return ps[:, 5 + p, :]

        consts_ready, norm_ready, inv_ready = sem("f_consts_ready"), sem("norm_ready"), sem("inv_ready")
        waited = sem("f_waited")
        wide_ready, norm_done, scaled_done, z_done, stats_done = (sem(n) for n in (
            "wide_ready", "norm_done", "scaled_done", "z_done", "stats_done"))
        moments_ready, root_ready, scale_ready, shift_ready = (sem(n) for n in (
            "moments_ready", "f_root_ready", "f_scale_ready", "f_shift_ready"))
        x2_ready, kept, t_done, hi_ready, xT_ready = (sem(n) for n in (
            "x2_ready", "x2_kept", "x2T_done", "x2T_hi_ready", "x2T_ready"))
        gu_done, silu_done, h_done, hhi_done, h_ready = (sem(n) for n in (
            "gu_done", "silu_done", "h_done", "h_hi_done", "h_ready"))
        down_done, y3_done, y3_stats, result_ready, stored = (sem(n) for n in (
            "down_done", "y3_done", "y3_stats", "result_ready", "stored"))

        with nc.Block() as block:
            @block.sync
            def _(sp):
                def store(t):
                    sp.wait_ge(result_ready, 2 * t + 2)
                    sp.dma_start(out_d[:, bass.ds(2 * t, 2), :], result[:, :, :]).then_inc(stored, 16)

                sp.sem_inc(stored, 16)
                with sp.Fori(0, NT) as t:
                    store(t)
                sp.wait_ge(stored, 16 * NT + 16)

            @block.gpsimd
            def _(pool):
                def widen(t):
                    pool.wait_ge(norm_done, 2 * t + 1)
                    pool.sem_inc(waited, 1)
                    for p in range(2):
                        pool.tensor_copy(inv_wide[:, p, :, :, :].rearrange("p n b c -> p (n b) c"),
                                         inv_norm[:, bass.ds(16 * t + 8 * p, 8)].unsqueeze(2).broadcast_to([P, 8, L]))\
                            .then_inc(wide_ready, 1)

                def low(t, f):
                    pool.wait_ge(hhi_done, FC * t + f + 1)
                    pool.tensor_tensor(h_lo[:, f, :], h[:, f % 2, :], h_hi[:, f, :], ALU.subtract).then_inc(h_ready, 1)

                pool.wait_ge(inv_ready, 1)

                def iteration(t, last):
                    if not last:
                        widen(t + 1)
                    for f in range(FC):
                        low(t, f)

                with pool.Fori(0, NT - 1) as t:
                    iteration(t, False)
                iteration(NT - 1, True)

            @block.scalar
            def _(act):
                act.activation(norm[:, :], sumsq[:, :], ACT.Sqrt).then_inc(norm_ready, 1)

                def roots(n):
                    act.wait_ge(moments_ready, n)
                    act.activation(root[:, :], moments[:, :, 1], ACT.Sqrt, bias=eps[:, :]).then_inc(root_ready, 1)

                def high(t, p):
                    act.wait_ge(t_done, 2 * t + p + 1)
                    act.activation(xT_hi[:, :, P * p:P * p + P], T(p).rearrange("p (c t) -> p c t", c=DC), ACT.Copy)\
                       .then_inc(hi_ready, 1)

                def silu(t, f):
                    act.wait_ge(gu_done, FC * t + f + 1)
                    act.activation(gate[:, f % 2, :], GU(f)[:, 0:TOK], ACT.Silu).then_inc(silu_done, 1)

                def h_high(t, f):
                    act.wait_ge(h_done, FC * t + f + 1)
                    act.activation(h_hi[:, f, :], h[:, f % 2, :], ACT.Copy).then_inc(hhi_done, 1)

                act.wait_ge(consts_ready, 2)

                def iteration(t, last):
                    for f in range(FC):
                        if f == 6:
                            roots(t + 2)
                        silu(t, f)
                        if f >= 1:
                            h_high(t, f - 1)
                    if not last:
                        high(t + 1, 0)
                    h_high(t, FC - 1)
                    if not last:
                        high(t + 1, 1)

                with act.Fori(0, NT - 1) as t:
                    iteration(t, False)
                iteration(NT - 1, True)
                roots(NT + 2)

            @block.vector
            def _(dve):
                dve.memset(eps[:, :], EPS).then_inc(consts_ready, 1)
                dve.memset(moments[:, :, :], 1.0).then_inc(consts_ready, 1)
                for s, n in ((norm_done, 1 + 2), (h_ready, 2), (y3_done, 2), (wide_ready, 2), (scaled_done, 2),
                             (z_done, 2), (stats_done, 2), (moments_ready, 1), (root_ready, 1), (scale_ready, 1),
                             (shift_ready, 1), (x2_ready, 2), (kept, 2), (t_done, 2), (hi_ready, 2), (xT_ready, 2)):
                    dve.sem_inc(s, n)
                dve.wait_ge(consts_ready, 2)
                dve.wait_ge(norm_ready, 1)
                dve.reciprocal(inv_norm[:, :], norm[:, :]).then_inc(inv_ready, 1)

                def add(t, p):
                    pair = bass.ds(2 * t + p, 1)
                    dve.wait_ge(norm_done, 2 * t + p + 2)
                    dve.tensor_tensor(scaled[:, p:p + 1, :], norm_bank.unsqueeze(1), cross_y[:, pair, :], ALU.mult)\
                       .then_inc(scaled_done, 1)
                    dve.wait_ge(scaled_done, 2 * t + p + 1)
                    dve.scalar_tensor_tensor(z[:, p, :], scaled[:, p, :], g_scaled[:, :], x[:, pair, :].squeeze(1),
                                             ALU.mult, ALU.add).then_inc(z_done, 1)
                    dve.wait_ge(z_done, 2 * t + p + 1)
                    dve.bn_stats(row_stats[:, 2 + p, :], z[:, p, :]).then_inc(stats_done, 1)

                def aggregate(t, first_row, n):
                    dve.sem_inc(waited, 1)
                    for p in range(2):
                        ins = dve.bn_aggr(moments[:, first_row + p, :], row_stats[:, first_row + p, :])
                        if p == 1 and n is not None:
                            ins.then_inc(moments_ready, 1)

                def norm_terms(n):
                    dve.wait_ge(root_ready, n)
                    dve.reciprocal(scale[:, :], root[:, :]).then_inc(scale_ready, 1)
                    dve.wait_ge(scale_ready, n)
                    dve.scalar_tensor_tensor(shift[:, :], moments[:, :, 0], -1.0, scale[:, :], ALU.mult, ALU.mult)\
                       .then_inc(shift_ready, 1)
                    dve.wait_ge(shift_ready, n)

                def normalise(t):
                    for p in range(2):
                        dve.tensor_scalar(x2[:, p, :], z[:, p, :], scale[:, 2 + p:3 + p], shift[:, 2 + p:3 + p],
                                          ALU.mult, ALU.add).then_inc(x2_ready, 1)

                def keep(t):
                    for p in range(2):
                        dve.tensor_scalar(x[:, bass.ds(2 * t + p, 1), :], z[:, p:p + 1, :], scale[:, 2 + p:3 + p],
                                          shift[:, 2 + p:3 + p], ALU.mult, ALU.add).then_inc(kept, 1)

                def finish(t):
                    dve.wait_ge(stored, 16 * t + 16)
                    for p in range(2):
                        dve.tensor_scalar(result[:, p, :], y3[:, p, :], scale[:, p:p + 1], shift[:, p:p + 1],
                                          ALU.mult, ALU.add).then_inc(result_ready, 1)

                def low(t, p):
                    dve.wait_ge(hi_ready, 2 * t + p + 1)
                    dve.tensor_tensor(xT_lo[:, :, P * p:P * p + P], T(p).rearrange("p (c t) -> p c t", c=DC),
                                      xT_hi[:, :, P * p:P * p + P], ALU.subtract).then_inc(xT_ready, 1)

                def gated(t, f):
                    dve.wait_ge(silu_done, FC * t + f + 1)
                    dve.wait_ge(h_ready, FC * t + f + 1)
                    dve.tensor_tensor(h[:, f % 2, :], GU(f)[:, TOK:2 * TOK], gate[:, f % 2, :], ALU.mult)\
                       .then_inc(h_done, 1)

                def residual(t):
                    dve.wait_ge(down_done, t + 1)
                    dve.wait_ge(kept, 2 * t + 2)
                    for p in range(2):
                        dve.tensor_tensor(y3[:, p:p + 1, :], down(p).unsqueeze(1), x[:, bass.ds(2 * t + p, 1), :],
                                          ALU.add).then_inc(y3_done, 1)
                    for p in range(2):
                        dve.wait_ge(y3_done, 2 * t + p + 3)
                        dve.bn_stats(row_stats[:, p, :], y3[:, p, :]).then_inc(y3_stats, 1)

                def iteration(t, first, last):
                    for f in range(FC):
                        gated(t, f)
                        if not last and f in (1, 3):
                            add(t + 1, f // 2)
                        if f == 3:
                            if not first:
                                dve.wait_ge(y3_stats, 2 * t)
                                aggregate(t, 0, None)
                            if not last:
                                dve.wait_ge(stats_done, 2 * t + 4)
                                aggregate(t, 2, 1)
                            else:
                                dve.wait_ge(y3_stats, 2 * t)
                                dve.tensor_copy(moments[:, 2:4, :], moments[:, 2:4, :]).then_inc(moments_ready, 1)
                        if f == 6:
                            norm_terms(t + 2)
                            if not last:
                                normalise(t + 1)
                                keep(t + 1)
                        if f == 7 and not first:
                            finish(t - 1)
                    if not last:
                        for p in range(2):
                            low(t + 1, p)
                    residual(t)

                iteration(0, True, False)
                with dve.Fori(1, NT - 1) as t:
                    iteration(t, False, False)
                iteration(NT - 1, False, True)
                dve.wait_ge(y3_stats, 2 * NT)
                aggregate(NT, 0, 1)
                norm_terms(NT + 2)
                finish(NT - 1)

            @block.tensor
            def _(pe):
                def spread_norms(t, p):
                    pe.wait_ge(wide_ready, 2 * t + p + 1)
                    pe.wait_ge(scaled_done, 2 * t + p)
                    for n in range(DC):
                        ins = pe.matmul(norm_bank[:, P * n:P * n + P],
                                        inv_wide[:, p, n, :, :].rearrange("p b c -> p (b c)"), ident[:, :],
                                        start=True, stop=True)
                    ins.then_inc(norm_done, 1)

                def transposes(t, p):
                    pe.wait_ge(x2_ready, 2 * t + p + 1)
                    for n in range(DC):
                        ins = pe.transpose(T(p)[:, P * n:P * n + P], x2[:, p, P * n:P * n + P], ident[:, :])
                    ins.then_inc(t_done, 1)

                def gate_up(t, f):
                    if f >= 2 or not isinstance(t, int) or t > 0:
                        pe.wait_ge(h_done, FC * t + f - 1)
                    fs = slice(P * f, P * f + P)
                    for k, w in enumerate((wg, wu)):
                        for cc in range(DC):
                            for r, part in enumerate((xT_hi, xT_lo)):
                                ins = pe.matmul(GU(f)[:, TOK * k:TOK * k + TOK], w[:, cc, fs], part[:, cc, :],
                                                start=(cc == 0 and r == 0), stop=(cc == DC - 1 and r == 1))
                    ins.then_inc(gu_done, 1)

                def down_product(t, f):
                    pe.wait_ge(h_ready, FC * t + f + 3)
                    if f == 0:
                        pe.wait_ge(y3_done, 2 * t + 2)
                    for tt in range(2):
                        for r, part in enumerate((h_hi, h_lo)):
                            ins = pe.matmul(down(tt), part[:, f, P * tt:P * tt + P], wd[:, f, :],
                                            start=(f == 0 and r == 0), stop=(f == FC - 1 and r == 1))
                    if f == FC - 1:
                        ins.then_inc(down_done, 1)

                pe.wait_ge(w_in, 48)

                def iteration(t, last):
                    pe.wait_ge(xT_ready, 2 * t + 2)
                    for f in range(FC):
                        gate_up(t, f)
                        if not last and f in (1, 3):
                            spread_norms(t + 1, f // 2)
                        if f >= 2 and f < FC - 1:
                            down_product(t, f - 2)
                    if not last:
                        for p in range(2):
                            transposes(t + 1, p)
                    for f in range(FC - 3, FC):
                        down_product(t, f)

                iteration(0, False)
                with pe.Fori(1, NT - 1) as t:
                    iteration(t, False)
                iteration(NT - 1, True)


def program(nc, x, xT, ctx, ctxT, wqT, wkT, wvT, woT, bq, bk, bv, bo, xwqT, xwkT, xwv, xwoT, xbo, g, wgT, wuT, wdT, out):
    with ExitStack() as c:
        y1 = c.enter_context(nc.sbuf_tensor("y1", [P, PAIRS, D], F32))
        ident = c.enter_context(nc.sbuf_tensor("ident", [P, P], F32))
        identb = c.enter_context(nc.sbuf_tensor("identb", [P, P], BF16))
        stats = c.enter_context(nc.sbuf_tensor("stats", [P, PAIRS * 6], F32))
        cross = CrossOperands(nc, c)
        ctx_l, ctxT_n = ctx.rearrange("b l d -> l b d"), ctxT.rearrange("b (n p) c -> p (b n) c", p=P)
        zeroed = c.enter_context(nc.semaphore("zeroed"))
        with nc.Block() as block:
            @block.gpsimd
            def _(pool):
                pool.memset(ident[:, :], 0.0).then_inc(zeroed, 1)
                pool.memset(identb[:, :], 0.0).then_inc(zeroed, 1)
                pool.wait_ge(zeroed, 2)
                for m in (ident, identb):
                    pool.affine_select(out=m[:, :], in_=m[:, :], compare_op=ALU.not_equal, fill=1.0, base=0,
                                       pattern=[[-1, P]], channel_multiplier=1).then_inc(zeroed, 1)
                pool.wait_ge(zeroed, 4)
        pairs = "(i b) l d -> (b l) i d"
        x_d = x.rearrange(pairs, b=2)
        attention_phase(nc, (ident, identb), x_d, xT.rearrange("(c p) t -> p c t", p=P),
                        [w.rearrange("(c p) f -> p c f", p=P) for w in (wqT, wkT, wvT, woT)],
                        (bq, bk),
                        bo.rearrange("(a d) -> a d", a=1).broadcast_to([P, D]),
                        bv.rearrange("(a d) -> a d", a=1).broadcast_to([P, D]), y1, stats, cross, (xwkT, xwqT),
                        xwv.rearrange("(j p) c -> p j c", p=P), xwoT.rearrange("(j p) c -> p j c", p=P),
                        xbo.rearrange("(c a) -> c a", a=1), ctx_l, ctxT_n)
        cross_y = c.enter_context(nc.sbuf_tensor("cross_y", [P, PAIRS, D], F32))
        sumsq = c.enter_context(nc.sbuf_tensor("sumsq", [P, PAIRS * 8], F32))
        FC = wdT.shape[0] // P
        wg = c.enter_context(nc.sbuf_tensor("wg", [P, DC, FC * P], F16))
        wu = c.enter_context(nc.sbuf_tensor("wu", [P, DC, FC * P], F16))
        wd = c.enter_context(nc.sbuf_tensor("wd", [P, FC, D], F16))
        w_in = c.enter_context(nc.semaphore("ffn_w_in"))
        g_scaled = c.enter_context(nc.sbuf_tensor("g_scaled", [P, 1], F32))
        x2T_hi = c.enter_context(nc.sbuf_tensor("x2T_hi", [P, DC, TOK], F16))
        x2T_lo = c.enter_context(nc.sbuf_tensor("x2T_lo", [P, DC, TOK], F16))
        cross_phase(nc, (ident, identb), y1, stats, cross, ctx_l, ctxT_n, cross_y, sumsq,
                    [(w, w_d.rearrange("(c p) f -> p c f", p=P)) for w, w_d in ((wg, wgT), (wu, wuT), (wd, wdT))], w_in,
                    g.rearrange("(c a) -> c a", a=1), g_scaled, x2T_hi, x2T_lo)
        feed_forward_phase(nc, (ident, identb), y1, cross_y, sumsq, (wg, wu, wd), w_in, g_scaled, x2T_hi, x2T_lo,
                           out.rearrange(pairs, b=2))


def kernel(**inputs):
    import numpy as _np
    import concourse.bacc as _bacc
    from concourse import mybir as _mybir
    from concourse.bass_utils import run_bass_kernel_spmd as _run

    nc = _bacc.Bacc("TRN2", target_bir_lowering=False, num_devices=1)
    i = {k: _np.asarray(v) for k, v in inputs.items()}
    given = {
        "x": i["x"], "xT": i["x"].reshape(B * L, D).T,
        "ctx": i["ctx_4096"], "ctxT": i["ctx_4096"].transpose(0, 2, 1),
        "wqT": i["L0_attn_Wq"].T, "wkT": i["L0_attn_Wk"].T, "wvT": i["L0_attn_Wv"].T, "woT": i["L0_attn_Wo"].T,
        "bq": i["L0_attn_bq"].reshape(DC, P).T, "bk": i["L0_attn_bk"].reshape(DC, P).T, "bv": i["L0_attn_bv"], "bo": i["L0_attn_bo"],
        "xwqT": i["L0_xattn_Wq"].T, "xwkT": i["L0_xattn_Wk"].T, "xwv": i["L0_xattn_Wv"], "xwoT": i["L0_xattn_Wo"].T,
        "xbo": i["L0_xattn_bo"], "g": i["L0_xattn_g"].reshape(L),
        "wgT": i["L0_ffn_W_gate"].T, "wuT": i["L0_ffn_W_up"].T, "wdT": i["L0_ffn_W_down"].T,
    }
    arrays, args = {}, []
    for name, a in given.items():
        a = _np.ascontiguousarray(a)
        arrays[f"in_{name}"] = a
        args.append(nc.dram_tensor(f"in_{name}", a.shape, _mybir.dt.from_np(a.dtype), kind="ExternalInput").ap())
    args.append(nc.dram_tensor("out", (B, L, D), _mybir.dt.float32, kind="ExternalOutput").ap())
    program(nc, *args)
    return _run(nc, [arrays], core_ids=[0]).results[0]["out"]
```

```python
from contextlib import ExitStack

import concourse.bass as bass
from concourse import mybir

F32 = mybir.dt.float32
F32R = mybir.dt.float32r
F16 = mybir.dt.float16
BF16 = mybir.dt.bfloat16
ACT = mybir.ActivationFunctionType
ALU = mybir.AluOpType
AX = mybir.AxisListType

P = 128
B, L, D, H = 32, 64, 512, 32
HD = D // H
DC = D // P
TOK = 256
NT = B * L // TOK
PAIRS = B // 2
HC = P // HD
VW = HD + 1
MASKED = -1.0e30
EPS = 1e-5
XH = 8
HW = D // XH


class CrossOperands:

    def __init__(self, nc, c):
        def sb(name, shape, dt=F32):
            return c.enter_context(nc.sbuf_tensor(name, shape, dt))

        def sem(name):
            return c.enter_context(nc.semaphore(name))

        self.w_raw = [sb(f"xw_raw{i}", [P, D]) for i in range(2)]
        self.w_same = [sb(f"xw_same{i}", [P, D], F32R) for i in range(2)]
        self.w_cross = [sb(f"xw_cross{i}", [P, D], F32R) for i in range(2)]
        self.bo = sb("xbo", [P, 1])
        self.c_raw, self.c_split = sb("c_raw", [P, 2, D]), sb("c_split", [P, 2, D], F32R)
        self.wvo = sb("wvo", [P, XH, HW])
        self.wvo_done, self.wvo_ready = sem("wvo_done"), sem("wvo_ready")
        self.w_in, self.small_in, self.w_rounded, self.w_split = (sem(n) for n in (
            "xw_in", "xsmall_in", "xw_rounded", "xw_split"))
        self.c_in, self.c_rounded, self.c_ready = (sem(n) for n in ("c_in", "c_rounded", "c_ready"))


def low_part(pool, split, raw, half):
    rows = slice(L * half, L * half + L)
    return pool.tensor_tensor(split[rows], raw[rows], split[rows].bitcast(F32), ALU.subtract)


def attention_phase(nc, ident, x_d, xT_d, wT_d, b_d, bo_d, bv_d, y1, stats, cross, xwT_d, xwv_d, xwoT_d, xbo_d,
                    ctx_d):
    with ExitStack() as c:
        def sb(name, shape, dt=F32):
            return c.enter_context(nc.sbuf_tensor(name, shape, dt))

        def sem(name):
            return c.enter_context(nc.semaphore(name))

        w_hi = [sb(f"w_hi{i}", [P, DC, D], F32R) for i in range(4)]
        w_lo = [sb(f"w_lo{i}", [P, DC, D], F32R) for i in range(4)]
        xT = sb("xT", [P, DC, TOK])
        xT_hi = sb("xT_hi", [P, DC, TOK], F32R)
        xT_lo = sb("xT_lo", [P, DC, TOK], F32R)
        xb = sb("xb", [P, 2, D])
        bo_all = sb("bo_all", [P, D])
        bv_all = sb("bv_all", [P, D])
        bq_col = sb("bq_col", [P, DC])
        bq_scaled = sb("bq_scaled", [P, DC])
        bk_col = sb("bk_col", [P, DC])
        qT = sb("qT", [P, DC, TOK])
        kT = sb("kT", [P, DC, TOK])
        wv, woT = kT[:, :, 0:HW], kT[:, :, HW:2 * HW]
        k_diag = sb("k_diag", [P, DC, HC, TOK])
        v_diag = sb("v_diag", [P, 4, H // 2, 2 * VW])
        mask = sb("mask", [P, L])
        neg_max = sb("neg_max", [P, 4, HC])
        prob = sb("prob", [P, 4, 512])
        probT = sb("probT", [P, 2, 512])
        inv_sum = sb("inv_sum", [P, 2, 16])
        o = sb("o", [P, D])
        landed = sb("landed", [P, 2])
        oT_hi = sb("oT_hi", [P, DC, P], F32R)
        oT_lo = sb("oT_lo", [P, DC, P], F32R)
        ps = c.enter_context(nc.psum_tensor("ps_a", [P, 8, 512], F32))
        M0, M1 = ps[:, 0, :], ps[:, 1, :]

        def S(g):
            return ps[:, 2 + g % 2, :]

        def T(g):
            return ps[:, 4 + g % 2, :]

        def o_bank(p):
            return (M0, T(0))[p]

        O = ps[:, 6:8, :]

        bias_in, bv_in, bo_in = sem("bias_in"), sem("bv_in"), sem("bo_in")
        pieces = [(0, 0, DC // 2), (0, DC // 2, DC), (1, 0, DC), (2, 0, DC), (3, 0, DC)]
        w_in = [sem(f"w_in{i}") for i in range(len(pieces))]
        w_hi_ready, w_ready = sem("w_hi_ready"), sem("w_ready")
        zeros_ready = sem("zeros_ready")
        pool_step, dve_step = sem("pool_step"), sem("dve_step")
        bq_ready = sem("bq_ready")
        xThi_ready = sem("xThi_ready")
        xT_in, xres_in, xT_ready, xb_ready = sem("xT_in"), sem("xres_in"), sem("xT_ready"), sem("xb_ready")
        kq_done, v_done = sem("kq_done"), sem("v_done")
        kq_ready, kdiag_ready, v_ready = sem("kq_ready"), sem("kdiag_ready"), sem("v_ready")
        masked_done = sem("masked_done")
        s_done, max_done, shift_done, exp_done = sem("s_done"), sem("max_done"), sem("shift_done"), sem("exp_done")
        t_done, probT_done, av_done = sem("t_done"), sem("probT_done"), sem("av_done")
        o_ready, oT_done, oThi_ready, oT_ready = sem("o_ready"), sem("oT_done"), sem("oThi_ready"), sem("oT_ready")
        proj_done, y_done = sem("proj_done"), sem("y_done")

        def staged(piece):
            w, first, end = pieces[piece]
            return y1[:, DC * w + first:DC * w + end, :]

        def split_of(parts, piece):
            w, first, end = pieces[piece]
            return parts[w][:, first:end, :]

        with nc.Block() as block:
            @block.sync
            def _(sp):
                def load_xT(t):
                    sp.dma_start(xT[:, :, :], xT_d[:, :, bass.ds(t * TOK, TOK)]).then_inc(xT_in, 16)

                def load_xres(t):
                    sp.dma_start(xb[:, :, :], x_d[:, bass.ds(t * 2, 2), :]).then_inc(xres_in, 16)

                def diagonal(t):
                    sp.wait_ge(kq_ready, 4 * t + 2)
                    for h in range(HC):
                        sp.dma_start(k_diag[HD * h:HD * h + HD, :, h, :],
                                     kT[HD * h:HD * h + HD, :, :]).then_inc(kdiag_ready, 16)

                load_xT(0)
                for i, (w, first, end) in enumerate(pieces):
                    sp.dma_start(staged(i), wT_d[w][:, first:end, :]).then_inc(w_in[i], 16)
                    if i == 1:
                        sp.dma_start(bq_col[:, :], b_d[0]).then_inc(bias_in, 16)
                        sp.dma_start(bk_col[:, :], b_d[1]).then_inc(bias_in, 16)
                    if i == 2:
                        sp.dma_start(bv_all[:, :], bv_d).then_inc(bv_in, 16)
                load_xres(0)
                sp.dma_start(bo_all[:, :], bo_d).then_inc(bo_in, 16)
                sp.wait_ge(zeros_ready, 1)
                diagonal(0)
                sp.wait_ge(xT_ready, 1)
                load_xT(1)
                for half in range(2):
                    rows = slice(L * half, L * half + L)
                    for w in range(2):
                        sp.dma_start(cross.w_raw[w][rows, :], xwT_d[w]).then_inc(cross.w_in, 16)
                    sp.dma_start(cross.c_raw[rows, :, :], ctx_d[:, 0:2, :]).then_inc(cross.c_in, 16)
                    sp.dma_start(cross.bo[rows, :], xbo_d).then_inc(cross.small_in, 16)
                with sp.Fori(0, NT - 2) as t:
                    diagonal(t + 1)
                    sp.wait_ge(xT_ready, t + 2)
                    load_xT(t + 2)
                    sp.wait_ge(y_done, 2 * t + 4)
                    load_xres(t + 1)
                diagonal(NT - 1)
                sp.wait_ge(y_done, 2 * NT)
                load_xres(NT - 1)
                sp.wait_ge(kdiag_ready, 16 * HC * NT)
                sp.dma_start(wv, xwv_d).then_inc(cross.small_in, 16)
                sp.dma_start(woT, xwoT_d).then_inc(cross.small_in, 16)

            @block.gpsimd
            def _(pool):
                pool.memset(mask[:, :], 0.0).then_inc(pool_step, 1)
                pool.memset(v_diag[:, :, :, :], 0.0).then_inc(pool_step, 1)
                for b in range(2):
                    pool.wait_ge(pool_step, 2 + b)
                    m = mask[L * b:L * b + L, :]
                    pool.affine_select(out=m, in_=m, compare_op=ALU.is_ge, fill=MASKED, base=0,
                                       pattern=[[-1, L]], channel_multiplier=1).then_inc(pool_step, 1)
                for half in range(2):
                    pool.wait_ge(pool_step, 4 + half)
                    pool.memset(v_diag[L * half:L * half + L, :, :, half * VW + HD], 1.0).then_inc(pool_step, 1)
                pool.wait_ge(pool_step, 6)

                def low_x(t):
                    pool.wait_ge(xThi_ready, t + 1)
                    pool.tensor_tensor(xT_lo[:, :, :], xT[:, :, :], xT_hi[:, :, :].bitcast(F32),
                                       ALU.subtract).then_inc(xT_ready, 1)

                low_x(0)
                pool.memset(k_diag[:, :, :, :], 0.0).then_inc(zeros_ready, 1)
                pool.wait_ge(bo_in, 16)

                def residual(t):
                    pool.wait_ge(xres_in, 16 * t + 16)
                    for p in range(2):
                        ins = pool.tensor_tensor(xb[:, p, :], xb[:, p, :], bo_all[:, :], ALU.add)
                    ins.then_inc(xb_ready, 1)

                def shift(t, s):
                    pool.wait_ge(max_done, 8 * t + s + 1)
                    scores = prob[:, s % 4, :].rearrange("p (h k) -> p h k", k=L)
                    pool.tensor_tensor(scores, scores, neg_max[:, s % 4, :].unsqueeze(2).broadcast_to([P, HC, L]),
                                       ALU.add).then_inc(shift_done, 1)

                def attention(t, last):
                    for s in range(8):
                        shift(t, s)
                        if s == 5 and not last:
                            low_x(t + 1)
                    residual(t)

                with pool.Fori(0, NT - 1) as t:
                    attention(t, False)
                attention(NT - 1, True)

                pool.wait_ge(xb_ready, NT)
                for w in range(2):
                    pool.wait_ge(cross.w_rounded, 2 * w + 2)
                    low_part(pool, cross.w_same[w], cross.w_raw[w], 1).then_inc(cross.w_split, 1)
                    pool.wait_ge(cross.w_split, 2 * w + 1)
                    low_part(pool, cross.w_cross[w], cross.w_raw[w], 0).then_inc(cross.w_split, 1)
                    pool.wait_ge(cross.w_split, 2 * w + 2)
                pool.wait_ge(cross.c_rounded, 1)
                low_part(pool, cross.c_split, cross.c_raw, 1).then_inc(cross.c_ready, 1)

            @block.scalar
            def _(act):
                def split_x(t):
                    act.wait_ge(xT_in, 16 * t + 16)
                    act.activation(xT_hi[:, :, :], xT[:, :, :], ACT.Copy).then_inc(xThi_ready, 1)

                split_x(0)

                def high_piece(i):
                    act.wait_ge(w_in[i], 16)
                    act.activation(split_of(w_hi, i), staged(i), ACT.Copy).then_inc(w_hi_ready, 1)

                for i in range(2):
                    high_piece(i)
                act.wait_ge(bias_in, 32)
                act.activation(bq_scaled[:, :], bq_col[:, :], ACT.Copy, scale=HD ** -0.5).then_inc(bq_ready, 1)
                act.wait_ge(bq_ready, 1)
                high_piece(2)

                def kq(t, n):
                    bank = M0 if n == 2 else M1
                    act.wait_ge(kq_done, 4 * t + n + 1)
                    for half in range(2):
                        f, src = 2 * (n % 2) + half, bank[:, TOK * half:TOK * half + TOK]
                        if n < 2:
                            ins = act.activation(kT[:, f, :], src, ACT.Identity, bias=bk_col[:, f:f + 1])
                        else:
                            ins = act.activation(qT[:, f, :], src, ACT.Identity, bias=bq_scaled[:, f:f + 1],
                                                 scale=HD ** -0.5)
                    ins.then_inc(kq_ready, 1)

                def exp(t, s):
                    act.wait_ge(shift_done, 8 * t + s + 1)
                    act.activation(prob[:, s % 4, :], prob[:, s % 4, :], ACT.Exp).then_inc(exp_done, 1)

                def evacuate(t, s):
                    act.wait_ge(t_done, 8 * t + s + 5)
                    act.wait_ge(av_done, 8 * t + s + 1)
                    act.activation(probT[:, s % 2, :], T(s), ACT.Copy).then_inc(probT_done, 1)

                def oT(t, p):
                    act.wait_ge(oT_done, 2 * t + p + 1)
                    act.wait_ge(proj_done, 2 * t + p + 1)
                    act.activation(oT_hi[:, :, :], o_bank(p).rearrange("p (c t) -> p c t", c=DC), ACT.Copy)\
                       .then_inc(oThi_ready, 1)

                for n in range(4):
                    kq(0, n)
                    if n < 2:
                        high_piece(3 + n)

                def round_cross_operand(n):
                    if n < 2:
                        act.wait_ge(cross.w_in, 64)
                        for w in (cross.w_same, cross.w_cross):
                            act.activation(w[n][:, :], cross.w_raw[n][:, :], ACT.Copy).then_inc(cross.w_rounded, 1)
                    else:
                        act.wait_ge(cross.c_in, 32)
                        act.activation(cross.c_split[:, :, :], cross.c_raw[:, :, :], ACT.Copy)\
                           .then_inc(cross.c_rounded, 1)

                def attention(t, last):
                    for s in range(8):
                        if s >= 2:
                            evacuate(t, s - 2)
                        exp(t, s)
                        if s == 0 and not last:
                            act.wait_ge(v_done, 2 * t + 2)
                            split_x(t + 1)
                        if last and s < 3:
                            round_cross_operand(s)
                    if not last:
                        act.wait_ge(kdiag_ready, 16 * HC * (t + 1))
                        kq(t + 1, 0)
                    oT(t, 0)
                    evacuate(t, 6)
                    evacuate(t, 7)
                    if not last:
                        for n in range(1, 3):
                            kq(t + 1, n)
                    oT(t, 1)
                    if not last:
                        kq(t + 1, 3)
                    else:
                        copy_wvo()

                def copy_wvo():
                    act.wait_ge(cross.wvo_done, 1)
                    for odd in range(2):
                        act.activation(cross.wvo[:, :, :].rearrange("p (j two) c -> p j two c", two=2)[:, :, odd, :],
                                       S(odd)[:, 0:DC * HW].rearrange("p (j c) -> p j c", c=HW),
                                       ACT.Copy, scale=HW ** -0.5).then_inc(cross.wvo_ready, 1)

                with act.Fori(0, NT - 1) as t:
                    attention(t, False)
                attention(NT - 1, True)

            @block.vector
            def _(dve):
                for i in range(len(pieces)):
                    dve.wait_ge(w_hi_ready, i + 1)
                    dve.tensor_tensor(split_of(w_lo, i), staged(i), split_of(w_hi, i).bitcast(F32),
                                      ALU.subtract).then_inc(w_ready, 1)
                for s, n in ((t_done, 4), (masked_done, 2), (exp_done, 2), (probT_done, 2), (av_done, 2), (o_ready, 1),
                             (proj_done, 1), (y_done, 2)):
                    dve.sem_inc(s, n)
                dve.memset(landed[:, :], 0.0)
                dve.wait_ge(bv_in, 16)
                dve.wait_ge(pool_step, 6)

                def v(t, tt):
                    dve.wait_ge(v_done, 2 * t + tt + 1)
                    for b in range(2):
                        src = M0[L * b:L * b + L, :].rearrange("p (h two d) -> p h two d", two=2, d=HD)
                        bv = bv_all[L * b:L * b + L, :].rearrange("p (h two d) -> p h two d", two=2, d=HD)
                        for half in range(2):
                            ins = dve.tensor_tensor(
                                v_diag[L * half:L * half + L, 2 * tt + b, :, half * VW:half * VW + HD],
                                src[:, :, half, :], bv[:, :, half, :], ALU.add)
                            ins.then_inc(v_ready, 1)

                def masked(t, s):
                    dve.wait_ge(s_done, 8 * t + s + 1)
                    dve.wait_ge(t_done, 8 * t + s + 1)
                    dve.tensor_tensor(prob[:, s % 4, :].rearrange("p (h k) -> p h k", k=L),
                                      S(s).rearrange("p (h k) -> p h k", k=L),
                                      mask[:, :].unsqueeze(1).broadcast_to([P, HC, L]), ALU.add)\
                       .then_inc(masked_done, 1)

                def row_max(t, s):
                    dve.wait_ge(masked_done, 8 * t + s + 3)
                    dve.tensor_reduce(neg_max[:, s % 4, :], prob[:, s % 4, :].rearrange("p (h k) -> p h k", k=L), AX.X,
                                      ALU.max, negate=True).then_inc(max_done, 1)

                def normalise(t, p):
                    dve.wait_ge(av_done, 8 * t + 4 * p + 6)
                    Oh = O[:, :, 0:16 * VW].rearrange("p n (h w) -> p n h w", w=VW)
                    dve.reciprocal(inv_sum[:, :, :], Oh[:, :, :, HD]).then_inc(dve_step, 1)
                    dve.wait_ge(dve_step, 2 * t + p + 1)
                    for n in range(2):
                        ins = dve.tensor_tensor(
                            o[:, 256 * n:256 * n + 256].rearrange("p (h d) -> p h d", d=HD), Oh[:, n, :, 0:HD],
                            inv_sum[:, n, :].unsqueeze(2).broadcast_to([P, 16, HD]), ALU.mult)
                    ins.then_inc(o_ready, 1)

                def oT(t, p):
                    dve.wait_ge(oThi_ready, 2 * t + p + 1)
                    dve.tensor_tensor(oT_lo[:, :, :], o_bank(p).rearrange("p (c t) -> p c t", c=DC),
                                      oT_hi[:, :, :].bitcast(F32), ALU.subtract).then_inc(oT_ready, 1)

                def y(t, p):
                    dve.wait_ge(proj_done, 2 * t + p + 2)
                    dve.wait_ge(xb_ready, t + 1)
                    dve.tensor_tensor(y1[:, bass.ds(2 * t + p, 1), :], (M0, M1)[p].unsqueeze(1), xb[:, p:p + 1, :],
                                      ALU.add).then_inc(y_done, 1)
                    dve.wait_ge(y_done, 2 * t + p + 3)
                    dve.tensor_copy(landed[:, 0:1], landed[:, 1:2])
                    dve.bn_stats(stats[:, bass.ds((2 * t + p) * 6, 6)], y1[:, bass.ds(2 * t + p, 1), :])

                v(0, 0)

                def attention(t, last):
                    for s in range(8):
                        masked(t, s)
                        row_max(t, s)
                        if s == 0:
                            v(t, 1)
                        if s == 7:
                            normalise(t, 0)
                    oT(t, 0)
                    if last:
                        normalise(t, 1)
                        y(t, 0)
                    else:
                        y(t, 0)
                        normalise(t, 1)
                    oT(t, 1)
                    if not last:
                        v(t + 1, 0)
                    y(t, 1)

                with dve.Fori(0, NT - 1) as t:
                    attention(t, False)
                attention(NT - 1, True)

            @block.tensor
            def _(pe):
                def three(out, stat_hi, stat_lo, mov_hi, mov_lo, c, n=DC):
                    parts = [(stat_hi, mov_hi), (stat_hi, mov_lo), (stat_lo, mov_hi)]
                    for k, (a, b) in enumerate(parts):
                        ins = pe.matmul(out, a, b, start=(c == 0 and k == 0), stop=(c == n - 1 and k == 2))
                    return ins

                def kq(t, n, first=False):
                    w, bank = n // 2, M0 if n == 2 else M1
                    for half in range(2):
                        f = 2 * (n % 2) + half
                        for cc in range(DC):
                            if first and cc == DC // 2:
                                pe.wait_ge(w_ready, 2)
                            fs = slice(P * f, P * f + P)
                            ins = three(bank[:, TOK * half:TOK * half + TOK], w_hi[w][:, cc, fs], w_lo[w][:, cc, fs],
                                        xT_hi[:, cc, :], xT_lo[:, cc, :], cc)
                    ins.then_inc(kq_done, 1)

                def v(t, tt):
                    for cc in range(DC):
                        ts = slice(P * tt, P * tt + P)
                        ins = three(M0, xT_hi[:, cc, ts], xT_lo[:, cc, ts], w_hi[2][:, cc, :], w_lo[2][:, cc, :], cc)
                    ins.then_inc(v_done, 1)

                def scores(t, s):
                    p, cc = s // 4, s % 4
                    if s == 0:
                        pe.wait_ge(kdiag_ready, 16 * HC * (t + 1))
                    pe.wait_ge(masked_done, 8 * t + s + 1)
                    for b in range(2):
                        ts = slice(L * (2 * p + b), L * (2 * p + b) + L)
                        ins = pe.matmul(S(s)[L * b:L * b + L, :].rearrange("p (h k) -> p h k", k=L),
                                        qT[:, cc, ts], k_diag[:, cc, :, ts], start=True, stop=True)
                    ins.then_inc(s_done, 1)

                def transposes(t, s):
                    pe.wait_ge(exp_done, 8 * t + s + 3)
                    pe.wait_ge(probT_done, 8 * t + s + 1)
                    for k in range(4):
                        ins = pe.transpose(T(s)[:, P * k:P * k + P], prob[:, s % 4, P * k:P * k + P], ident[:, :])
                    ins.then_inc(t_done, 1)

                def values(t, s):
                    p, cc = s // 4, s % 4
                    pe.wait_ge(probT_done, 8 * t + s + 3)
                    if cc == 0:
                        pe.wait_ge(o_ready, 2 * t + p + 1)
                    if s == 0:
                        pe.wait_ge(v_ready, 8 * t + 8)
                    for k in range(4):
                        hp = 4 * cc + k
                        for b in range(2):
                            ins = pe.matmul(O[L * b:L * b + L, hp // 8, 2 * VW * (hp % 8):2 * VW * (hp % 8 + 1)],
                                            probT[:, s % 2, P * k + L * b:P * k + L * b + L],
                                            v_diag[:, 2 * p + b, hp, :], start=True, stop=True)
                    ins.then_inc(av_done, 1)

                def oT(t, p):
                    pe.wait_ge(o_ready, 2 * t + p + 2)
                    for k in range(DC):
                        ins = pe.transpose(o_bank(p)[:, P * k:P * k + P], o[:, P * k:P * k + P], ident[:, :])
                    ins.then_inc(oT_done, 1)

                def project(t, p):
                    pe.wait_ge(oT_ready, 2 * t + p + 1)
                    for cc in range(DC):
                        ins = three((M0, M1)[p], oT_hi[:, cc, :], oT_lo[:, cc, :], w_hi[3][:, cc, :], w_lo[3][:, cc, :], cc)
                    ins.then_inc(proj_done, 1)

                pe.wait_ge(xT_ready, 1)
                for n in range(4):
                    pe.wait_ge(w_ready, (1, 2, 3, 3)[n])
                    if n == 1 or n == 3:
                        pe.wait_ge(kq_ready, n)
                    kq(0, n, n == 0)
                pe.wait_ge(w_ready, 4)
                pe.wait_ge(kq_ready, 3)
                v(0, 0)
                pe.wait_ge(w_ready, 5)
                pe.wait_ge(kq_ready, 4)

                def mix_cross_weights():
                    pe.wait_ge(cross.small_in, 64)
                    for j in range(DC):
                        for odd in range(2):
                            rows = slice(HW * odd, HW * odd + HW)
                            for half in range(2):
                                ins = pe.matmul(S(odd)[HW * half:HW * half + HW, HW * j:HW * j + HW],
                                                wv[rows, j, :], woT[rows, j, :], start=True, stop=True)
                    ins.then_inc(cross.wvo_done, 1)

                def attention(t, last):
                    for s in range(8):
                        scores(t, s)
                        if s == 0:
                            pe.wait_ge(v_ready, 8 * t + 4)
                            v(t, 1)
                        if s >= 3:
                            transposes(t, s - 3)
                        if s >= 4:
                            values(t, s - 4)
                    transposes(t, 5)
                    if not last:
                        pe.wait_ge(xT_ready, t + 2)
                        pe.wait_ge(y_done, 2 * t + 2)
                        kq(t + 1, 0)
                    pe.wait_ge(v_ready, 8 * t + 8)
                    oT(t, 0)
                    values(t, 4)
                    transposes(t, 6)
                    values(t, 5)
                    transposes(t, 7)
                    values(t, 6)
                    project(t, 0)
                    if not last:
                        pe.wait_ge(kq_ready, 4 * t + 5)
                        kq(t + 1, 1)
                    values(t, 7)
                    if not last:
                        pe.wait_ge(y_done, 2 * t + 3)
                        kq(t + 1, 2)
                    else:
                        mix_cross_weights()
                    oT(t, 1)
                    if not last:
                        pe.wait_ge(kq_ready, 4 * t + 6)
                        kq(t + 1, 3)
                        pe.wait_ge(kq_ready, 4 * t + 7)
                        v(t + 1, 0)
                        pe.wait_ge(kq_ready, 4 * t + 8)
                    project(t, 1)

                with pe.Fori(0, NT - 1) as t:
                    attention(t, False)
                attention(NT - 1, True)


def cross_phase(nc, ident, identb, x1, stats, cross, ctx_d, ctxT_d, out_y, sumsq, ffn_weights, ffn_w_in, g_d,
                g_scaled, xT_hi, xT_lo):
    w_same, w_cross, wvo, bo = cross.w_same, cross.w_cross, cross.wvo, cross.bo
    c_raw, c_split, c_in, c_rounded, c_ready = cross.c_raw, cross.c_split, cross.c_in, cross.c_rounded, cross.c_ready
    with ExitStack() as c:
        def sb(name, shape, dt=F32):
            return c.enter_context(nc.sbuf_tensor(name, shape, dt))

        def sem(name):
            return c.enter_context(nc.semaphore(name))

        x_raw = sb("x_raw", [P, 2, D])
        x_split = sb("x_split", [P, 2, D], F32R)
        ctxT = sb("ctxT", [P, DC, 2, HW])
        e = sb("e", [P, 4, 2, D])
        kT = sb("ekT", [P, 2, 2, DC, P])
        q = sb("qs", [P, 2, DC, D])
        gT = sb("gT", [P, D])
        m = sb("m", [P, 2, DC, HW])
        k_max = sb("k_max", [P, 4, 2, 1])
        k_sum = sb("k_sum", [P, 2, DC])
        k_inv = sb("k_inv", [P, 2, DC])
        q_max = sb("q_max", [P, 2, XH], BF16)
        q_maxv = sb("q_maxv", [P, 2, XH])
        q_sum = sb("q_sum", [P, 4, 2, XH])
        q_inv = sb("q_inv", [P, 4, 2, XH])
        square = sb("square", [P, D])
        half_ones = sb("half_ones", [P, 2])
        half_sum, half_diff, var, sq, mean, ln_root, ln_scale, ln_shift = (sb(n, [P, PAIRS]) for n in (
            "ln_sum", "ln_diff", "ln_var", "ln_sq", "ln_mean", "ln_root", "ln_scale", "ln_shift"))
        ps = c.enter_context(nc.psum_tensor("ps_b", [P, 8, 512], F32))

        vector_shifts, tensor_shifts = [0, 2], [1, 3]

        def proj_bank(s, b):
            return ps[:, 2 * (s % 2) + b, :]

        def t_bank(b):
            return ps[:, 4 + b, :]

        G, Y = ps[:, 6, :], ps[:, 7, :]
        m_bank = (G, Y)

        g_raw = sb("g_raw", [P, 1])
        inv_wide, scaled, z = x_raw, c_raw, e[:, 0, :, :]
        x2 = scaled
        r_norm, r_inv = sb("r_norm", [P, 2 * 2 * DC]), sb("r_inv", [P, 2 * 2 * DC])
        r_eps = sb("r_eps", [P, 1])
        r_stats, r_moments = sb("r_stats", [P, 2, 6]), sb("r_moments", [P, 2, 2])
        r_root, r_scale, r_shift = sb("r_root", [P, 2]), sb("r_scale", [P, 2]), sb("r_shift", [P, 2])
        g_in, g_ready = sem("g_in"), sem("g_ready")
        r_norm_ready, r_wide_ready, r_spread, r_step, r_moments_ready, r_root_ready, r_x2_ready, r_t_done, r_hi_ready = (
            sem(n) for n in ("r_norm_ready", "r_wide_ready", "r_spread", "r_step", "r_moments_ready", "r_root_ready",
                             "r_x2_ready", "r_t_done", "r_hi_ready"))
        ln_step, ln_var_ready, ln_root_ready = sem("ln_step"), sem("ln_var_ready"), sem("ln_root_ready")
        ctxT_in, ones_step = sem("ctxT_in"), sem("ones_step")
        x1_ready, x_in, x_rounded, x_ready = sem("x1_ready"), sem("x_in"), sem("x_rounded"), sem("x_ready")
        p_done, kmax_done, qmax_done, shift_done, exp_done = (sem(n) for n in (
            "p_done", "kmax_done", "qmax_done", "xshift_done", "xexp_done"))
        vshift_done = sem("vshift_done")
        sum_done, inv_done, q_ready = sem("sum_done"), sem("inv_done"), sem("q_ready")
        t_done, g_done, gT_ready = sem("xt_done"), sem("g_done"), sem("gT_ready")
        tcopy_done = [sem("tcopy_done0"), sem("tcopy_done1")]
        m_done, kinv_done, m_ready = sem("m_done"), sem("kinv_done"), sem("m_ready")
        waited, sp_waited = sem("waited"), sem("sp_waited")
        y_done, y_ready, sq_ready, sumsq_done, sumsq_ready = (sem(n) for n in (
            "xy_done", "xy_ready", "sq_ready", "sumsq_done", "sumsq_ready"))

        with nc.Block() as block:
            @block.sync
            def _(sp):
                def load_ctx(i):
                    for half in range(2):
                        sp.dma_start(c_raw[L * half:L * half + L, :, :],
                                     ctx_d[:, bass.ds(2 * i, 2), :]).then_inc(c_in, 16)

                def load_ctxT(i):
                    for b in range(2):
                        sp.dma_start(ctxT[:, :, b, :], ctxT_d[:, bass.ds((2 * i + b) * DC, DC), :]).then_inc(ctxT_in, 16)

                def load_x(i):
                    sp.wait_ge(x1_ready, i + 1)
                    sp.sem_inc(sp_waited, 1)
                    for b in range(2):
                        for half in range(2):
                            sp.dma_start(x_raw[L * half:L * half + L, b, :].unsqueeze(1),
                                         x1[L * b:L * b + L, bass.ds(i, 1), :]).then_inc(x_in, 16)

                def load_next(i):
                    sp.wait_ge(c_ready, i + 1)
                    sp.sem_inc(sp_waited, 1)
                    load_ctx(i + 1)
                    sp.wait_ge(x_ready, i + 1)
                    sp.sem_inc(sp_waited, 1)
                    load_x(i + 1)
                    sp.wait_ge(g_done, 4 * i + 4)
                    sp.sem_inc(sp_waited, 1)
                    load_ctxT(i + 1)

                load_ctxT(0)
                load_x(0)
                for half in range(2):
                    sp.dma_start(g_raw[L * half:L * half + L, :], g_d).then_inc(g_in, 16)
                load_next(0)
                for w, w_d in ffn_weights:
                    sp.dma_start(w[:, :, :], w_d).then_inc(ffn_w_in, 16)
                with sp.Fori(1, PAIRS - 1) as i:
                    load_next(i)

            @block.gpsimd
            def _(pool):
                pool.memset(half_ones[:, :], 0.0).then_inc(ones_step, 1)
                for b in range(2):
                    pool.wait_ge(ones_step, b + 1)
                    pool.memset(half_ones[L * b:L * b + L, b:b + 1], 1.0).then_inc(ones_step, 1)
                pool.wait_ge(ones_step, 3)

                def split_ctx(i):
                    pool.wait_ge(c_rounded, i + 1)
                    low_part(pool, c_split, c_raw, 1).then_inc(c_ready, 1)

                def divide(i, n, b):
                    pool.wait_ge(inv_done, 8 * i + 2 * n + b + 1)
                    es = e[:, n, b, :].rearrange("p (h d) -> p h d", d=HW)
                    pool.tensor_tensor(es, es, q_inv[:, n, b, :].unsqueeze(2).broadcast_to([P, XH, HW]), ALU.mult)\
                        .then_inc(q_ready, 1)

                def iteration(i, first, last):
                    if not first:
                        for b in range(2):
                            divide(i - 1, 3, b)
                        pool.wait_ge(q_ready, 8 * i)
                    pool.wait_ge(x_rounded, i + 1)
                    low_part(pool, x_split, x_raw, 1).then_inc(x_ready, 1)
                    pool.wait_ge(x_ready, i + 1)
                    if not first:
                        squares(i - 1)
                    if not last:
                        if not first:
                            pool.wait_ge(sq_ready, i)
                        split_ctx(i + 1)
                        pool.wait_ge(c_ready, i + 2)
                    for n in range(3):
                        for b in range(2):
                            divide(i, n, b)

                def squares(i):
                    pool.wait_ge(y_ready, i + 1)
                    ys = out_y[:, bass.ds(i, 1), :]
                    pool.tensor_tensor(square[:, :].unsqueeze(1), ys, ys, ALU.mult).then_inc(sq_ready, 1)

                iteration(0, True, False)
                with pool.Fori(1, PAIRS - 1) as i:
                    iteration(i, False, False)
                iteration(PAIRS - 1, False, True)
                for b in range(2):
                    divide(PAIRS - 1, 3, b)
                squares(PAIRS - 1)

            @block.scalar
            def _(act):
                def split_ctx(i):
                    act.wait_ge(c_in, 32 * i + 32)
                    act.activation(c_split[:, :, :], c_raw[:, :, :], ACT.Copy).then_inc(c_rounded, 1)

                act.wait_ge(ln_var_ready, 1)
                act.activation(ln_root[:, :], var[:, :], ACT.Sqrt).then_inc(ln_root_ready, 1)

                def exp_k(i, j):
                    for b in range(2):
                        act.wait_ge(kmax_done, 8 * i + 2 * j + b + 1)
                        act.activation(e[:, j, b, :], proj_bank(j, b), ACT.Exp, bias=k_max[:, j, b, :],
                                       accum_out=k_sum[:, b, j:j + 1]).then_inc(exp_done, 1)

                def exp_q(i, n):
                    for b in range(2):
                        if n in vector_shifts:
                            k = vector_shifts.index(n)
                            act.wait_ge(vshift_done, 2 * len(vector_shifts) * i + 2 * k + b + 1)
                            act.activation(e[:, n, b, :], e[:, n, b, :], ACT.Exp).then_inc(exp_done, 1)
                        else:
                            k = tensor_shifts.index(n)
                            act.wait_ge(shift_done, 2 * len(tensor_shifts) * i + 2 * k + b + 1)
                            act.activation(e[:, n, b, :], proj_bank(n, b), ACT.Exp).then_inc(exp_done, 1)

                def copy_k(i, j):
                    for b in range(2):
                        act.wait_ge(t_done, 16 * i + 2 * j + b + 1)
                        act.activation(kT[:, j % 2, b, :, :], t_bank(b).rearrange("p (n k) -> p n k", k=P), ACT.Copy)\
                           .then_inc(tcopy_done[b], 1)

                def copy_q(i, n, batches=(0, 1)):
                    for b in batches:
                        act.wait_ge(t_done, 16 * i + 8 + 2 * n + b + 1)
                        act.activation(q[:, b, :, P * n:P * n + P], t_bank(b).rearrange("p (j n) -> p j n", n=P),
                                       ACT.Copy).then_inc(tcopy_done[b], 1)

                def copy_g(i):
                    act.wait_ge(g_done, 4 * i + 4)
                    act.activation(gT[:, :], G, ACT.Copy).then_inc(gT_ready, 1)

                def copy_y(i):
                    act.wait_ge(y_done, i + 1)
                    act.activation(out_y[:, bass.ds(i, 1), :], Y.unsqueeze(1), ACT.Identity, bias=bo[:, :])\
                       .then_inc(y_ready, 1)

                def first_rows_high(p):
                    act.wait_ge(r_t_done, p + 1)
                    act.activation(xT_hi[:, :, P * p:P * p + P], ps[:, 2 + p, :].rearrange("p (c t) -> p c t", c=DC),
                                   ACT.Copy).then_inc(r_hi_ready, 1)

                def iteration(i, first, last):
                    if not first:
                        exp_q(i - 1, 3)
                        copy_q(i - 1, 1, (1,))
                        copy_g(i - 1)
                    exp_k(i, 0)
                    if not first:
                        copy_q(i - 1, 2, (1,))
                    exp_k(i, 1)
                    if not first:
                        copy_q(i - 1, 3)
                    act.wait_ge(x_in, 64 * i + 64)
                    act.activation(x_split[:, :, :], x_raw[:, :, :], ACT.Copy).then_inc(x_rounded, 1)
                    exp_k(i, 2)
                    exp_k(i, 3)
                    if not first:
                        copy_y(i - 1)
                    copy_k(i, 1)
                    if not last:
                        split_ctx(i + 1)
                    exp_q(i, 0)
                    copy_k(i, 2)
                    exp_q(i, 1)
                    copy_k(i, 3)
                    exp_q(i, 2)
                    copy_q(i, 0)

                act.wait_ge(cross.small_in, 64)
                iteration(0, True, False)
                act.wait_ge(g_in, 32)
                act.activation(g_scaled[:, :], g_raw[:, :], ACT.Copy, scale=float(L) ** 0.5).then_inc(g_ready, 1)
                with act.Fori(1, PAIRS - 1) as i:
                    iteration(i, False, False)
                iteration(PAIRS - 1, False, True)
                exp_q(PAIRS - 1, 3)
                copy_q(PAIRS - 1, 1, (1,))
                copy_g(PAIRS - 1)
                act.activation(r_norm[:, :], sumsq[:, 0:2 * 2 * DC], ACT.Sqrt).then_inc(r_norm_ready, 1)
                act.wait_ge(r_moments_ready, 1)
                act.activation(r_root[:, :], r_moments[:, :, 1], ACT.Sqrt, bias=r_eps[:, :]).then_inc(r_root_ready, 1)
                copy_y(PAIRS - 1)
                for p in range(2):
                    first_rows_high(p)

            @block.vector
            def _(dve):
                for s, n in ((exp_done, 4), (tcopy_done[0], 1), (tcopy_done[1], 1), (sumsq_ready, 1)):
                    dve.sem_inc(s, n)

                def max_k(i, j, batches=(0, 1)):
                    for b in batches:
                        dve.wait_ge(p_done, 16 * i + 2 * j + b + 1)
                        dve.tensor_reduce(k_max[:, j, b, :], proj_bank(j, b), AX.X, ALU.max, negate=True)\
                           .then_inc(kmax_done, 1)

                def max_q(i, n):
                    for b in range(2):
                        dve.wait_ge(p_done, 16 * i + 8 + 2 * n + b + 1)
                        top = q_maxv[:, b, :] if n in vector_shifts else q_max[:, b, :]
                        dve.tensor_reduce(top, proj_bank(n, b).rearrange("p (h d) -> p h d", d=HW),
                                          AX.X, ALU.max, negate=True).then_inc(qmax_done, 1)
                    if n in vector_shifts:
                        for b in range(2):
                            dve.wait_ge(qmax_done, 8 * i + 2 * n + b + 1)
                            dve.tensor_tensor(e[:, n, b, :].rearrange("p (h d) -> p h d", d=HW),
                                              proj_bank(n, b).rearrange("p (h d) -> p h d", d=HW),
                                              q_maxv[:, b, :].unsqueeze(2).broadcast_to([P, XH, HW]), ALU.add)\
                               .then_inc(vshift_done, 1)

                def sum_q(i, n):
                    for b in range(2):
                        dve.wait_ge(exp_done, 16 * i + 8 + 2 * n + b + 5)
                        dve.tensor_reduce(q_sum[:, n, b, :], e[:, n, b, :].rearrange("p (h d) -> p h d", d=HW), AX.X,
                                          ALU.add).then_inc(sum_done, 1)
                        dve.wait_ge(sum_done, 8 * i + 2 * n + b + 1)
                        dve.reciprocal(q_inv[:, n, b, :], q_sum[:, n, b, :]).then_inc(inv_done, 1)

                def normalise(i):
                    rows = x1[:, bass.ds(i, 1), :]
                    dve.tensor_scalar(rows, rows, ln_scale[:, bass.ds(i, 1)], ln_shift[:, bass.ds(i, 1)],
                                      ALU.mult, ALU.add).then_inc(x1_ready, 1)

                def invert_k_sums(i):
                    dve.wait_ge(exp_done, 16 * i + 12)
                    dve.reciprocal(k_inv[:, :, :], k_sum[:, :, :]).then_inc(kinv_done, 1)

                def fold_sums(i):
                    dve.wait_ge(m_done, 2 * i + 2)
                    dve.wait_ge(kinv_done, i + 1)
                    for b in range(2):
                        dve.tensor_tensor(m[:, b, :, :], m_bank[b][:, 0:DC * HW].rearrange("p (j c) -> p j c", c=HW),
                                          k_inv[:, b, :].unsqueeze(2).broadcast_to([P, DC, HW]), ALU.mult)\
                           .then_inc(m_ready, 1)

                def copy_k(i, j):
                    for b in range(2):
                        dve.wait_ge(t_done, 16 * i + 2 * j + b + 1)
                        dve.tensor_copy(kT[:, j % 2, b, :, :], t_bank(b).rearrange("p (n k) -> p n k", k=P))\
                           .then_inc(tcopy_done[b], 1)

                def copy_q(i, n, batches=(0, 1)):
                    for b in batches:
                        dve.wait_ge(t_done, 16 * i + 8 + 2 * n + b + 1)
                        dve.tensor_copy(q[:, b, :, P * n:P * n + P], t_bank(b).rearrange("p (j n) -> p j n", n=P))\
                           .then_inc(tcopy_done[b], 1)

                def copy_sumsq(i):
                    dve.wait_ge(sumsq_done, i + 1)
                    dve.tensor_scalar(sumsq[:, bass.ds(i * 8, 8)], Y[:, 0:8], 1e-24, None, ALU.max)\
                       .then_inc(sumsq_ready, 1)

                def layer_norm_variances():
                    st = stats[:, :].rearrange("p (i k) -> p i k", k=6)
                    dve.tensor_tensor(half_sum[:, :], st[:, :, 1], st[:, :, 4], ALU.add)
                    dve.tensor_tensor(half_diff[:, :], st[:, :, 1], st[:, :, 4], ALU.subtract)
                    dve.tensor_tensor(var[:, :], st[:, :, 2], st[:, :, 5], ALU.add).then_inc(ln_step, 1)
                    dve.wait_ge(ln_step, 1)
                    dve.tensor_scalar(mean[:, :], half_sum[:, :], 0.5, None, ALU.mult)
                    dve.tensor_tensor(sq[:, :], half_diff[:, :], half_diff[:, :], ALU.mult).then_inc(ln_step, 1)
                    dve.wait_ge(ln_step, 2)
                    dve.tensor_scalar(sq[:, :], sq[:, :], 0.25, EPS, ALU.mult, ALU.add).then_inc(ln_step, 1)
                    dve.wait_ge(ln_step, 3)
                    dve.scalar_tensor_tensor(var[:, :], var[:, :], 1.0 / D, sq[:, :], ALU.mult, ALU.add)\
                       .then_inc(ln_var_ready, 1)

                def layer_norm_terms():
                    dve.wait_ge(ln_root_ready, 1)
                    dve.reciprocal(ln_scale[:, :], ln_root[:, :]).then_inc(ln_step, 1)
                    dve.wait_ge(ln_step, 4)
                    dve.scalar_tensor_tensor(ln_shift[:, :], mean[:, :], -1.0, ln_scale[:, :], ALU.mult, ALU.mult)\
                       .then_inc(ln_step, 1)
                    dve.wait_ge(ln_step, 5)

                def iteration(i, first, last):
                    max_k(i, 0)
                    if first:
                        layer_norm_terms()
                        normalise(0)
                    if not first:
                        copy_q(i - 1, 1, (0,))
                        sum_q(i - 1, 3)
                    max_k(i, 1, (0,))
                    if not first:
                        copy_q(i - 1, 2, (0,))
                    max_k(i, 1, (1,))
                    if not first:
                        fold_sums(i - 1)
                    max_k(i, 2)
                    max_k(i, 3)
                    copy_k(i, 0)
                    max_q(i, 0)
                    invert_k_sums(i)
                    if not last:
                        normalise(i + 1)
                    max_q(i, 1)
                    sum_q(i, 0)
                    max_q(i, 2)
                    sum_q(i, 1)
                    max_q(i, 3)
                    sum_q(i, 2)
                    if not first:
                        copy_sumsq(i - 1)

                def first_rows_norms():
                    dve.wait_ge(r_norm_ready, 1)
                    dve.reciprocal(r_inv[:, :], r_norm[:, :]).then_inc(r_step, 1)
                    dve.wait_ge(r_step, 1)
                    dve.wait_ge(x_ready, PAIRS)
                    dve.wait_ge(c_ready, PAIRS)
                    for p in range(2):
                        dve.tensor_copy(inv_wide[:, p, :].rearrange("p (n c) -> p n c", c=L),
                                        r_inv[:, 2 * DC * p:2 * DC * p + 2 * DC].unsqueeze(2).broadcast_to([P, 2 * DC, L]))\
                           .then_inc(r_wide_ready, 1)

                def first_rows_add(p):
                    dve.wait_ge(r_spread, p + 1)
                    dve.tensor_tensor(scaled[:, p, :], ps[:, p, :], out_y[:, p, :], ALU.mult).then_inc(r_step, 1)
                    dve.wait_ge(r_step, 3 * p + 2)
                    dve.scalar_tensor_tensor(z[:, p, :], scaled[:, p, :], g_scaled[:, :], x1[:, p, :],
                                             ALU.mult, ALU.add).then_inc(r_step, 1)
                    dve.wait_ge(r_step, 3 * p + 3)
                    dve.bn_stats(r_stats[:, p, :], z[:, p, :]).then_inc(r_step, 1)

                def first_rows_normalise():
                    dve.wait_ge(r_step, 7)
                    for p in range(2):
                        ins = dve.bn_aggr(r_moments[:, p, :], r_stats[:, p, :])
                    ins.then_inc(r_moments_ready, 1)
                    dve.wait_ge(r_root_ready, 1)
                    dve.reciprocal(r_scale[:, :], r_root[:, :]).then_inc(r_step, 1)
                    dve.wait_ge(r_step, 8)
                    dve.scalar_tensor_tensor(r_shift[:, :], r_moments[:, :, 0], -1.0, r_scale[:, :], ALU.mult, ALU.mult)\
                       .then_inc(r_step, 1)
                    dve.wait_ge(r_step, 9)
                    for p in range(2):
                        dve.tensor_scalar(x2[:, p, :], z[:, p, :], r_scale[:, p:p + 1], r_shift[:, p:p + 1],
                                          ALU.mult, ALU.add).then_inc(r_x2_ready, 1)
                    for p in range(2):
                        dve.tensor_scalar(x1[:, p, :], z[:, p, :], r_scale[:, p:p + 1], r_shift[:, p:p + 1],
                                          ALU.mult, ALU.add)

                def first_rows_low(p):
                    dve.wait_ge(r_hi_ready, p + 1)
                    dve.tensor_tensor(xT_lo[:, :, P * p:P * p + P], ps[:, 2 + p, :].rearrange("p (c t) -> p c t", c=DC),
                                      xT_hi[:, :, P * p:P * p + P], ALU.subtract)

                layer_norm_variances()
                dve.memset(r_eps[:, :], EPS)
                iteration(0, True, False)
                with dve.Fori(1, PAIRS - 1) as i:
                    iteration(i, False, False)
                iteration(PAIRS - 1, False, True)
                copy_q(PAIRS - 1, 1, (0,))
                sum_q(PAIRS - 1, 3)
                copy_q(PAIRS - 1, 2)
                fold_sums(PAIRS - 1)
                first_rows_norms()
                copy_q(PAIRS - 1, 3)
                dve.wait_ge(g_ready, 1)
                for p in range(2):
                    first_rows_add(p)
                first_rows_normalise()
                copy_sumsq(PAIRS - 1)
                for p in range(2):
                    first_rows_low(p)

            @block.tensor
            def _(pe):
                def project_k(i, j):
                    if j == 0:
                        pe.wait_ge(c_ready, i + 1)
                    for b in range(2):
                        pe.wait_ge(exp_done, 16 * i + 2 * j + b + 1)
                        for r, w in enumerate((w_same[0], w_cross[0])):
                            ins = pe.matmul(proj_bank(j, b), w[:, P * j:P * j + P], c_split[:, b, :],
                                            start=(r == 0), stop=(r == 1))
                        ins.then_inc(p_done, 1)

                def project_q(i, n):
                    if n == 0:
                        pe.wait_ge(x_ready, i + 1)
                    for b in range(2):
                        pe.wait_ge(exp_done, 16 * i + 8 + 2 * n + b + 1)
                        for r, w in enumerate((w_same[1], w_cross[1])):
                            ins = pe.matmul(proj_bank(n, b), x_split[:, b, P * n:P * n + P], w[:, :],
                                            start=(r == 0), stop=(r == 1))
                        ins.then_inc(p_done, 1)

                def shift_q(i, n):
                    for b in (range(2) if n in tensor_shifts else ()):
                        pe.wait_ge(qmax_done, 8 * i + 2 * n + b + 1)
                        pe.matmul(proj_bank(n, b).rearrange("p (h d) -> p h d", d=HW), identb[:, :],
                                  q_max[:, b, :].unsqueeze(2).broadcast_to([P, XH, HW]), start=False, stop=True,
                                  skip_group_check=True).then_inc(shift_done, 1)

                def transpose_e(index, slot):
                    for b in range(2):
                        pe.wait_ge(tcopy_done[b], index + 1)
                        for r in range(4):
                            ins = pe.transpose(t_bank(b)[:, P * r:P * r + P], e[:, slot, b, P * r:P * r + P], ident[:, :])
                        ins.then_inc(t_done, 1)

                def transpose_k(i, j):
                    pe.wait_ge(exp_done, 16 * i + 2 * j + 6)
                    transpose_e(8 * i + j, j)

                def transpose_q(i, n):
                    pe.wait_ge(q_ready, 8 * i + 2 * n + 2)
                    transpose_e(8 * i + 4 + n, n)

                def keys_ctx(i, j):
                    for b in range(2):
                        pe.wait_ge(tcopy_done[b], 8 * i + j + 2)
                    if j == 0:
                        pe.wait_ge(ctxT_in, 32 * i + 32)
                    for n in range(DC):
                        for b in range(2):
                            ins = pe.matmul(G[HW * b:HW * b + HW, P * j:P * j + P], ctxT[:, n, b, :], kT[:, j % 2, b, n, :],
                                            start=(n == 0), stop=(n == DC - 1))
                    ins.then_inc(g_done, 1)

                def mix(i):
                    pe.wait_ge(gT_ready, i + 1)
                    pe.wait_ge(sumsq_ready, i + 1)
                    pe.sem_inc(waited, 1)
                    for b in range(2):
                        rows = slice(HW * b, HW * b + HW)
                        for h in range(XH):
                            half = h % 2
                            ins = pe.matmul(m_bank[b][HW * half:HW * half + HW, HW * (h // 2):HW * (h // 2) + HW],
                                            gT[rows, HW * h:HW * h + HW], wvo[rows, h, :], start=True, stop=True)
                        ins.then_inc(m_done, 1)

                def output(i):
                    pe.wait_ge(m_ready, 2 * i + 2)
                    for b in range(2):
                        pe.wait_ge(tcopy_done[b], 8 * i + 9)
                    for j in range(DC):
                        for b in range(2):
                            ins = pe.matmul(Y[HW * b:HW * b + HW, :], m[:, b, j, :], q[:, b, j, :],
                                            start=(j == 0), stop=(j == DC - 1))
                    ins.then_inc(y_done, 1)

                def sum_squares(i):
                    pe.wait_ge(sq_ready, i + 1)
                    for n in range(DC):
                        ins = pe.matmul(Y[:, 2 * n:2 * n + 2], square[:, P * n:P * n + P], half_ones[:, :],
                                        start=True, stop=True)
                    ins.then_inc(sumsq_done, 1)

                pe.wait_ge(ones_step, 3)
                pe.wait_ge(cross.w_split, 4)

                def iteration(i, first):
                    project_k(i, 0)
                    if not first:
                        shift_q(i - 1, 3)
                        transpose_q(i - 1, 1)
                    project_k(i, 1)
                    if not first:
                        transpose_q(i - 1, 2)
                        mix(i - 1)
                    project_k(i, 2)
                    if not first:
                        transpose_q(i - 1, 3)
                    project_k(i, 3)
                    transpose_k(i, 0)
                    if not first:
                        output(i - 1)
                    project_q(i, 0)
                    transpose_k(i, 1)
                    keys_ctx(i, 0)
                    project_q(i, 1)
                    shift_q(i, 0)
                    transpose_k(i, 2)
                    keys_ctx(i, 1)
                    project_q(i, 2)
                    shift_q(i, 1)
                    transpose_k(i, 3)
                    keys_ctx(i, 2)
                    if not first:
                        sum_squares(i - 1)
                    project_q(i, 3)
                    shift_q(i, 2)
                    transpose_q(i, 0)
                    keys_ctx(i, 3)

                iteration(0, True)
                with pe.Fori(1, PAIRS) as i:
                    iteration(i, False)
                shift_q(PAIRS - 1, 3)
                transpose_q(PAIRS - 1, 1)
                transpose_q(PAIRS - 1, 2)
                mix(PAIRS - 1)
                transpose_q(PAIRS - 1, 3)
                for p in range(2):
                    pe.wait_ge(r_wide_ready, p + 1)
                    for n in range(DC):
                        ins = pe.transpose(ps[:, p, P * n:P * n + P], inv_wide[:, p, P * n:P * n + P], ident[:, :])
                    ins.then_inc(r_spread, 1)
                output(PAIRS - 1)
                for p in range(2):
                    pe.wait_ge(r_x2_ready, p + 1)
                    for n in range(DC):
                        ins = pe.transpose(ps[:, 2 + p, P * n:P * n + P], x2[:, p, P * n:P * n + P], ident[:, :])
                    ins.then_inc(r_t_done, 1)
                sum_squares(PAIRS - 1)


def feed_forward_phase(nc, ident, x, cross_y, sumsq, weights, w_in, g_scaled, xT_hi, xT_lo, out_d):
    wg, wu, wd = weights
    FC = wd.shape[1]
    with ExitStack() as c:
        def sb(name, shape, dt=F32):
            return c.enter_context(nc.sbuf_tensor(name, shape, dt))

        def sem(name):
            return c.enter_context(nc.semaphore(name))

        norm, inv_norm = sb("norm", [P, PAIRS * 8]), sb("inv_norm", [P, PAIRS * 8])
        eps = sb("f_eps", [P, 1])
        inv_wide = sb("inv_wide", [P, 2, DC, 2, L])
        scaled = sb("scaled", [P, 2, D])
        z = sb("z", [P, 2, D])
        x2 = sb("x2", [P, 2, D])
        gate = sb("gate", [P, 2, TOK])
        h = sb("h", [P, 2, TOK])
        h_hi = sb("h_hi", [P, FC, TOK], BF16)
        h_lo = sb("h_lo", [P, FC, TOK], F16)
        y3 = sb("y3", [P, 2, D])
        result = sb("result", [P, 2, D])
        row_stats = sb("row_stats", [P, 4, 6])
        moments = sb("moments", [P, 4, 2])
        root = sb("f_root", [P, 4])
        scale = sb("f_scale", [P, 4])
        shift = sb("f_shift", [P, 4])
        ps = c.enter_context(nc.psum_tensor("ps_c", [P, 8, 512], F32))

        def GU(f):
            return ps[:, f % 2, :]

        def down(tt):
            return ps[:, 2 + tt, :]

        norm_bank = ps[:, 4, :]

        def T(p):
            return ps[:, 5 + p, :]

        consts_ready, norm_ready, inv_ready = sem("f_consts_ready"), sem("norm_ready"), sem("inv_ready")
        waited = sem("f_waited")
        wide_ready, norm_done, scaled_done, z_done, stats_done = (sem(n) for n in (
            "wide_ready", "norm_done", "scaled_done", "z_done", "stats_done"))
        moments_ready, root_ready, scale_ready, shift_ready = (sem(n) for n in (
            "moments_ready", "f_root_ready", "f_scale_ready", "f_shift_ready"))
        x2_ready, kept, t_done, hi_ready, xT_ready = (sem(n) for n in (
            "x2_ready", "x2_kept", "x2T_done", "x2T_hi_ready", "x2T_ready"))
        gu_done, silu_done, h_done, hhi_done, h_ready = (sem(n) for n in (
            "gu_done", "silu_done", "h_done", "h_hi_done", "h_ready"))
        down_done, y3_done, y3_stats, result_ready, stored = (sem(n) for n in (
            "down_done", "y3_done", "y3_stats", "result_ready", "stored"))

        with nc.Block() as block:
            @block.sync
            def _(sp):
                def store(t):
                    sp.wait_ge(result_ready, 2 * t + 2)
                    sp.dma_start(out_d[:, bass.ds(2 * t, 2), :], result[:, :, :]).then_inc(stored, 16)

                sp.sem_inc(stored, 16)
                with sp.Fori(0, NT) as t:
                    store(t)
                sp.wait_ge(stored, 16 * NT + 16)

            @block.gpsimd
            def _(pool):
                def widen(t):
                    pool.wait_ge(norm_done, 2 * t + 1)
                    pool.sem_inc(waited, 1)
                    for p in range(2):
                        pool.tensor_copy(inv_wide[:, p, :, :, :].rearrange("p n b c -> p (n b) c"),
                                         inv_norm[:, bass.ds(16 * t + 8 * p, 8)].unsqueeze(2).broadcast_to([P, 8, L]))\
                            .then_inc(wide_ready, 1)

                def low(t, f):
                    pool.wait_ge(hhi_done, FC * t + f + 1)
                    pool.tensor_tensor(h_lo[:, f, :], h[:, f % 2, :], h_hi[:, f, :], ALU.subtract).then_inc(h_ready, 1)

                pool.wait_ge(inv_ready, 1)

                def iteration(t, last):
                    if not last:
                        widen(t + 1)
                    for f in range(FC):
                        low(t, f)

                with pool.Fori(0, NT - 1) as t:
                    iteration(t, False)
                iteration(NT - 1, True)

            @block.scalar
            def _(act):
                act.activation(norm[:, :], sumsq[:, :], ACT.Sqrt).then_inc(norm_ready, 1)

                def roots(n):
                    act.wait_ge(moments_ready, n)
                    act.activation(root[:, :], moments[:, :, 1], ACT.Sqrt, bias=eps[:, :]).then_inc(root_ready, 1)

                def high(t, p):
                    act.wait_ge(t_done, 2 * t + p + 1)
                    act.activation(xT_hi[:, :, P * p:P * p + P], T(p).rearrange("p (c t) -> p c t", c=DC), ACT.Copy)\
                       .then_inc(hi_ready, 1)

                def silu(t, f):
                    act.wait_ge(gu_done, FC * t + f + 1)
                    act.activation(gate[:, f % 2, :], GU(f)[:, 0:TOK], ACT.Silu).then_inc(silu_done, 1)

                def h_high(t, f):
                    act.wait_ge(h_done, FC * t + f + 1)
                    act.activation(h_hi[:, f, :], h[:, f % 2, :], ACT.Copy).then_inc(hhi_done, 1)

                act.wait_ge(consts_ready, 2)

                def iteration(t, last):
                    for f in range(FC):
                        if f == 6:
                            roots(t + 2)
                        silu(t, f)
                        if f >= 1:
                            h_high(t, f - 1)
                    if not last:
                        high(t + 1, 0)
                    h_high(t, FC - 1)
                    if not last:
                        high(t + 1, 1)

                with act.Fori(0, NT - 1) as t:
                    iteration(t, False)
                iteration(NT - 1, True)
                roots(NT + 2)

            @block.vector
            def _(dve):
                dve.memset(eps[:, :], EPS).then_inc(consts_ready, 1)
                dve.memset(moments[:, :, :], 1.0).then_inc(consts_ready, 1)
                for s, n in ((norm_done, 1 + 2), (h_ready, 2), (y3_done, 2), (wide_ready, 2), (scaled_done, 2),
                             (z_done, 2), (stats_done, 2), (moments_ready, 1), (root_ready, 1), (scale_ready, 1),
                             (shift_ready, 1), (x2_ready, 2), (kept, 2), (t_done, 2), (hi_ready, 2), (xT_ready, 2)):
                    dve.sem_inc(s, n)
                dve.wait_ge(consts_ready, 2)
                dve.wait_ge(norm_ready, 1)
                dve.reciprocal(inv_norm[:, :], norm[:, :]).then_inc(inv_ready, 1)

                def add(t, p):
                    pair = bass.ds(2 * t + p, 1)
                    dve.wait_ge(norm_done, 2 * t + p + 2)
                    dve.tensor_tensor(scaled[:, p:p + 1, :], norm_bank.unsqueeze(1), cross_y[:, pair, :], ALU.mult)\
                       .then_inc(scaled_done, 1)
                    dve.wait_ge(scaled_done, 2 * t + p + 1)
                    dve.scalar_tensor_tensor(z[:, p, :], scaled[:, p, :], g_scaled[:, :], x[:, pair, :].squeeze(1),
                                             ALU.mult, ALU.add).then_inc(z_done, 1)
                    dve.wait_ge(z_done, 2 * t + p + 1)
                    dve.bn_stats(row_stats[:, 2 + p, :], z[:, p, :]).then_inc(stats_done, 1)

                def aggregate(t, first_row, n):
                    dve.sem_inc(waited, 1)
                    for p in range(2):
                        ins = dve.bn_aggr(moments[:, first_row + p, :], row_stats[:, first_row + p, :])
                        if p == 1 and n is not None:
                            ins.then_inc(moments_ready, 1)

                def norm_terms(n):
                    dve.wait_ge(root_ready, n)
                    dve.reciprocal(scale[:, :], root[:, :]).then_inc(scale_ready, 1)
                    dve.wait_ge(scale_ready, n)
                    dve.scalar_tensor_tensor(shift[:, :], moments[:, :, 0], -1.0, scale[:, :], ALU.mult, ALU.mult)\
                       .then_inc(shift_ready, 1)
                    dve.wait_ge(shift_ready, n)

                def normalise(t):
                    for p in range(2):
                        dve.tensor_scalar(x2[:, p, :], z[:, p, :], scale[:, 2 + p:3 + p], shift[:, 2 + p:3 + p],
                                          ALU.mult, ALU.add).then_inc(x2_ready, 1)

                def keep(t):
                    for p in range(2):
                        dve.tensor_scalar(x[:, bass.ds(2 * t + p, 1), :], z[:, p:p + 1, :], scale[:, 2 + p:3 + p],
                                          shift[:, 2 + p:3 + p], ALU.mult, ALU.add).then_inc(kept, 1)

                def finish(t):
                    dve.wait_ge(stored, 16 * t + 16)
                    for p in range(2):
                        dve.tensor_scalar(result[:, p, :], y3[:, p, :], scale[:, p:p + 1], shift[:, p:p + 1],
                                          ALU.mult, ALU.add).then_inc(result_ready, 1)

                def low(t, p):
                    dve.wait_ge(hi_ready, 2 * t + p + 1)
                    dve.tensor_tensor(xT_lo[:, :, P * p:P * p + P], T(p).rearrange("p (c t) -> p c t", c=DC),
                                      xT_hi[:, :, P * p:P * p + P], ALU.subtract).then_inc(xT_ready, 1)

                def gated(t, f):
                    dve.wait_ge(silu_done, FC * t + f + 1)
                    dve.wait_ge(h_ready, FC * t + f + 1)
                    dve.tensor_tensor(h[:, f % 2, :], GU(f)[:, TOK:2 * TOK], gate[:, f % 2, :], ALU.mult)\
                       .then_inc(h_done, 1)

                def residual(t):
                    dve.wait_ge(down_done, t + 1)
                    dve.wait_ge(kept, 2 * t + 2)
                    for p in range(2):
                        dve.tensor_tensor(y3[:, p:p + 1, :], down(p).unsqueeze(1), x[:, bass.ds(2 * t + p, 1), :],
                                          ALU.add).then_inc(y3_done, 1)
                    for p in range(2):
                        dve.wait_ge(y3_done, 2 * t + p + 3)
                        dve.bn_stats(row_stats[:, p, :], y3[:, p, :]).then_inc(y3_stats, 1)

                def iteration(t, first, last):
                    for f in range(FC):
                        gated(t, f)
                        if not last and f in (1, 3):
                            add(t + 1, f // 2)
                        if f == 3:
                            if not first:
                                dve.wait_ge(y3_stats, 2 * t)
                                aggregate(t, 0, None)
                            if not last:
                                dve.wait_ge(stats_done, 2 * t + 4)
                                aggregate(t, 2, 1)
                            else:
                                dve.wait_ge(y3_stats, 2 * t)
                                dve.tensor_copy(moments[:, 2:4, :], moments[:, 2:4, :]).then_inc(moments_ready, 1)
                        if f == 6:
                            norm_terms(t + 2)
                            if not last:
                                normalise(t + 1)
                                keep(t + 1)
                        if f == 7 and not first:
                            finish(t - 1)
                    if not last:
                        for p in range(2):
                            low(t + 1, p)
                    residual(t)

                iteration(0, True, False)
                with dve.Fori(1, NT - 1) as t:
                    iteration(t, False, False)
                iteration(NT - 1, False, True)
                dve.wait_ge(y3_stats, 2 * NT)
                aggregate(NT, 0, 1)
                norm_terms(NT + 2)
                finish(NT - 1)

            @block.tensor
            def _(pe):
                def spread_norms(t, p):
                    pe.wait_ge(wide_ready, 2 * t + p + 1)
                    pe.wait_ge(scaled_done, 2 * t + p)
                    for n in range(DC):
                        ins = pe.transpose(norm_bank[:, P * n:P * n + P],
                                           inv_wide[:, p, n, :, :].rearrange("p b c -> p (b c)"), ident[:, :])
                    ins.then_inc(norm_done, 1)

                def transposes(t, p):
                    pe.wait_ge(x2_ready, 2 * t + p + 1)
                    for n in range(DC):
                        ins = pe.transpose(T(p)[:, P * n:P * n + P], x2[:, p, P * n:P * n + P], ident[:, :])
                    ins.then_inc(t_done, 1)

                def gate_up(t, f):
                    if f >= 2 or not isinstance(t, int) or t > 0:
                        pe.wait_ge(h_done, FC * t + f - 1)
                    fs = slice(P * f, P * f + P)
                    for k, w in enumerate((wg, wu)):
                        for cc in range(DC):
                            for r, part in enumerate((xT_hi, xT_lo)):
                                ins = pe.matmul(GU(f)[:, TOK * k:TOK * k + TOK], w[:, cc, fs], part[:, cc, :],
                                                start=(cc == 0 and r == 0), stop=(cc == DC - 1 and r == 1))
                    ins.then_inc(gu_done, 1)

                def down_product(t, f):
                    pe.wait_ge(h_ready, FC * t + f + 3)
                    if f == 0:
                        pe.wait_ge(y3_done, 2 * t + 2)
                    for tt in range(2):
                        for r, part in enumerate((h_hi, h_lo)):
                            ins = pe.matmul(down(tt), part[:, f, P * tt:P * tt + P], wd[:, f, :],
                                            start=(f == 0 and r == 0), stop=(f == FC - 1 and r == 1))
                    if f == FC - 1:
                        ins.then_inc(down_done, 1)

                pe.wait_ge(w_in, 48)

                def iteration(t, last):
                    pe.wait_ge(xT_ready, 2 * t + 2)
                    for f in range(FC):
                        gate_up(t, f)
                        if not last and f in (1, 3):
                            spread_norms(t + 1, f // 2)
                        if f >= 2 and f < FC - 1:
                            down_product(t, f - 2)
                    if not last:
                        for p in range(2):
                            transposes(t + 1, p)
                    for f in range(FC - 3, FC):
                        down_product(t, f)

                iteration(0, False)
                with pe.Fori(1, NT - 1) as t:
                    iteration(t, False)
                iteration(NT - 1, True)


def program(nc, x, xT, ctx, ctxT, wqT, wkT, wvT, woT, bq, bk, bv, bo, xwqT, xwkT, xwv, xwoT, xbo, g, wgT, wuT, wdT, out):
    with ExitStack() as c:
        y1 = c.enter_context(nc.sbuf_tensor("y1", [P, PAIRS, D], F32))
        ident = c.enter_context(nc.sbuf_tensor("ident", [P, P], F32))
        identb = c.enter_context(nc.sbuf_tensor("identb", [P, P], BF16))
        stats = c.enter_context(nc.sbuf_tensor("stats", [P, PAIRS * 6], F32))
        cross = CrossOperands(nc, c)
        ctx_l, ctxT_n = ctx.rearrange("b l d -> l b d"), ctxT.rearrange("b (n p) c -> p (b n) c", p=P)
        zeroed = c.enter_context(nc.semaphore("zeroed"))
        with nc.Block() as block:
            @block.gpsimd
            def _(pool):
                pool.memset(ident[:, :], 0.0).then_inc(zeroed, 1)
                pool.memset(identb[:, :], 0.0).then_inc(zeroed, 1)
                pool.wait_ge(zeroed, 2)
                for m in (ident, identb):
                    pool.affine_select(out=m[:, :], in_=m[:, :], compare_op=ALU.not_equal, fill=1.0, base=0,
                                       pattern=[[-1, P]], channel_multiplier=1).then_inc(zeroed, 1)
                pool.wait_ge(zeroed, 4)
        pairs = "(i b) l d -> (b l) i d"
        x_d = x.rearrange(pairs, b=2)
        attention_phase(nc, ident, x_d, xT.rearrange("(c p) t -> p c t", p=P),
                        [w.rearrange("(c p) f -> p c f", p=P) for w in (wkT, wqT, wvT, woT)],
                        (bq, bk),
                        bo.rearrange("(a d) -> a d", a=1).broadcast_to([P, D]),
                        bv.rearrange("(a d) -> a d", a=1).broadcast_to([P, D]), y1, stats, cross, (xwkT, xwqT),
                        xwv.rearrange("(j p) c -> p j c", p=P), xwoT.rearrange("(j p) c -> p j c", p=P),
                        xbo.rearrange("(c a) -> c a", a=1), ctx_l)
        cross_y = c.enter_context(nc.sbuf_tensor("cross_y", [P, PAIRS, D], F32))
        sumsq = c.enter_context(nc.sbuf_tensor("sumsq", [P, PAIRS * 8], F32))
        FC = wdT.shape[0] // P
        wg = c.enter_context(nc.sbuf_tensor("wg", [P, DC, FC * P], F16))
        wu = c.enter_context(nc.sbuf_tensor("wu", [P, DC, FC * P], F16))
        wd = c.enter_context(nc.sbuf_tensor("wd", [P, FC, D], F16))
        w_in = c.enter_context(nc.semaphore("ffn_w_in"))
        g_scaled = c.enter_context(nc.sbuf_tensor("g_scaled", [P, 1], F32))
        x2T_hi = c.enter_context(nc.sbuf_tensor("x2T_hi", [P, DC, TOK], F16))
        x2T_lo = c.enter_context(nc.sbuf_tensor("x2T_lo", [P, DC, TOK], F16))
        cross_phase(nc, ident, identb, y1, stats, cross, ctx_l, ctxT_n, cross_y, sumsq,
                    [(w, w_d.rearrange("(c p) f -> p c f", p=P)) for w, w_d in ((wg, wgT), (wu, wuT), (wd, wdT))], w_in,
                    g.rearrange("(c a) -> c a", a=1), g_scaled, x2T_hi, x2T_lo)
        feed_forward_phase(nc, ident, y1, cross_y, sumsq, (wg, wu, wd), w_in, g_scaled, x2T_hi, x2T_lo,
                           out.rearrange(pairs, b=2))


def kernel(**inputs):
    import numpy as _np
    import concourse.bacc as _bacc
    from concourse import mybir as _mybir
    from concourse.bass_utils import run_bass_kernel_spmd as _run

    nc = _bacc.Bacc("TRN2", target_bir_lowering=False, num_devices=1)
    i = {k: _np.asarray(v) for k, v in inputs.items()}
    given = {
        "x": i["x"], "xT": i["x"].reshape(B * L, D).T,
        "ctx": i["ctx_4096"], "ctxT": i["ctx_4096"].transpose(0, 2, 1),
        "wqT": i["L0_attn_Wq"].T, "wkT": i["L0_attn_Wk"].T, "wvT": i["L0_attn_Wv"].T, "woT": i["L0_attn_Wo"].T,
        "bq": i["L0_attn_bq"].reshape(DC, P).T, "bk": i["L0_attn_bk"].reshape(DC, P).T,
        "bv": i["L0_attn_bv"], "bo": i["L0_attn_bo"],
        "xwqT": i["L0_xattn_Wq"].T, "xwkT": i["L0_xattn_Wk"].T, "xwv": i["L0_xattn_Wv"], "xwoT": i["L0_xattn_Wo"].T,
        "xbo": i["L0_xattn_bo"], "g": i["L0_xattn_g"].reshape(L),
        "wgT": i["L0_ffn_W_gate"].T, "wuT": i["L0_ffn_W_up"].T, "wdT": i["L0_ffn_W_down"].T,
    }
    arrays, args = {}, []
    for name, a in given.items():
        a = _np.ascontiguousarray(a)
        arrays[f"in_{name}"] = a
        args.append(nc.dram_tensor(f"in_{name}", a.shape, _mybir.dt.from_np(a.dtype), kind="ExternalInput").ap())
    args.append(nc.dram_tensor("out", (B, L, D), _mybir.dt.float32, kind="ExternalOutput").ap())
    program(nc, *args)
    return _run(nc, [arrays], core_ids=[0]).results[0]["out"]
```
